# Optimizing a Trainium2 kernel written in Bass

```python
import numpy as np
import jax
import jax.numpy as jnp

def _softmax(x, axis=-1):
    return jax.nn.softmax(x, axis=axis)

def _gelu(x):
    return jax.nn.gelu(x, approximate=True)

def _silu(x):
    return jax.nn.silu(x)

def _sigmoid(x):
    return jax.nn.sigmoid(x)

def _layernorm(x, axis=-1, eps=1e-05):
    m = jnp.mean(x, axis=axis, keepdims=True)
    v = jnp.var(x, axis=axis, keepdims=True)
    return (x - m) / jnp.sqrt(v + eps)

def _scatter_add(tgt, idx, src, axis=0):
    return tgt.at[idx].add(src)

def _segment_sum(src, seg, n):
    return jax.ops.segment_sum(src, seg, n)
kernel_name = 'mk_gnn_resnorm_d2_gnn_r8_030360'

def setup_inputs(seed: int=0):
    np.random.seed(seed)
    _w = jnp.asarray

    def _rec_inputs():
        import jax
        import jax.numpy as jnp
        _gk = jax.random.key(seed)
        x = -0.0003713 + 1 * jax.random.normal(jax.random.fold_in(_gk, 1), (12500, 128), jnp.float32)
        src = jax.random.randint(jax.random.fold_in(_gk, 2), (400000,), 0, 12500, jnp.int32)
        dst = jnp.minimum((12500 * jax.random.uniform(jax.random.fold_in(_gk, 3), (400000,)) ** 2.0).astype(jnp.int32), 99999)
        _o = jnp.argsort(dst, stable=True)
        src = src[_o]
        dst = dst[_o]
        edge_attr_64 = 0.000189758 + 1.00013 * jax.random.normal(jax.random.fold_in(_gk, 11), (400000, 64), jnp.float32)
        return (x, src, dst, edge_attr_64)
    x, src, dst, edge_attr_64 = _rec_inputs()

    def _L0_gnn_setup():
        import jax, jax.numpy as jnp
        import numpy as np
        N_NODES = 12500
        N_EDGES = 200000
        IN_C = 128
        OUT_C = 128
        HEADS = 8
        HEAD_C = OUT_C // HEADS
        NEG_SLOPE = 0.2
        EPS = 1e-16
        key = jax.random.key(seed)
        k1, k2, k3, k4, k5, k6 = jax.random.split(key, 6)
        node_features = jax.random.normal(k1, (N_NODES, IN_C), dtype=jnp.float32)
        edge_index = jax.random.randint(k2, (2, N_EDGES), 0, N_NODES, dtype=jnp.int64)
        W = jax.random.normal(k3, (IN_C, OUT_C), dtype=jnp.float32) * (1.0 / np.sqrt(IN_C))
        a_left = jax.random.normal(k4, (HEAD_C, HEADS), dtype=jnp.float32) * 0.1
        a_right = jax.random.normal(k5, (HEAD_C, HEADS), dtype=jnp.float32) * 0.1
        bias = jnp.zeros((OUT_C,), dtype=jnp.float32)
        return {'node_features': node_features, 'edge_index': edge_index, 'W': W, 'a_left': a_left, 'a_right': a_right, 'bias': bias}
    _L0_gnn_all = _L0_gnn_setup()
    _L0_gnn_in = {k: v for k, v in _L0_gnn_all.items() if k in ('W', 'a_left', 'a_right', 'bias')}
    del _L0_gnn_all

    def _L1_gnn_setup():
        import jax, jax.numpy as jnp
        import numpy as np
        N, E, D, H, ED = (6250, 100000, 128, 8, 64)
        C = D // H

        def _ln(x, g, b, eps=1e-05):
            m = jnp.mean(x, axis=-1, keepdims=True)
            v = jnp.var(x, axis=-1, keepdims=True)
            return (x - m) * jax.lax.rsqrt(v + eps) * g + b
        key = jax.random.key(seed)
        ks = jax.random.split(key, 16)
        p = lambda k, shape: jax.random.normal(k, shape, dtype=jnp.float32) * 0.05
        return {'x': jax.random.normal(ks[0], (N, D), dtype=jnp.float32), 'edge_index': jax.random.randint(ks[1], (2, E), 0, N, dtype=jnp.int64), 'edge_attr': jax.random.normal(ks[2], (E, ED), dtype=jnp.float32), 'Wq': p(ks[3], (D, D)), 'bq': jnp.zeros((D,), jnp.float32), 'Wk': p(ks[4], (D, D)), 'bk': jnp.zeros((D,), jnp.float32), 'Wv': p(ks[5], (D, D)), 'bv': jnp.zeros((D,), jnp.float32), 'We': p(ks[6], (ED, D)), 'Wskip': p(ks[7], (D, D)), 'bskip': jnp.zeros((D,), jnp.float32), 'g1': jnp.ones((D,), jnp.float32), 'b1': jnp.zeros((D,), jnp.float32), 'g2': jnp.ones((D,), jnp.float32), 'b2': jnp.zeros((D,), jnp.float32), 'Wf1': p(ks[8], (D, 4 * D)), 'bf1': jnp.zeros((4 * D,), jnp.float32), 'Wf2': p(ks[9], (4 * D, D)), 'bf2': jnp.zeros((D,), jnp.float32)}
    _L1_gnn_all = _L1_gnn_setup()
    _L1_gnn_in = {k: v for k, v in _L1_gnn_all.items() if k in ('Wq', 'bq', 'Wk', 'bk', 'Wv', 'bv', 'We', 'Wskip', 'bskip', 'g1', 'b1', 'g2', 'b2', 'Wf1', 'bf1', 'Wf2', 'bf2')}
    del _L1_gnn_all
    return {'x': x, 'src': src, 'dst': dst, 'edge_attr_64': edge_attr_64, 'L0_gnn_W': _L0_gnn_in['W'], 'L0_gnn_a_left': _L0_gnn_in['a_left'], 'L0_gnn_a_right': _L0_gnn_in['a_right'], 'L0_gnn_bias': _L0_gnn_in['bias'], 'L1_gnn_Wq': _L1_gnn_in['Wq'], 'L1_gnn_bq': _L1_gnn_in['bq'], 'L1_gnn_Wk': _L1_gnn_in['Wk'], 'L1_gnn_bk': _L1_gnn_in['bk'], 'L1_gnn_Wv': _L1_gnn_in['Wv'], 'L1_gnn_bv': _L1_gnn_in['bv'], 'L1_gnn_We': _L1_gnn_in['We'], 'L1_gnn_Wskip': _L1_gnn_in['Wskip'], 'L1_gnn_bskip': _L1_gnn_in['bskip'], 'L1_gnn_g1': _L1_gnn_in['g1'], 'L1_gnn_b1': _L1_gnn_in['b1'], 'L1_gnn_g2': _L1_gnn_in['g2'], 'L1_gnn_b2': _L1_gnn_in['b2'], 'L1_gnn_Wf1': _L1_gnn_in['Wf1'], 'L1_gnn_bf1': _L1_gnn_in['bf1'], 'L1_gnn_Wf2': _L1_gnn_in['Wf2'], 'L1_gnn_bf2': _L1_gnn_in['bf2']}

def reference(x, src, dst, edge_attr_64, L0_gnn_W, L0_gnn_a_left, L0_gnn_a_right, L0_gnn_bias, L1_gnn_Wq, L1_gnn_bq, L1_gnn_Wk, L1_gnn_bk, L1_gnn_Wv, L1_gnn_bv, L1_gnn_We, L1_gnn_Wskip, L1_gnn_bskip, L1_gnn_g1, L1_gnn_b1, L1_gnn_g2, L1_gnn_b2, L1_gnn_Wf1, L1_gnn_bf1, L1_gnn_Wf2, L1_gnn_bf2):
    import jax
    import jax.numpy as jnp

    def _L0_gnn_ref(node_features, edge_index, W, a_left, a_right, bias):
        import jax, jax.numpy as jnp
        import numpy as np
        N_NODES = 12500
        N_EDGES = 200000
        IN_C = 128
        OUT_C = 128
        HEADS = 8
        HEAD_C = OUT_C // HEADS
        NEG_SLOPE = 0.2
        EPS = 1e-16
        N = node_features.shape[0]
        emb = (node_features @ W).reshape(N, HEADS, HEAD_C)
        src_scores = jnp.einsum('nhc,ch->nh', emb, a_left)
        tgt_scores = jnp.einsum('nhc,ch->nh', emb, a_right)
        src, tgt = (edge_index[0], edge_index[1])
        edge_scores = jax.nn.leaky_relu(src_scores[src] + tgt_scores[tgt], NEG_SLOPE)
        exp_scores = jnp.exp(edge_scores)
        denom = jax.ops.segment_sum(exp_scores, tgt, num_segments=N)
        attn = exp_scores / (denom[tgt] + EPS)
        weighted = emb[src] * attn[:, :, None]
        out = jax.ops.segment_sum(weighted, tgt, num_segments=N)
        return out.reshape(N, OUT_C) + bias

    def _L1_gnn_ref(x, edge_index, edge_attr, Wq, bq, Wk, bk, Wv, bv, We, Wskip, bskip, g1, b1, g2, b2, Wf1, bf1, Wf2, bf2):
        import jax, jax.numpy as jnp
        import numpy as np
        N, E, D, H, ED = (6250, 100000, 128, 8, 64)
        C = D // H

        def _ln(x, g, b, eps=1e-05):
            m = jnp.mean(x, axis=-1, keepdims=True)
            v = jnp.var(x, axis=-1, keepdims=True)
            return (x - m) * jax.lax.rsqrt(v + eps) * g + b
        n = x.shape[0]
        src, dst = (edge_index[0], edge_index[1])
        q = (x @ Wq + bq).reshape(n, H, C)
        k = (x @ Wk + bk).reshape(n, H, C)
        v = (x @ Wv + bv).reshape(n, H, C)
        e = (edge_attr @ We).reshape(-1, H, C)
        k_j = k[src] + e
        v_j = v[src] + e
        logits = jnp.sum(q[dst] * k_j, axis=-1) / np.sqrt(C)
        m = jax.ops.segment_max(logits, dst, num_segments=n)
        ex = jnp.exp(logits - m[dst])
        denom = jax.ops.segment_sum(ex, dst, num_segments=n)
        alpha = ex / denom[dst]
        agg = jax.ops.segment_sum(alpha[..., None] * v_j, dst, num_segments=n)
        conv = agg.reshape(n, D) + x @ Wskip + bskip
        h = _ln(conv + x, g1, b1)
        ffn = jax.nn.gelu(h @ Wf1 + bf1, approximate=False) @ Wf2 + bf2
        return _ln(ffn + h, g2, b2)
    edge_index = jnp.stack([src, dst])
    x = _layernorm(x + _L0_gnn_ref(x, edge_index, L0_gnn_W, L0_gnn_a_left, L0_gnn_a_right, L0_gnn_bias), axis=-1)
    x = _layernorm(x + _L1_gnn_ref(x, edge_index, edge_attr_64, L1_gnn_Wq, L1_gnn_bq, L1_gnn_Wk, L1_gnn_bk, L1_gnn_Wv, L1_gnn_bv, L1_gnn_We, L1_gnn_Wskip, L1_gnn_bskip, L1_gnn_g1, L1_gnn_b1, L1_gnn_g2, L1_gnn_b2, L1_gnn_Wf1, L1_gnn_bf1, L1_gnn_Wf2, L1_gnn_bf2), axis=-1)
    return x

_drawn_inputs = setup_inputs


def setup_inputs(seed=0):
    import zlib

    import numpy as np

    out = dict(_drawn_inputs(seed))
    spreads = {'L0_gnn_bias': (0.0, 0.1),
     'L1_gnn_bq': (0.0, 0.8),
     'L1_gnn_bk': (0.0, 0.8),
     'L1_gnn_bv': (0.0, 0.1),
     'L1_gnn_bskip': (0.0, 0.1),
     'L1_gnn_g1': (1.0, 0.2),
     'L1_gnn_b1': (0.0, 0.1),
     'L1_gnn_g2': (1.0, 0.2),
     'L1_gnn_b2': (0.0, 0.1),
     'L1_gnn_bf1': (0.0, 0.1),
     'L1_gnn_bf2': (0.0, 0.1)}
    factors = {}
    for name, (base, spread) in spreads.items():
        noise = np.random.default_rng([zlib.crc32(name.encode()), seed]).standard_normal(out[name].shape)
        drawn = base * np.exp(spread * noise) if base else spread * noise
        out[name] = jnp.asarray(drawn.astype(out[name].dtype))
    for name, factor in factors.items():
        out[name] = (out[name] * factor).astype(out[name].dtype)
    return out
```

```python
from contextlib import ExitStack

import concourse.bass as bass
from concourse import mybir

F32 = mybir.dt.float32
I32 = mybir.dt.int32
ALU = mybir.AluOpType
ACT = mybir.ActivationFunctionType
AX = mybir.AxisListType

P = 128
NODES, EDGES, D, H, ED, FF = 12500, 400000, 128, 8, 64, 512
C = D // H
TILES = 4
GE = TILES * P
GROUPS = -(-EDGES // GE)
RING = 4
BLOCKS = -(-NODES // P) + 1
UNITS = GROUPS + BLOCKS - 1
NPAD = BLOCKS * P
FLAG_TILES = 25
HC = C + 1
ROW0 = D + H
AGG = H * HC
NODE1 = 3 * D
FAR = 1.0e30
NBLK = 3
EPS_LN = 1e-5

assert UNITS % RING == 0 and BLOCKS % NBLK == 0


def has(j, d, total):
    return 0 <= j + d < total if isinstance(j, int) else True


def laps(j, p, ring, n):
    if isinstance(j, int):
        return n * (j // ring + 1)
    return (j - p) * (n // ring) + n if n % ring == 0 else ((j - p) * n) // ring + n


def over_ring(eng, total, ring, step):
    for p in range(ring):
        step(p, p)
    with eng.Fori(ring, total - 2 * ring + 1, ring) as base:
        for p in range(ring):
            step(base + p, p)
    for p in range(ring):
        step(total - ring + p, p)


def gate(eng, passed):
    eng.sem_inc(passed, 1)


class Store:

    def __init__(self, nc, ctx, whole):
        self.nc, self.ctx, self.whole, self.counted = nc, ctx, whole, []

    def sb(self, name, shape, dt=F32):
        return self.ctx.enter_context(self.nc.sbuf_tensor(name, shape, dt))

    def ps(self, name, shape, dt=F32):
        return self.ctx.enter_context(self.nc.psum_tensor(name, shape, dt))

    def sem(self, name):
        self.counted.append(self.ctx.enter_context(self.nc.semaphore(name)))
        return self.counted[-1]

    def dma_sem(self, name):
        return self.whole.enter_context(self.nc.semaphore(name))

    def ring_sems(self, name, n):
        return [self.dma_sem(f"{name}{i}") for i in range(n)]

    def over(self):
        with self.nc.Block() as block:

            @block.sync
            def _(sp):
                for sem in self.counted:
                    sp.sem_clear(sem)


class Names:
    pass


def constants(nc, st, k):
    iota_i = st.sb("iota_i", [P, P], I32)
    part_i = st.sb("part_i", [P, 1], I32)
    unit_i = st.sb("unit_i", [P, UNITS], I32)
    part_f = st.sb("part_f", [P, 1])
    iota_s = st.sem("c_iota")
    done_s = st.sem("c_done")
    conv_s = st.sem("c_conv")
    with nc.Block() as block:

        @block.gpsimd
        def _(pool):
            nc.gpsimd.iota(iota_i[:, :], pattern=[[1, P]], base=0, channel_multiplier=0).then_inc(iota_s, 1)
            nc.gpsimd.iota(part_i[:, :], pattern=[[0, 1]], base=0, channel_multiplier=1).then_inc(iota_s, 1)
            nc.gpsimd.iota(unit_i[:, :], pattern=[[1, UNITS]], base=0, channel_multiplier=0).then_inc(iota_s, 1)

        @block.vector
        def _(dve):
            dve.wait_ge(iota_s, 3)
            nc.vector.tensor_copy(k.iota[:, :], iota_i[:, :]).then_inc(conv_s, 1)
            nc.vector.tensor_copy(part_f[:, :], part_i[:, :]).then_inc(conv_s, 1)
            nc.vector.tensor_copy(k.unit_row[:, :], unit_i[:, :]).then_inc(conv_s, 1)
            nc.vector.memset(k.ones[:, :], 1.0).then_inc(done_s, 1)
            nc.vector.memset(k.eps[:, :], EPS_LN).then_inc(done_s, 1)
            dve.wait_ge(conv_s, 3)
            nc.vector.tensor_scalar(k.ident[:, :], k.iota[:, :], part_f[:, 0:1], None, ALU.is_equal).then_inc(done_s, 1)
            nc.vector.tensor_scalar(k.block_start[:, :], part_f[:, :], float(P), None, ALU.mult).then_inc(done_s, 1)
            nc.vector.tensor_copy(k.part[:, :], part_f[:, :]).then_inc(done_s, 1)

        @block.sync
        def _(sp):
            n = 0
            for dst, src in k.loads:
                sp.dma_start(dst, src).then_inc(k.loaded, 16)
                n += 16
            sp.wait_ge(k.loaded, n)


def unit_tables(nc, st, k, a):
    last_i = st.sb("u_last_i", [BLOCKS, GROUPS], I32)
    below = st.sb("u_below", [BLOCKS, GROUPS])
    first = st.sb("u_first", [BLOCKS, 2])
    begun = st.sb("u_begun", [BLOCKS, UNITS])
    blk = st.sb("u_blk", [P, UNITS + 1])
    grp = st.sb("u_grp", [1, UNITS])
    pb = [st.ps(f"u_psum{i}", [P, UNITS // 2]) for i in range(2)]
    last_in = st.dma_sem("u_last_in")
    step = st.sem("u_step")
    counted = st.sem("u_counted")
    begun_s = st.sem("u_begun_s")
    half = UNITS // 2
    with nc.Block() as block:

        @block.sync
        def _(sp):
            sp.dma_start(last_i[:, :], a["last_dst"].to_broadcast([BLOCKS, GROUPS])).then_inc(last_in, 16)

        @block.vector
        def _(dve):
            dve.wait_ge(last_in, 16)
            nc.vector.tensor_scalar(below[:, :], last_i[:, :], k.block_start[0:BLOCKS, 0:1], None, ALU.is_lt).then_inc(step, 1)
            dve.wait_ge(step, 1)
            nc.vector.tensor_reduce(out=first[:, 0:1], in_=below[:, :], op=ALU.add, axis=AX.X).then_inc(step, 1)
            dve.wait_ge(step, 2)
            nc.vector.tensor_tensor(first[:, 1:2], first[:, 0:1], k.part[0:BLOCKS, :], ALU.add).then_inc(step, 1)
            dve.wait_ge(step, 3)
            nc.vector.tensor_scalar(begun[:, :], k.unit_row[0:BLOCKS, :], first[:, 1:2], None, ALU.is_ge).then_inc(begun_s, 1)
            nc.vector.memset(blk[:, 0:1], -1.0).then_inc(step, 1)
            for i in range(2):
                dve.wait_ge(counted, i + 1)
                nc.vector.tensor_scalar(blk[:, 1 + i * half:1 + (i + 1) * half], pb[i][:, :], -1.0, None, ALU.add).then_inc(step, 1)
            dve.wait_ge(step, 6)
            nc.vector.tensor_scalar(k.ucol[:, :, 0], blk[:, 1:], float(P), None, ALU.mult).then_inc(step, 1)
            nc.vector.tensor_tensor(k.ucol[:, :, 1], blk[:, 1:], blk[:, 0:UNITS], ALU.is_equal).then_inc(step, 1)
            nc.vector.tensor_tensor(grp[:, :], k.unit_row[0:1, :], blk[0:1, 1:], ALU.subtract).then_inc(step, 1)
            nc.vector.tensor_copy(k.ureg[:, :, 1], blk[0:1, 1:]).then_inc(step, 1)
            dve.wait_ge(step, 10)
            nc.vector.tensor_scalar(k.ucol[:, :, 2], k.ucol[:, :, 1], -1.0, 2.0 * FAR, ALU.add, ALU.mult).then_inc(step, 1)
            nc.vector.tensor_copy(k.ureg[:, :, 0], grp[:, :]).then_inc(step, 1)

        @block.tensor
        def _(pe):
            pe.wait_ge(begun_s, 1)
            for i in range(2):
                nc.tensor.matmul(pb[i][:, :], k.ones[0:BLOCKS, :], begun[:, i * half:(i + 1) * half],
                                 start=True, stop=True).then_inc(counted, 1)


def run_flags(nc, st, a, far_rows):
    here = st.sb("f_here", [P, FLAG_TILES * P], I32)
    prev = st.sb("f_prev", [P, FLAG_TILES * P], I32)
    flag = st.sb("f_flag", [P, FLAG_TILES * P])
    neg = st.sb("f_neg", [P, FLAG_TILES * P])
    come = st.dma_sem("f_in")
    made = st.sem("f_made")
    out = st.dma_sem("f_out")
    rows = far_rows.rearrange("(p k) h e -> p k h e", p=P)
    with nc.Block() as block:

        @block.sync
        def _(sp):
            sp.dma_start(here[:, :], a["dst_rows"]).then_inc(come, 16)
            sp.dma_start(prev[:, :], a["dst_prev_rows"]).then_inc(come, 16)
            sp.wait_ge(made, 2)
            for h in range(H):
                sp.dma_start(rows[:, :, h, :], neg[:, :].rearrange("p (k e) -> p k e", e=P)).then_inc(out, 16)
            sp.wait_ge(out, 16 * H)

        @block.vector
        def _(dve):
            dve.wait_ge(come, 32)
            nc.vector.tensor_tensor(flag[:, :], here[:, :], prev[:, :], ALU.not_equal).then_inc(made, 1)
            dve.wait_ge(made, 1)
            nc.vector.tensor_scalar(neg[:, :], flag[:, :], -3.0e38, None, ALU.mult).then_inc(made, 1)


def project0(nc, st, k, a, table0, tgt0):
    wcat = st.sb("p_wcat", [P, D + 2 * H])
    xt = st.sb("p_xt", [P, NBLK, 3 * P])
    res = st.sb("p_res", [P, NBLK, 3, D + 2 * H])
    pw = st.ps("p_pw", [P, 2 * H])
    pp = [st.ps(f"p_pp{i}", [P, 3, D + 2 * H]) for i in range(NBLK)]
    w_ready, w_mm = st.sem("p_w_ready"), st.sem("p_w_mm")
    x_in = st.ring_sems("p_x_in", NBLK)
    mm_done, res_done = st.sem("p_mm_done"), st.sem("p_res_done")
    stored = st.ring_sems("p_stored", NBLK)
    steps = BLOCKS // 3
    t0 = table0.rearrange("(s b p) c -> s p b c", b=3, p=P)
    t1 = tgt0.rearrange("(s b p) c -> s p b c", b=3, p=P)
    xs = a["xT"].rearrange("p (s c) -> s p c", s=steps)
    with nc.Block() as block:

        @block.sync
        def _(sp):
            def step(j, p):
                if has(j, -NBLK, steps):
                    sp.wait_ge(mm_done, j - NBLK + 1)
                sp.dma_start(xt[:, p, :], xs[bass.ds(j, 1), :, :].rearrange("o p c -> (o p) c")).then_inc(x_in[p], 16)

            over_ring(sp, steps, NBLK, step)

        @block.tensor
        def _(pe):
            nc.tensor.matmul(pw[:, :], k.w0t[:, :], k.att0[:, :], start=True, stop=True).then_inc(w_mm, 1)
            pe.wait_ge(w_ready, 2)

            def step(j, p):
                if has(j, -NBLK, steps):
                    pe.wait_ge(res_done, j - NBLK + 1)
                pe.wait_ge(x_in[p], laps(j, p, NBLK, 16))
                for b in range(3):
                    last = nc.tensor.matmul(pp[p][:, b, :], xt[:, p, b * P:(b + 1) * P], wcat[:, :], start=True, stop=True)
                last.then_inc(mm_done, 1)

            over_ring(pe, steps, NBLK, step)

        @block.vector
        def _(dve):
            nc.vector.tensor_copy(wcat[:, 0:D], k.w0[:, :]).then_inc(w_ready, 1)
            dve.wait_ge(w_mm, 1)
            nc.vector.tensor_copy(wcat[:, D:], pw[:, :]).then_inc(w_ready, 1)

            def step(j, p):
                if has(j, -NBLK, steps):
                    dve.wait_ge(stored[p], laps(j - NBLK, p, NBLK, 32))
                dve.wait_ge(mm_done, j + 1)
                nc.vector.tensor_copy(res[:, p, :, :], pp[p][:, :, :]).then_inc(res_done, 1)

            over_ring(dve, steps, NBLK, step)

        @block.scalar
        def _(act):
            def step(j, p):
                act.wait_ge(res_done, j + 1)
                act.dma_start(t0[bass.ds(j, 1), :, :, :].rearrange("o p b c -> (o p) b c"), res[:, p, :, 0:ROW0]).then_inc(stored[p], 16)
                act.dma_start(t1[bass.ds(j, 1), :, :, :].rearrange("o p b c -> (o p) b c"), res[:, p, :, ROW0:]).then_inc(stored[p], 16)

            over_ring(act, steps, NBLK, step)
            for p in range(NBLK):
                act.wait_ge(stored[p], laps(steps - NBLK + p, p, NBLK, 32))


def rows_of(table, b):
    return table.rearrange("(b p) c -> b p c", p=P)[bass.ds(b, 1), :, :].rearrange("o p c -> (o p) c")


def one_hot_stage(nc, dve, k, u, j, p, cols_in):
    dve.wait_ge(cols_in[p], laps(j, p, RING, 16))
    dve.wait_ge(u.ucol_in, j + 1)
    nc.vector.tensor_scalar(u.rel[:, p, :], u.cols[:, p, TILES:2 * TILES], u.unit[:, p, 0:1], None, ALU.subtract).then_inc(u.rel_done, 1)
    dve.wait_ge(u.rel_done, j + 1)
    nc.vector.tensor_tensor(
        u.onehot[:, p, :, :],
        k.iota[:, :].unsqueeze(1).to_broadcast([P, TILES, P]),
        u.rel[:, p, :].unsqueeze(2).to_broadcast([P, TILES, P]), ALU.is_equal).then_inc(u.onehot_done, 1)


def gather_step(nc, pool, u, j, p, table, dest, cols_in, gathered, rows_used):
    if has(j, -RING, UNITS):
        pool.wait_ge(rows_used, j - RING + 1)
    pool.wait_ge(cols_in[p], laps(j, p, RING, 16))
    gate(pool, u.admitted)
    for t in range(TILES):
        nc.gpsimd.indirect_dma_start(
            out=dest(p, t), out_offset=None, in_=table,
            in_offset=bass.IndirectOffsetOnAxis(ap=u.cols[:, p, t:t + 1], axis=0)).then_inc(gathered[p], 16)


def gat_layer(nc, st, k, a, table0, tgt0, agg0):
    u = Names()
    u.cols = st.sb("g_cols", [P, RING, 3 * TILES], I32)
    u.unit = st.sb("g_unit", [P, RING, 3])
    u.rel = st.sb("g_rel", [P, RING, TILES])
    u.onehot = st.sb("g_onehot", [P, RING, TILES, P])
    onehot_t = st.sb("g_onehot_t", [P, RING, TILES * P])
    rows = st.sb("g_rows", [P, RING, TILES, ROW0])
    tblk = st.sb("g_tblk", [P, RING, H])
    score = st.sb("g_score", [P, 2, TILES, H])
    leak = st.sb("g_leak", [P, 2, TILES, H])
    wgt = st.sb("g_wgt", [P, RING, TILES, H, HC])
    acc = st.sb("g_acc", [P, RING, AGG])
    p_oht = [st.ps(f"g_p_oht{i}", [P, TILES * P]) for i in range(2)]
    p_tgt = [st.ps(f"g_p_tgt{i}", [P, TILES, H]) for i in range(2)]
    p_sum = [st.ps(f"g_p_sum{i}", [P, AGG]) for i in range(2)]
    sp_passed = st.sem("g_sp_passed")
    cols_in = st.ring_sems("g_cols_in", RING)
    tblk_in = st.ring_sems("g_tblk_in", RING)
    gathered = st.ring_sems("g_gathered", RING)
    stored = st.ring_sems("g_stored", RING)
    u.ucol_in, u.rel_done = st.sem("g_ucol_in"), st.sem("g_rel_done")
    u.onehot_done, u.admitted = st.sem("g_onehot_done"), st.sem("g_admitted")
    oht_mm, oht_done, tgt_mm = st.sem("g_oht_mm"), st.sem("g_oht_done"), st.sem("g_tgt_mm")
    score_done, leak_done, exp_done = st.sem("g_score_done"), st.sem("g_leak_done"), st.sem("g_exp_done")
    wgt_done, sum_mm, acc_done, zeroed = st.sem("g_wgt_done"), st.sem("g_sum_mm"), st.sem("g_acc_done"), st.sem("g_zeroed")

    with nc.Block() as block:

        @block.sync
        def _(sp):
            def store(j, p):
                blk = sp.value_load(k.ureg[0:1, bass.ds(j, 1), 1], min_val=0, max_val=BLOCKS - 1)
                sp.wait_ge(acc_done, j + 1)
                gate(sp, sp_passed)
                if has(j, -1, UNITS):
                    q = (p - 1) % RING
                    sp.wait_ge(stored[q], laps(j - 1, q, RING, 16))
                    gate(sp, sp_passed)
                sp.dma_start(rows_of(agg0, blk), acc[:, p, :]).then_inc(stored[p], 16)

            def step(j, p):
                grp = sp.value_load(k.ureg[0:1, bass.ds(j, 1), 0], min_val=0, max_val=GROUPS - 1)
                blk = sp.value_load(k.ureg[0:1, bass.ds(j, 1), 1], min_val=0, max_val=BLOCKS - 1)
                if has(j, -RING, UNITS):
                    sp.wait_ge(gathered[p], laps(j - RING, p, RING, 16 * TILES))
                    gate(sp, sp_passed)
                    sp.wait_ge(u.rel_done, j - RING + 1)
                    gate(sp, sp_passed)
                sp.dma_start(u.cols[:, p, :], a["edge_cols"][bass.ds(grp, 1), :, :].rearrange("o p c -> (o p) c")).then_inc(cols_in[p], 16)
                if has(j, -RING, UNITS):
                    sp.wait_ge(tgt_mm, j - RING + 1)
                    gate(sp, sp_passed)
                sp.dma_start(tblk[:, p, :], rows_of(tgt0, blk)).then_inc(tblk_in[p], 16)
                if has(j, -3, UNITS):
                    store(j - 3, (p - 3) % RING)

            over_ring(sp, UNITS, RING, step)
            for j in range(UNITS - 3, UNITS):
                store(j, j % RING)
            for p in range(RING):
                sp.wait_ge(stored[p], laps(UNITS - RING + p, p, RING, 16))

        @block.gpsimd
        def _(pool):
            over_ring(pool, UNITS, RING, lambda j, p: gather_step(
                nc, pool, u, j, p, table0, lambda s, t: rows[:, s, t, :], cols_in, gathered, wgt_done))

        @block.vector
        def _(dve):
            nc.vector.memset(acc[:, RING - 1, :], 0.0).then_inc(zeroed, 1)
            one_hot_stage(nc, dve, k, u, 0, 0, cols_in)

            def sums(j, p):
                dve.wait_ge(sum_mm, j + 1)
                if has(j, -RING, UNITS):
                    dve.wait_ge(stored[p], laps(j - RING, p, RING, 16))
                if has(j, -1, UNITS):
                    dve.wait_ge(acc_done, j)
                nc.vector.scalar_tensor_tensor(
                    out=acc[:, p, :], in0=acc[:, (p - 1) % RING, :], scalar=u.unit[:, p, 1:2], in1=p_sum[p % 2][:, :],
                    op0=ALU.mult, op1=ALU.add).then_inc(acc_done, 1)

            def step(j, p):
                q = p % 2
                dve.wait_ge(gathered[p], laps(j, p, RING, 16 * TILES))
                dve.wait_ge(tgt_mm, j + 1)
                if has(j, -2, UNITS):
                    dve.wait_ge(exp_done, j - 1)
                nc.vector.tensor_tensor(score[:, q, :, :], rows[:, p, :, D:], p_tgt[q][:, :, :], ALU.add).then_inc(score_done, 1)
                dve.wait_ge(score_done, j + 1)
                nc.vector.scalar_tensor_tensor(
                    out=leak[:, q, :, :].rearrange("p t h -> p (t h)"), in0=score[:, q, :, :].rearrange("p t h -> p (t h)"),
                    scalar=0.2, in1=score[:, q, :, :].rearrange("p t h -> p (t h)"), op0=ALU.mult, op1=ALU.max).then_inc(leak_done, 1)
                if has(j, 1, UNITS):
                    n = (p + 1) % RING
                    if has(j, 1 - RING, UNITS):
                        dve.wait_ge(sum_mm, j + 2 - RING)
                    one_hot_stage(nc, dve, k, u, j + 1, n, cols_in)
                if has(j, -1, UNITS):
                    sums(j - 1, (p - 1) % RING)
                dve.wait_ge(exp_done, j + 1)
                nc.vector.tensor_tensor(
                    wgt[:, p, :, :, 0:C], rows[:, p, :, 0:D].rearrange("p t (h c) -> p t h c", h=H),
                    wgt[:, p, :, :, C:HC].to_broadcast([P, TILES, H, C]), ALU.mult).then_inc(wgt_done, 1)

            over_ring(dve, UNITS, RING, step)
            sums(UNITS - 1, (UNITS - 1) % RING)

        @block.scalar
        def _(act):
            def unit_col(j, p):
                if has(j, -RING, UNITS):
                    act.wait_ge(acc_done, j - RING + 1)
                nc.scalar.copy(u.unit[:, p, :], k.ucol[:, bass.ds(j, 1), :].rearrange("p o c -> p (o c)")).then_inc(u.ucol_in, 1)

            def transposed(j, p):
                act.wait_ge(oht_mm, j + 1)
                if has(j, -RING, UNITS):
                    act.wait_ge(tgt_mm, j - RING + 1)
                nc.scalar.copy(onehot_t[:, p, :], p_oht[p % 2][:, :]).then_inc(oht_done, 1)

            unit_col(0, 0)
            unit_col(1, 1)
            transposed(0, 0)

            def step(j, p):
                if has(j, 2, UNITS):
                    unit_col(j + 2, (p + 2) % RING)
                act.wait_ge(leak_done, j + 1)
                if has(j, -RING, UNITS):
                    act.wait_ge(sum_mm, j - RING + 1)
                nc.scalar.activation(wgt[:, p, :, :, C], leak[:, p % 2, :, :], ACT.Exp).then_inc(exp_done, 1)
                if has(j, 1, UNITS):
                    transposed(j + 1, (p + 1) % RING)

            over_ring(act, UNITS, RING, step)

        @block.tensor
        def _(pe):
            def transposes(j, p):
                pe.wait_ge(u.onehot_done, j + 1)
                if has(j, -2, UNITS):
                    pe.wait_ge(oht_done, j - 1)
                for t in range(TILES):
                    last = nc.tensor.transpose(p_oht[p % 2][:, t * P:(t + 1) * P], u.onehot[:, p, t, :], k.ident[:, :])
                last.then_inc(oht_mm, 1)

            def target_scores(j, p):
                pe.wait_ge(oht_done, j + 1)
                pe.wait_ge(tblk_in[p], laps(j, p, RING, 16))
                if has(j, -2, UNITS):
                    pe.wait_ge(score_done, j - 1)
                for t in range(TILES):
                    last = nc.tensor.matmul(p_tgt[p % 2][:, t, :], onehot_t[:, p, t * P:(t + 1) * P], tblk[:, p, :], start=True, stop=True)
                last.then_inc(tgt_mm, 1)

            transposes(0, 0)
            target_scores(0, 0)

            def step(j, p):
                if has(j, 1, UNITS):
                    transposes(j + 1, (p + 1) % RING)
                pe.wait_ge(wgt_done, j + 1)
                if has(j, -2, UNITS):
                    pe.wait_ge(acc_done, j - 1)
                for t in range(TILES):
                    last = nc.tensor.matmul(p_sum[p % 2][:, :], u.onehot[:, p, t, :], wgt[:, p, t, :, :].rearrange("p h c -> p (h c)"),
                                            start=(t == 0), stop=(t == TILES - 1))
                last.then_inc(sum_mm, 1)
                if has(j, 1, UNITS):
                    target_scores(j + 1, (p + 1) % RING)

            over_ring(pe, UNITS, RING, step)


def step_rows(table, j):
    return table.rearrange("(s b p) c -> s p b c", b=NBLK, p=P)[bass.ds(j, 1), :, :, :].rearrange("o p b c -> (o p) b c")


class LayerNorm:

    def __init__(self, nc, st, name):
        self.nc = nc
        self.stats = st.sb(name + "_stats", [P, NBLK, 6])
        self.mv = st.sb(name + "_mv", [P, NBLK, 2])
        self.std = st.sb(name + "_std", [P, NBLK])
        self.rstd = st.sb(name + "_rstd", [P, NBLK])
        self.stats_done, self.mv_done = st.sem(name + "_stats_done"), st.sem(name + "_mv_done")
        self.passed = st.sem(name + "_passed")
        self.std_done, self.rstd_done = st.sem(name + "_std_done"), st.sem(name + "_rstd_done")

    def on_vector(self, dve, j, y, out, done):
        nc = self.nc
        for b in range(NBLK):
            last = nc.vector.bn_stats(self.stats[:, b, :], y[:, b, :])
        last.then_inc(self.stats_done, 1)
        dve.wait_ge(self.stats_done, j + 1)
        gate(dve, self.passed)
        for b in range(NBLK):
            last = nc.vector.bn_aggr(self.mv[:, b, :], self.stats[:, b, :])
        last.then_inc(self.mv_done, 1)
        dve.wait_ge(self.std_done, j + 1)
        nc.vector.reciprocal(self.rstd[:, :], self.std[:, :]).then_inc(self.rstd_done, 1)
        dve.wait_ge(self.rstd_done, j + 1)
        for b in range(NBLK):
            last = nc.vector.tensor_scalar(out[:, b, :], y[:, b, :], self.mv[:, b, 0:1], self.rstd[:, b:b + 1],
                                           ALU.subtract, ALU.mult)
        last.then_inc(done, 1)

    def on_scalar(self, act, k, j):
        act.wait_ge(self.mv_done, j + 1)
        self.nc.scalar.activation(self.std[:, :], self.mv[:, :, 1], ACT.Sqrt, bias=k.eps[:, 0:1]).then_inc(self.std_done, 1)


def middle(nc, st, k, a, agg0, kv_table, node1):
    agg = st.sb("m_agg", [P, NBLK, NBLK, H, HC])
    xin = st.sb("m_xin", [P, NBLK, NBLK, D])
    den = st.sb("m_den", [P, NBLK, H])
    rec = st.sb("m_rec", [P, NBLK, H])
    att = st.sb("m_att", [P, NBLK, D])
    attb = st.sb("m_attb", [P, NBLK, D])
    y = st.sb("m_y", [P, NBLK, D])
    x1t = st.sb("m_x1t", [P, NBLK, P])
    node = st.sb("m_node", [P, NBLK, NBLK, NODE1])
    kv = st.sb("m_kv", [P, NBLK, NBLK, 2 * D])
    p_t = st.ps("m_p_t", [P, NBLK, P])
    p_w = [st.ps(f"m_p_w{b}", [P, 4 * D]) for b in range(NBLK)]
    ln = LayerNorm(nc, st, "m_ln")
    loaded = st.ring_sems("m_loaded", NBLK)
    stored = st.ring_sems("m_stored", NBLK)
    scaled, den_done, rec_done = st.sem("m_scaled"), st.sem("m_den_done"), st.sem("m_rec_done")
    att_done, attb_done, y_done = st.sem("m_att_done"), st.sem("m_attb_done"), st.sem("m_y_done")
    x1_done, t_mm, x1t_done = st.sem("m_x1_done"), st.sem("m_t_mm"), st.sem("m_x1t_done")
    w_mm, split_done, node_done = st.sem("m_w_mm"), st.sem("m_split_done"), st.sem("m_node_done")
    steps = BLOCKS // NBLK
    with nc.Block() as block:

        @block.sync
        def _(sp):
            def step(j, p):
                if has(j, -NBLK, steps):
                    sp.wait_ge(y_done, j - NBLK + 1)
                sp.dma_start(agg[:, p, :, :, :].rearrange("p b h c -> p b (h c)"), step_rows(agg0, j)).then_inc(loaded[p], 16)
                sp.dma_start(xin[:, p, :, :], step_rows(a["x_rows"], j)).then_inc(loaded[p], 16)

            over_ring(sp, steps, NBLK, step)

        @block.vector
        def _(dve):
            nc.vector.tensor_scalar(k.wcat1[:, 0:D], k.wcat1[:, 0:D], float(C) ** -0.5, None, ALU.mult).then_inc(scaled, 1)
            nc.vector.tensor_scalar(k.bcat1[:, 0:D], k.bcat1[:, 0:D], float(C) ** -0.5, None, ALU.mult).then_inc(scaled, 1)
            dve.wait_ge(scaled, 2)

            def step(j, p):
                dve.wait_ge(loaded[p], laps(j, p, NBLK, 32))
                if has(j, -NBLK, steps):
                    dve.wait_ge(stored[p], laps(j - NBLK, p, NBLK, 32))
                nc.vector.tensor_scalar(den[:, :, :], agg[:, p, :, :, C], 1e-16, None, ALU.add).then_inc(den_done, 1)
                dve.wait_ge(den_done, j + 1)
                nc.vector.reciprocal(rec[:, :, :], den[:, :, :]).then_inc(rec_done, 1)
                dve.wait_ge(rec_done, j + 1)
                nc.vector.tensor_tensor(att[:, :, :].rearrange("p b (h c) -> p b h c", h=H), agg[:, p, :, :, 0:C],
                                        rec[:, :, :].unsqueeze(3).to_broadcast([P, NBLK, H, C]), ALU.mult).then_inc(att_done, 1)
                dve.wait_ge(att_done, j + 1)
                nc.vector.tensor_tensor(attb[:, :, :], att[:, :, :], k.bias0[:, :].unsqueeze(1).to_broadcast([P, NBLK, D]), ALU.add).then_inc(attb_done, 1)
                dve.wait_ge(attb_done, j + 1)
                nc.vector.tensor_tensor(y[:, :, :], attb[:, :, :], xin[:, p, :, :], ALU.add).then_inc(y_done, 1)
                dve.wait_ge(y_done, j + 1)
                ln.on_vector(dve, j, y[:, :, :], node[:, p, :, 2 * D:], x1_done)
                for b in range(NBLK):
                    if b == 0:
                        dve.wait_ge(w_mm, j + 1)
                    w = p_w[b]
                    nc.vector.tensor_tensor(kv[:, p, b, :], w[:, D:3 * D], k.bcat1[:, D:3 * D], ALU.add).then_inc(split_done, 1)
                    nc.vector.tensor_tensor(node[:, p, b, 0:D], w[:, 0:D], k.bcat1[:, 0:D], ALU.add).then_inc(split_done, 1)
                    nc.vector.tensor_tensor(node[:, p, b, D:2 * D], w[:, 3 * D:], k.bcat1[:, 3 * D:], ALU.add).then_inc(split_done, 1)
                dve.wait_ge(split_done, 9 * j + 9)
                nc.vector.tensor_tensor(node[:, p, :, D:2 * D], node[:, p, :, D:2 * D], node[:, p, :, 2 * D:], ALU.add).then_inc(node_done, 1)

            over_ring(dve, steps, NBLK, step)

        @block.tensor
        def _(pe):
            pe.wait_ge(scaled, 2)

            def step(j, p):
                pe.wait_ge(x1_done, j + 1)
                if has(j, -1, steps):
                    pe.wait_ge(x1t_done, j)
                for b in range(NBLK):
                    last = nc.tensor.transpose(p_t[:, b, :], node[:, p, b, 2 * D:], k.ident[:, :])
                last.then_inc(t_mm, 1)
                pe.wait_ge(x1t_done, j + 1)
                if has(j, -1, steps):
                    pe.wait_ge(node_done, j)
                for b in range(NBLK):
                    last = nc.tensor.matmul(p_w[b][:, :], x1t[:, b, :], k.wcat1[:, :], start=True, stop=True)
                last.then_inc(w_mm, 1)

            over_ring(pe, steps, NBLK, step)

        @block.scalar
        def _(act):
            def step(j, p):
                ln.on_scalar(act, k, j)
                act.wait_ge(t_mm, j + 1)
                if has(j, -1, steps):
                    act.wait_ge(w_mm, j)
                nc.scalar.copy(x1t[:, :, :], p_t[:, :, :]).then_inc(x1t_done, 1)

            over_ring(act, steps, NBLK, step)

        @block.gpsimd
        def _(pool):
            def step(j, p):
                pool.wait_ge(node_done, j + 1)
                pool.dma_start(step_rows(kv_table, j), kv[:, p, :, :]).then_inc(stored[p], 16)
                pool.dma_start(step_rows(node1, j), node[:, p, :, :]).then_inc(stored[p], 16)

            over_ring(pool, steps, NBLK, step)
            for p in range(NBLK):
                pool.wait_ge(stored[p], laps(steps - NBLK + p, p, NBLK, 32))


def edge_layer(nc, st, k, a, kv_table, node1, neg_rows, agg1):
    u = Names()
    u.cols = st.sb("e_cols", [P, RING, 3 * TILES], I32)
    u.unit = st.sb("e_unit", [P, RING, 3])
    u.rel = st.sb("e_rel", [P, RING, TILES])
    u.onehot = st.sb("e_onehot", [P, RING, TILES, P])
    onehot_t = st.sb("e_onehot_t", [P, RING, TILES * P])
    kv = st.sb("e_kv", [P, RING, TILES, 2, D])
    attr = st.sb("e_attr", [ED, RING, GE])
    neg = st.sb("e_neg", [TILES * H, RING, P])
    qblk = st.sb("e_qblk", [P, RING, D])
    prod = st.sb("e_prod", [P, TILES * H, C])
    logit = st.sb("e_logit", [P, RING, TILES, H])
    runmax = st.sb("e_runmax", [TILES * H, RING, P])
    lastmax = st.sb("e_lastmax", [P, RING, TILES, H + 1])
    absent = st.sb("e_absent", [P, TILES])
    cand = st.sb("e_cand", [P, TILES, H])
    newmax = st.sb("e_newmax", [P, H])
    before = st.sb("e_before", [P, H])
    top = st.sb("e_top", [P, RING, H])
    drop = st.sb("e_drop", [P, H])
    scale = st.sb("e_scale", [P, 2, H])
    shifted = st.sb("e_shifted", [P, 2, TILES, H])
    wgt = st.sb("e_wgt", [P, RING, TILES, H, HC])
    scaled = st.sb("e_scaled", [P, H, HC])
    acc = st.sb("e_acc", [P, RING, H, HC])
    p_oht = st.ps("e_p_oht", [P, TILES * P])
    p_e = st.ps("e_p_e", [P, TILES, D])
    p_q = st.ps("e_p_q", [P, TILES, D])
    p_lt = st.ps("e_p_lt", [TILES * H, P])
    p_small = st.ps("e_p_small", [P, 3, P])
    p_sum = st.ps("e_p_sum", [P, H, HC])
    p_run = p_small[:, 0, 0:TILES * H].rearrange("p (t h) -> p t h", h=H)
    p_node = p_small[:, 1, 0:TILES * (H + 1)].rearrange("p (t h) -> p t h", h=H + 1)
    p_top = p_small[:, 2, 0:TILES * H].rearrange("p (t h) -> p t h", h=H)
    sp_passed, pe_passed = st.sem("e_sp_passed"), st.sem("e_pe_passed")
    cols_in = st.ring_sems("e_cols_in", RING)
    blk_in = st.ring_sems("e_blk_in", RING)
    gathered = st.ring_sems("e_gathered", RING)
    stored = st.ring_sems("e_stored", RING)
    u.ucol_in, u.rel_done = st.sem("e_ucol_in"), st.sem("e_rel_done")
    u.onehot_done, u.admitted = st.sem("e_onehot_done"), st.sem("e_admitted")
    oht_mm, oht_done, e_mm, q_mm = st.sem("e_oht_mm"), st.sem("e_oht_done"), st.sem("e_e_mm"), st.sem("e_q_mm")
    kv_done, prod_done, logit_done = st.sem("e_kv_done"), st.sem("e_prod_done"), st.sem("e_logit_done")
    lt_mm, run_done, run_mm = st.sem("e_lt_mm"), st.sem("e_run_done"), st.sem("e_run_mm")
    last_done, lastmax_done, node_mm = st.sem("e_last_done"), st.sem("e_lastmax_done"), st.sem("e_node_mm")
    absent_done, cand_done, newmax_done = st.sem("e_absent_done"), st.sem("e_cand_done"), st.sem("e_newmax_done")
    before_done, top_done, drop_done = st.sem("e_before_done"), st.sem("e_top_done"), st.sem("e_drop_done")
    scale_done, top_mm, shifted_done = st.sem("e_scale_done"), st.sem("e_top_mm"), st.sem("e_shifted_done")
    exp_done, wgt_done, sum_mm = st.sem("e_exp_done"), st.sem("e_wgt_done"), st.sem("e_sum_mm")
    scaled_done, acc_done, zeroed = st.sem("e_scaled_done"), st.sem("e_acc_done"), st.sem("e_zeroed")

    with nc.Block() as block:

        @block.sync
        def _(sp):
            def store(j, p):
                blk = sp.value_load(k.ureg[0:1, bass.ds(j, 1), 1], min_val=0, max_val=BLOCKS - 1)
                sp.wait_ge(acc_done, j + 1)
                gate(sp, sp_passed)
                if has(j, -1, UNITS):
                    q = (p - 1) % RING
                    sp.wait_ge(stored[q], laps(j - 1, q, RING, 16))
                    gate(sp, sp_passed)
                sp.dma_start(rows_of(agg1, blk), acc[:, p, :, :].rearrange("p h c -> p (h c)")).then_inc(stored[p], 16)

            def step(j, p):
                grp = sp.value_load(k.ureg[0:1, bass.ds(j, 1), 0], min_val=0, max_val=GROUPS - 1)
                blk = sp.value_load(k.ureg[0:1, bass.ds(j, 1), 1], min_val=0, max_val=BLOCKS - 1)
                if has(j, -RING, UNITS):
                    sp.wait_ge(gathered[p], laps(j - RING, p, RING, 16 * TILES))
                    gate(sp, sp_passed)
                    sp.wait_ge(last_done, j - RING + 1)
                    gate(sp, sp_passed)
                sp.dma_start(u.cols[:, p, :], a["edge_cols"][bass.ds(grp, 1), :, :].rearrange("o p c -> (o p) c")).then_inc(cols_in[p], 16)
                if has(j, -RING, UNITS):
                    sp.wait_ge(run_done, j - RING + 1)
                    gate(sp, sp_passed)
                sp.dma_start(attr[:, p, :], a["attr_t"][bass.ds(grp, 1), :, :].rearrange("o p c -> (o p) c")).then_inc(blk_in[p], 16)
                sp.dma_start(qblk[:, p, :], rows_of(node1, blk)[:, 0:D]).then_inc(blk_in[p], 16)
                sp.dma_start(neg[:, p, :], neg_rows.rearrange("(g t) h e -> g (t h) e", t=TILES)[bass.ds(grp, 1), :, :]
                             .rearrange("o p c -> (o p) c")).then_inc(blk_in[p], 16)
                if has(j, -4, UNITS):
                    store(j - 4, p)

            over_ring(sp, UNITS, RING, step)
            for j in range(UNITS - 4, UNITS):
                store(j, j % RING)
            for p in range(RING):
                sp.wait_ge(stored[p], laps(UNITS - RING + p, p, RING, 16))

        @block.gpsimd
        def _(pool):
            over_ring(pool, UNITS, RING, lambda j, p: gather_step(
                nc, pool, u, j, p, kv_table, lambda s, t: kv[:, s, t, :, :].rearrange("p a c -> p (a c)"), cols_in, gathered, wgt_done))

        @block.vector
        def _(dve):
            def hot(j, p):
                if has(j, -RING, UNITS):
                    dve.wait_ge(sum_mm, j - RING + 1)
                one_hot_stage(nc, dve, k, u, j, p, cols_in)
                nc.vector.tensor_tensor(lastmax[:, p, :, H], u.cols[:, p, TILES:2 * TILES], u.cols[:, p, 2 * TILES:], ALU.not_equal).then_inc(last_done, 1)

            def keys(j, p):
                dve.wait_ge(gathered[p], laps(j, p, RING, 16 * TILES))
                dve.wait_ge(e_mm, j + 1)
                nc.vector.tensor_tensor(kv[:, p, :, :, :], kv[:, p, :, :, :], p_e[:, :, :].unsqueeze(2).to_broadcast([P, TILES, 2, D]), ALU.add).then_inc(kv_done, 1)

            def products(j, p):
                dve.wait_ge(kv_done, j + 1)
                dve.wait_ge(q_mm, j + 1)
                if has(j, -1, UNITS):
                    dve.wait_ge(logit_done, j)
                nc.vector.tensor_tensor(prod[:, :, :].rearrange("p (t h) c -> p t (h c)", t=TILES), kv[:, p, :, 0, :], p_q[:, :, :], ALU.mult).then_inc(prod_done, 1)

            def logits(j, p):
                dve.wait_ge(prod_done, j + 1)
                nc.vector.tensor_reduce(out=logit[:, p, :, :].rearrange("p t h -> p (t h)"), in_=prod[:, :, :], op=ALU.add, axis=AX.X).then_inc(logit_done, 1)

            nc.vector.memset(acc[:, RING - 1, :, :], 0.0).then_inc(zeroed, 1)
            nc.vector.memset(top[:, RING - 1, :], -FAR).then_inc(zeroed, 1)
            hot(0, 0)
            hot(1, 1)
            keys(0, 0)
            products(0, 0)
            logits(0, 0)
            dve.wait_ge(zeroed, 2)

            def step(j, p):
                n, b = (p + 1) % RING, p % 2
                more = has(j, 1, UNITS)
                dve.wait_ge(lt_mm, j + 1)
                dve.wait_ge(blk_in[p], laps(j, p, RING, 48))
                nc.vector.tensor_tensor_scan(runmax[:, p, :], neg[:, p, :], p_lt[:, :], -3.0e38, ALU.add, ALU.max).then_inc(run_done, 1)
                if more:
                    keys(j + 1, n)
                dve.wait_ge(run_mm, j + 1)
                dve.wait_ge(last_done, j + 1)
                nc.vector.tensor_tensor(lastmax[:, p, :, 0:H], p_run, lastmax[:, p, :, H:].to_broadcast([P, TILES, H]), ALU.mult).then_inc(lastmax_done, 1)
                if more:
                    products(j + 1, n)
                if has(j, -1, UNITS):
                    dve.wait_ge(top_done, j)
                nc.vector.tensor_scalar(before[:, :], top[:, (p - 1) % RING, :], u.unit[:, p, 1:2], u.unit[:, p, 2:3], ALU.mult, ALU.add).then_inc(before_done, 1)
                dve.wait_ge(node_mm, j + 1)
                nc.vector.tensor_scalar(absent[:, :], p_node[:, :, H], -1.0, FAR, ALU.add, ALU.mult).then_inc(absent_done, 1)
                dve.wait_ge(absent_done, j + 1)
                nc.vector.tensor_tensor(cand[:, :, :], p_node[:, :, 0:H], absent[:, :].unsqueeze(2).to_broadcast([P, TILES, H]), ALU.add).then_inc(cand_done, 1)
                dve.wait_ge(cand_done, j + 1)
                nc.vector.tensor_reduce(out=newmax[:, :], in_=cand[:, :, :].rearrange("p t h -> p h t"), op=ALU.max, axis=AX.X).then_inc(newmax_done, 1)
                dve.wait_ge(newmax_done, j + 1)
                dve.wait_ge(before_done, j + 1)
                nc.vector.tensor_tensor(top[:, p, :], newmax[:, :], before[:, :], ALU.max).then_inc(top_done, 1)
                dve.wait_ge(top_done, j + 1)
                if has(j, -1, UNITS):
                    dve.wait_ge(scale_done, j)
                nc.vector.tensor_tensor(drop[:, :], before[:, :], top[:, p, :], ALU.subtract).then_inc(drop_done, 1)
                if more:
                    logits(j + 1, n)
                dve.wait_ge(top_mm, j + 1)
                if has(j, -2, UNITS):
                    dve.wait_ge(exp_done, j - 1)
                nc.vector.tensor_tensor(shifted[:, b, :, :], logit[:, p, :, :], p_top, ALU.subtract).then_inc(shifted_done, 1)
                if has(j, 2, UNITS):
                    hot(j + 2, (p + 2) % RING)
                dve.wait_ge(exp_done, j + 1)
                nc.vector.tensor_tensor(
                    wgt[:, p, :, :, 0:C], kv[:, p, :, 1, :].rearrange("p t (h c) -> p t h c", h=H),
                    wgt[:, p, :, :, C:HC].to_broadcast([P, TILES, H, C]), ALU.mult).then_inc(wgt_done, 1)
                dve.wait_ge(scale_done, j + 1)
                if has(j, -1, UNITS):
                    dve.wait_ge(acc_done, j)
                nc.vector.tensor_tensor(scaled[:, :, :], acc[:, (p - 1) % RING, :, :],
                                        scale[:, b, :].unsqueeze(2).to_broadcast([P, H, HC]), ALU.mult).then_inc(scaled_done, 1)
                dve.wait_ge(scaled_done, j + 1)
                dve.wait_ge(sum_mm, j + 1)
                if has(j, -RING, UNITS):
                    dve.wait_ge(stored[p], laps(j - RING, p, RING, 16))
                nc.vector.tensor_tensor(acc[:, p, :, :], scaled[:, :, :], p_sum[:, :, :], ALU.add).then_inc(acc_done, 1)

            over_ring(dve, UNITS, RING, step)

        @block.scalar
        def _(act):
            def unit_col(j, p):
                if has(j, -RING, UNITS):
                    act.wait_ge(acc_done, j - RING + 1)
                nc.scalar.copy(u.unit[:, p, :], k.ucol[:, bass.ds(j, 1), :].rearrange("p o c -> p (o c)")).then_inc(u.ucol_in, 1)

            def transposed(j, p):
                act.wait_ge(oht_mm, j + 1)
                if has(j, -RING, UNITS):
                    act.wait_ge(top_mm, j - RING + 1)
                nc.scalar.copy(onehot_t[:, p, :], p_oht[:, :]).then_inc(oht_done, 1)

            for j in range(3):
                unit_col(j, j)
            transposed(0, 0)
            transposed(1, 1)

            def step(j, p):
                if has(j, 3, UNITS):
                    unit_col(j + 3, (p + 3) % RING)
                act.wait_ge(drop_done, j + 1)
                if has(j, -2, UNITS):
                    act.wait_ge(scaled_done, j - 1)
                nc.scalar.activation(scale[:, p % 2, :], drop[:, :], ACT.Exp).then_inc(scale_done, 1)
                act.wait_ge(shifted_done, j + 1)
                if has(j, -RING, UNITS):
                    act.wait_ge(sum_mm, j - RING + 1)
                nc.scalar.activation(wgt[:, p, :, :, C], shifted[:, p % 2, :, :], ACT.Exp).then_inc(exp_done, 1)
                if has(j, 2, UNITS):
                    transposed(j + 2, (p + 2) % RING)

            over_ring(act, UNITS, RING, step)

        @block.tensor
        def _(pe):
            def transposes(j, p):
                pe.wait_ge(u.onehot_done, j + 1)
                if has(j, -1, UNITS):
                    pe.wait_ge(oht_done, j)
                for t in range(TILES):
                    last = nc.tensor.transpose(p_oht[:, t * P:(t + 1) * P], u.onehot[:, p, t, :], k.ident[:, :])
                last.then_inc(oht_mm, 1)

            def edge_features(j, p):
                pe.wait_ge(blk_in[p], laps(j, p, RING, 48))
                if has(j, -1, UNITS):
                    pe.wait_ge(kv_done, j)
                for t in range(TILES):
                    last = nc.tensor.matmul(p_e[:, t, :], attr[:, p, t * P:(t + 1) * P], k.we[:, :], start=True, stop=True)
                last.then_inc(e_mm, 1)

            def queries(j, p):
                pe.wait_ge(oht_done, j + 1)
                if has(j, -1, UNITS):
                    pe.wait_ge(prod_done, j)
                for t in range(TILES):
                    last = nc.tensor.matmul(p_q[:, t, :], onehot_t[:, p, t * P:(t + 1) * P], qblk[:, p, :], start=True, stop=True)
                last.then_inc(q_mm, 1)

            def logits_t(j, p):
                pe.wait_ge(logit_done, j + 1)
                if has(j, -1, UNITS):
                    pe.wait_ge(run_done, j)
                nc.tensor.transpose(p_lt[:, :], logit[:, p, :, :].rearrange("p t h -> p (t h)"), k.ident[:, :]).then_inc(lt_mm, 1)

            for j in range(2):
                transposes(j, j)
                edge_features(j, j)
                queries(j, j)
            logits_t(0, 0)

            def step(j, p):
                pe.wait_ge(run_done, j + 1)
                if has(j, -1, UNITS):
                    pe.wait_ge(shifted_done, j)
                gate(pe, pe_passed)
                nc.tensor.transpose(p_small[:, 0, 0:TILES * H], runmax[:, p, :], k.ident[0:TILES * H, 0:TILES * H]).then_inc(run_mm, 1)
                pe.wait_ge(lastmax_done, j + 1)
                for t in range(TILES):
                    last = nc.tensor.matmul(p_node[:, t, :], u.onehot[:, p, t, :], lastmax[:, p, t, :], start=True, stop=True)
                last.then_inc(node_mm, 1)
                pe.wait_ge(top_done, j + 1)
                for t in range(TILES):
                    last = nc.tensor.matmul(p_top[:, t, :], onehot_t[:, p, t * P:(t + 1) * P], top[:, p, :], start=True, stop=True)
                last.then_inc(top_mm, 1)
                if has(j, 1, UNITS):
                    logits_t(j + 1, (p + 1) % RING)
                if has(j, 2, UNITS):
                    transposes(j + 2, (p + 2) % RING)
                    edge_features(j + 2, (p + 2) % RING)
                pe.wait_ge(wgt_done, j + 1)
                if has(j, -1, UNITS):
                    pe.wait_ge(acc_done, j)
                for t in range(TILES):
                    last = nc.tensor.matmul(p_sum[:, :, :].rearrange("p h c -> p (h c)"), u.onehot[:, p, t, :],
                                            wgt[:, p, t, :, :].rearrange("p h c -> p (h c)"), start=(t == 0), stop=(t == TILES - 1))
                last.then_inc(sum_mm, 1)
                if has(j, 2, UNITS):
                    queries(j + 2, (p + 2) % RING)

            over_ring(pe, UNITS, RING, step)


def finish(nc, st, k, agg1, node1, out):
    agg = st.sb("z_agg", [P, NBLK, NBLK, H, HC])
    nod = st.sb("z_nod", [P, NBLK, NBLK, 2 * D])
    den = st.sb("z_den", [P, NBLK, H])
    rec = st.sb("z_rec", [P, NBLK, H])
    conv = st.sb("z_conv", [P, NBLK, D])
    y1 = st.sb("z_y1", [P, NBLK, D])
    n1 = st.sb("z_n1", [P, NBLK, D])
    g1 = st.sb("z_g1", [P, NBLK, D])
    hid = st.sb("z_hid", [P, NBLK, D])
    hb = st.sb("z_hb", [P, NBLK, D])
    ht = st.sb("z_ht", [P, NBLK * P])
    act1 = st.sb("z_act1", [P, FF // P, NBLK * P])
    y2 = st.sb("z_y2", [P, NBLK, D])
    n2 = st.sb("z_n2", [P, NBLK, D])
    g2 = st.sb("z_g2", [P, NBLK, D])
    b2 = st.sb("z_b2", [P, NBLK, D])
    y3 = st.sb("z_y3", [P, NBLK, D])
    res = st.sb("z_res", [P, NBLK, NBLK, D])
    p_t = st.ps("z_p_t", [P, NBLK * P])
    p_f = [st.ps(f"z_p_f{i}", [P, NBLK * P]) for i in range(FF // P)]
    p_o = st.ps("z_p_o", [P, NBLK, D])
    ln1, ln2, ln3 = LayerNorm(nc, st, "z_ln1"), LayerNorm(nc, st, "z_ln2"), LayerNorm(nc, st, "z_ln3")
    loaded = st.ring_sems("z_loaded", NBLK)
    stored = st.ring_sems("z_stored", NBLK)
    den_done, rec_done, conv_done, y1_done = st.sem("z_den_done"), st.sem("z_rec_done"), st.sem("z_conv_done"), st.sem("z_y1_done")
    n1_done, g1_done, hid_done, hb_done = st.sem("z_n1_done"), st.sem("z_g1_done"), st.sem("z_hid_done"), st.sem("z_hb_done")
    t_mm, ht_done, f_mm, act_done = st.sem("z_t_mm"), st.sem("z_ht_done"), st.sem("z_f_mm"), st.sem("z_act_done")
    o_mm, y2_done, n2_done, g2_done = st.sem("z_o_mm"), st.sem("z_y2_done"), st.sem("z_n2_done"), st.sem("z_g2_done")
    b2_done, y3_done, res_done = st.sem("z_b2_done"), st.sem("z_y3_done"), st.sem("z_res_done")
    steps = BLOCKS // NBLK

    def wide(row):
        return row[:, :].unsqueeze(1).to_broadcast([P, NBLK, D])

    with nc.Block() as block:

        @block.sync
        def _(sp):
            def step(j, p):
                if has(j, -NBLK, steps):
                    sp.wait_ge(y3_done, j - NBLK + 1)
                sp.dma_start(agg[:, p, :, :, :].rearrange("p b h c -> p b (h c)"), step_rows(agg1, j)).then_inc(loaded[p], 16)
                sp.dma_start(nod[:, p, :, :], step_rows(node1, j)[:, :, D:]).then_inc(loaded[p], 16)

            over_ring(sp, steps, NBLK, step)

        @block.vector
        def _(dve):
            def step(j, p):
                dve.wait_ge(loaded[p], laps(j, p, NBLK, 32))
                nc.vector.tensor_scalar(den[:, :, :], agg[:, p, :, :, C], 1e-30, None, ALU.max).then_inc(den_done, 1)
                dve.wait_ge(den_done, j + 1)
                nc.vector.reciprocal(rec[:, :, :], den[:, :, :]).then_inc(rec_done, 1)
                dve.wait_ge(rec_done, j + 1)
                nc.vector.tensor_tensor(conv[:, :, :].rearrange("p b (h c) -> p b h c", h=H), agg[:, p, :, :, 0:C],
                                        rec[:, :, :].unsqueeze(3).to_broadcast([P, NBLK, H, C]), ALU.mult).then_inc(conv_done, 1)
                dve.wait_ge(conv_done, j + 1)
                nc.vector.tensor_tensor(y1[:, :, :], conv[:, :, :], nod[:, p, :, 0:D], ALU.add).then_inc(y1_done, 1)
                dve.wait_ge(y1_done, j + 1)
                ln1.on_vector(dve, j, y1[:, :, :], n1[:, :, :], n1_done)
                dve.wait_ge(n1_done, j + 1)
                nc.vector.tensor_tensor(g1[:, :, :], n1[:, :, :], wide(k.g1), ALU.mult).then_inc(g1_done, 1)
                dve.wait_ge(g1_done, j + 1)
                nc.vector.tensor_tensor(hid[:, :, :], g1[:, :, :], wide(k.b1), ALU.add).then_inc(hid_done, 1)
                dve.wait_ge(hid_done, j + 1)
                nc.vector.tensor_tensor(hb[:, :, :], hid[:, :, :], wide(k.bf2), ALU.add).then_inc(hb_done, 1)
                dve.wait_ge(hb_done, j + 1)
                dve.wait_ge(o_mm, j + 1)
                nc.vector.tensor_tensor(y2[:, :, :], hb[:, :, :], p_o[:, :, :], ALU.add).then_inc(y2_done, 1)
                dve.wait_ge(y2_done, j + 1)
                ln2.on_vector(dve, j, y2[:, :, :], n2[:, :, :], n2_done)
                dve.wait_ge(n2_done, j + 1)
                nc.vector.tensor_tensor(g2[:, :, :], n2[:, :, :], wide(k.g2), ALU.mult).then_inc(g2_done, 1)
                dve.wait_ge(g2_done, j + 1)
                nc.vector.tensor_tensor(b2[:, :, :], g2[:, :, :], wide(k.b2), ALU.add).then_inc(b2_done, 1)
                dve.wait_ge(b2_done, j + 1)
                nc.vector.tensor_tensor(y3[:, :, :], b2[:, :, :], nod[:, p, :, D:], ALU.add).then_inc(y3_done, 1)
                dve.wait_ge(y3_done, j + 1)
                if has(j, -NBLK, steps):
                    dve.wait_ge(stored[p], laps(j - NBLK, p, NBLK, 16))
                ln3.on_vector(dve, j, y3[:, :, :], res[:, p, :, :], res_done)

            over_ring(dve, steps, NBLK, step)

        @block.tensor
        def _(pe):
            def step(j, p):
                pe.wait_ge(hid_done, j + 1)
                for b in range(NBLK):
                    last = nc.tensor.transpose(p_t[:, b * P:(b + 1) * P], hid[:, b, :], k.ident[:, :])
                last.then_inc(t_mm, 1)
                pe.wait_ge(ht_done, j + 1)
                for f in range(FF // P):
                    nc.tensor.matmul(p_f[f][:, :], k.wf1[:, f * P:(f + 1) * P], ht[:, :], start=True, stop=True).then_inc(f_mm, 1)
                pe.wait_ge(act_done, 4 * j + 4)
                for b in range(NBLK):
                    for f in range(FF // P):
                        last = nc.tensor.matmul(p_o[:, b, :], act1[:, f, b * P:(b + 1) * P], k.wf2[:, f, :],
                                                start=(f == 0), stop=(f == FF // P - 1))
                last.then_inc(o_mm, 1)

            over_ring(pe, steps, NBLK, step)

        @block.scalar
        def _(act):
            def step(j, p):
                ln1.on_scalar(act, k, j)
                act.wait_ge(t_mm, j + 1)
                nc.scalar.copy(ht[:, :], p_t[:, :]).then_inc(ht_done, 1)
                for f in range(FF // P):
                    act.wait_ge(f_mm, 4 * j + f + 1)
                    nc.scalar.activation(act1[:, f, :], p_f[f][:, :], ACT.Gelu, bias=k.bf1[:, f:f + 1]).then_inc(act_done, 1)
                ln2.on_scalar(act, k, j)
                ln3.on_scalar(act, k, j)

            over_ring(act, steps, NBLK, step)

        @block.gpsimd
        def _(pool):
            def step(j, p):
                pool.wait_ge(res_done, j + 1)
                pool.dma_start(step_rows(out, j), res[:, p, :, :]).then_inc(stored[p], 16)

            over_ring(pool, steps, NBLK, step)
            for p in range(NBLK):
                pool.wait_ge(stored[p], laps(steps - NBLK + p, p, NBLK, 16))


def build(nc, a, out):

    def scratch(name, shape):
        return nc.dram_tensor(name, shape, F32, kind="Internal").ap()

    table0 = scratch("table0", [NPAD, ROW0])
    tgt0 = scratch("tgt0", [NPAD, H])
    agg0 = scratch("agg0", [NPAD, AGG])
    kv_table = scratch("kv_table", [NPAD, 2 * D])
    node1 = scratch("node1", [NPAD, NODE1])
    agg1 = scratch("agg1", [NPAD, AGG])
    neg_rows = scratch("neg_rows", [P * FLAG_TILES, H, P])

    with ExitStack() as ctx:
        st = Store(nc, ctx, ctx)
        k = Names()
        k.iota, k.ident, k.ones = st.sb("k_iota", [P, P]), st.sb("k_ident", [P, P]), st.sb("k_ones", [P, P])
        k.eps, k.part, k.block_start = st.sb("k_eps", [P, 1]), st.sb("k_part", [P, 1]), st.sb("k_block_start", [P, 1])
        k.ucol = st.sb("k_ucol", [P, UNITS, 3])
        k.ureg = st.sb("k_ureg", [1, UNITS, 2], I32)
        k.w0, k.w0t, k.att0 = st.sb("k_w0", [P, D]), st.sb("k_w0t", [P, D]), st.sb("k_att0", [P, 2 * H])
        k.bias0 = st.sb("k_bias0", [P, D])
        k.wcat1, k.bcat1, k.we = st.sb("k_wcat1", [P, 4 * D]), st.sb("k_bcat1", [P, 4 * D]), st.sb("k_we", [ED, D])
        k.g1, k.b1, k.g2, k.b2 = st.sb("k_g1", [P, D]), st.sb("k_b1", [P, D]), st.sb("k_g2", [P, D]), st.sb("k_b2", [P, D])
        k.wf1, k.bf1 = st.sb("k_wf1", [P, FF]), st.sb("k_bf1", [P, FF // P])
        k.wf2, k.bf2 = st.sb("k_wf2", [P, FF // P, D]), st.sb("k_bf2", [P, D])
        k.loaded = st.dma_sem("k_loaded")
        k.loads = [
            (k.w0[:, :], a["W0"]), (k.w0t[:, :], a["W0T"]), (k.att0[:, :], a["att0"]),
            (k.wcat1[:, :], a["wcat1"]), (k.we[:, :], a["We"]), (k.wf1[:, :], a["Wf1"]),
            (k.wf2[:, :, :], a["Wf2"]), (k.bf1[:, :], a["bf1"]),
            (k.bcat1[:, :], a["bcat1"].to_broadcast([P, 4 * D])),
        ] + [(t[:, :], a[n].to_broadcast([P, D])) for t, n in (
            (k.bias0, "bias0"), (k.g1, "g1"), (k.b1, "b1"), (k.g2, "g2"), (k.b2, "b2"), (k.bf2, "bf2"))]

        with ExitStack() as c:
            s = Store(nc, c, ctx)
            k.unit_row = s.sb("k_unit_row", [P, UNITS])
            constants(nc, s, k)
            unit_tables(nc, s, k, a)
            s.over()
        for stage, args in (
                (run_flags, (a, neg_rows)),
                (project0, (k, a, table0, tgt0)),
                (gat_layer, (k, a, table0, tgt0, agg0)),
                (middle, (k, a, agg0, kv_table, node1)),
                (edge_layer, (k, a, kv_table, node1, neg_rows, agg1)),
                (finish, (k, agg1, node1, out))):
            with ExitStack() as c:
                s = Store(nc, c, ctx)
                stage(nc, s, *args)
                s.over()


def kernel(**inputs):
    import numpy as np
    import concourse.bacc as bacc
    from concourse.bass_utils import run_bass_kernel_spmd

    i = {n: np.asarray(v) for n, v in inputs.items()}
    x = i["x"]
    x_rows = np.zeros((NPAD, D), x.dtype)
    x_rows[:NODES] = x
    src = np.zeros(GROUPS * GE, np.int32)
    src[:EDGES] = i["src"]
    dst = np.full(P * FLAG_TILES * P, NPAD, np.int32)
    dst[:EDGES] = i["dst"]
    prev = np.concatenate([dst[:1], dst[:-1]])
    dst_rows = dst.reshape(P, FLAG_TILES * P)
    prev_rows = prev.reshape(P, FLAG_TILES * P)
    dst = dst[:GROUPS * GE]
    nxt = np.concatenate([dst[1:], dst[-1:]]).reshape(-1, P).copy()
    nxt[:, -1] = -1
    edge_cols = np.concatenate([v.reshape(GROUPS, TILES, P).transpose(0, 2, 1) for v in (src, dst, nxt)], axis=2)
    attr = np.zeros((GROUPS * GE, ED), i["edge_attr_64"].dtype)
    attr[:EDGES] = i["edge_attr_64"]
    att0 = np.zeros((D, 2 * H), x.dtype)
    for h in range(H):
        att0[h * C:(h + 1) * C, h] = i["L0_gnn_a_left"][:, h]
        att0[h * C:(h + 1) * C, H + h] = i["L0_gnn_a_right"][:, h]
    arrays = {
        "x_rows": x_rows, "xT": x_rows.T, "edge_cols": edge_cols, "last_dst": dst[GE - 1::GE].reshape(1, GROUPS),
        "dst_rows": dst_rows, "dst_prev_rows": prev_rows, "attr_t": attr.reshape(GROUPS, GE, ED).transpose(0, 2, 1),
        "W0": i["L0_gnn_W"], "W0T": i["L0_gnn_W"].T, "att0": att0, "bias0": i["L0_gnn_bias"].reshape(1, D),
        "wcat1": np.concatenate([i["L1_gnn_W" + n] for n in ("q", "k", "v", "skip")], axis=1),
        "bcat1": np.concatenate([i["L1_gnn_b" + n] for n in ("q", "k", "v", "skip")]).reshape(1, 4 * D),
        "We": i["L1_gnn_We"], "Wf1": i["L1_gnn_Wf1"], "bf1": i["L1_gnn_bf1"].reshape(FF // P, P).T,
        "Wf2": i["L1_gnn_Wf2"].reshape(FF // P, P, D).transpose(1, 0, 2), "bf2": i["L1_gnn_bf2"].reshape(1, D),
        **{n: i["L1_gnn_" + n].reshape(1, D) for n in ("g1", "b1", "g2", "b2")},
    }
    nc = bacc.Bacc("TRN2", target_bir_lowering=False, num_devices=1)
    feed, aps = {}, {}
    for n, v in arrays.items():
        v = np.ascontiguousarray(v)
        feed["in_" + n] = v
        aps[n] = nc.dram_tensor("in_" + n, v.shape, mybir.dt.from_np(v.dtype), kind="ExternalInput").ap()
    out = nc.dram_tensor("out_rows", (NPAD, D), F32, kind="ExternalOutput").ap()
    build(nc, aps, out)
    r = run_bass_kernel_spmd(nc, [feed], core_ids=[0])
    return r.results[0]["out_rows"][:NODES]
```

```python
from contextlib import ExitStack

import concourse.bass as bass
from concourse import mybir

F32 = mybir.dt.float32
BF16 = mybir.dt.bfloat16
I32 = mybir.dt.int32
ALU = mybir.AluOpType
ACT = mybir.ActivationFunctionType
AX = mybir.AxisListType

P = 128
NODES, EDGES, D, H, ED, FF = 12500, 400000, 128, 8, 64, 512
C = D // H
TILES = 4
GE = TILES * P
GROUPS = -(-EDGES // GE)
RING = 8
BLOCKS = -(-NODES // P) + 1
UNITS = GROUPS + BLOCKS - 1
NPAD = BLOCKS * P
FLAG_TILES = 25
HC = C + 1
ROW0 = D + H
AGG = H * HC
NODE1 = 2 * D
PARTS = 3
FAR = 2.0 ** 100
NBLK = 3
EPS_LN = 1e-5

assert UNITS % RING == 0 and BLOCKS % NBLK == 0


def has(j, d, total):
    return 0 <= j + d < total if isinstance(j, int) else True


def staggered(eng, lead, lag, step):
    for s in range(-lead, RING):
        step(s, s % RING)
    with eng.Fori(RING, UNITS - 2 * RING + 1, RING) as base:
        for p in range(RING):
            step(base + p, p)
    for s in range(UNITS - RING, UNITS + lag):
        step(s, s % RING)


def laps(j, p, ring, n):
    if isinstance(j, int):
        return n * (j // ring + 1)
    return (j - p) * (n // ring) + n if n % ring == 0 else ((j - p) * n) // ring + n


def over_ring(eng, total, ring, step):
    for p in range(ring):
        step(p, p)
    with eng.Fori(ring, total - 2 * ring + 1, ring) as base:
        for p in range(ring):
            step(base + p, p)
    for p in range(ring):
        step(total - ring + p, p)


def gate(eng, passed):
    eng.sem_inc(passed, 1)


class Store:

    def __init__(self, nc, ctx, whole):
        self.nc, self.ctx, self.whole, self.counted = nc, ctx, whole, []

    def sb(self, name, shape, dt=F32):
        return self.ctx.enter_context(self.nc.sbuf_tensor(name, shape, dt))

    def ps(self, name, shape, dt=F32):
        return self.ctx.enter_context(self.nc.psum_tensor(name, shape, dt))

    def sem(self, name):
        self.counted.append(self.ctx.enter_context(self.nc.semaphore(name)))
        return self.counted[-1]

    def dma_sem(self, name):
        return self.whole.enter_context(self.nc.semaphore(name))

    def ring_sems(self, name, n):
        return [self.dma_sem(f"{name}{i}") for i in range(n)]

    def over(self):
        with self.nc.Block() as block:

            @block.sync
            def _(sp):
                for sem in self.counted:
                    sp.sem_clear(sem)


class Names:
    pass


def constants(nc, st, k):
    iota_i = st.sb("iota_i", [P, P], I32)
    part_i = st.sb("part_i", [P, 1], I32)
    unit_i = st.sb("unit_i", [P, UNITS], I32)
    part_f = st.sb("part_f", [P, 1])
    iota_s = st.sem("c_iota")
    done_s = st.sem("c_done")
    conv_s = st.sem("c_conv")
    with nc.Block() as block:

        @block.gpsimd
        def _(pool):
            nc.gpsimd.iota(iota_i[:, :], pattern=[[1, P]], base=0, channel_multiplier=0).then_inc(iota_s, 1)
            nc.gpsimd.iota(part_i[:, :], pattern=[[0, 1]], base=0, channel_multiplier=1).then_inc(iota_s, 1)
            nc.gpsimd.iota(unit_i[:, :], pattern=[[1, UNITS]], base=0, channel_multiplier=0).then_inc(iota_s, 1)

        @block.vector
        def _(dve):
            dve.wait_ge(iota_s, 3)
            nc.vector.tensor_copy(k.iota_b[:, :], iota_i[:, :]).then_inc(done_s, 1)
            nc.vector.tensor_copy(k.iota[:, :], iota_i[:, :]).then_inc(conv_s, 1)
            nc.vector.tensor_copy(part_f[:, :], part_i[:, :]).then_inc(conv_s, 1)
            nc.vector.tensor_copy(k.unit_row[:, :], unit_i[:, :]).then_inc(conv_s, 1)
            nc.vector.memset(k.ones[:, :], 1.0).then_inc(done_s, 1)
            nc.vector.memset(k.eps[:, :], EPS_LN).then_inc(done_s, 1)
            dve.wait_ge(conv_s, 3)
            nc.vector.tensor_scalar(k.ident_b[:, :], k.iota[:, :], part_f[:, 0:1], None, ALU.is_equal).then_inc(done_s, 1)
            nc.vector.tensor_scalar(k.ident[:, :], k.iota[:, :], part_f[:, 0:1], None, ALU.is_equal).then_inc(done_s, 1)
            nc.vector.tensor_scalar(k.block_start[:, :], part_f[:, :], float(P), None, ALU.mult).then_inc(done_s, 1)
            nc.vector.tensor_copy(k.part[:, :], part_f[:, :]).then_inc(done_s, 1)

        @block.sync
        def _(sp):
            n = 0
            for dst, src in k.loads:
                sp.dma_start(dst, src).then_inc(k.loaded, 16)
                n += 16
            sp.wait_ge(k.loaded, n)


def unit_tables(nc, st, k, a):
    last_i = st.sb("u_last_i", [BLOCKS, GROUPS], I32)
    below = st.sb("u_below", [BLOCKS, GROUPS])
    first = st.sb("u_first", [BLOCKS, 2])
    begun = st.sb("u_begun", [BLOCKS, UNITS])
    blk = st.sb("u_blk", [P, UNITS + 1])
    grp = st.sb("u_grp", [1, UNITS])
    pb = [st.ps(f"u_psum{i}", [P, UNITS // 2]) for i in range(2)]
    last_in = st.dma_sem("u_last_in")
    step = st.sem("u_step")
    counted = st.sem("u_counted")
    begun_s = st.sem("u_begun_s")
    half = UNITS // 2
    with nc.Block() as block:

        @block.sync
        def _(sp):
            sp.dma_start(last_i[:, :], a["last_dst"].to_broadcast([BLOCKS, GROUPS])).then_inc(last_in, 16)

        @block.vector
        def _(dve):
            dve.wait_ge(last_in, 16)
            nc.vector.tensor_scalar(below[:, :], last_i[:, :], k.block_start[0:BLOCKS, 0:1], None, ALU.is_lt).then_inc(step, 1)
            dve.wait_ge(step, 1)
            nc.vector.tensor_reduce(out=first[:, 0:1], in_=below[:, :], op=ALU.add, axis=AX.X).then_inc(step, 1)
            dve.wait_ge(step, 2)
            nc.vector.tensor_tensor(first[:, 1:2], first[:, 0:1], k.part[0:BLOCKS, :], ALU.add).then_inc(step, 1)
            dve.wait_ge(step, 3)
            nc.vector.tensor_scalar(begun[:, :], k.unit_row[0:BLOCKS, :], first[:, 1:2], None, ALU.is_ge).then_inc(begun_s, 1)
            nc.vector.memset(blk[:, 0:1], -1.0).then_inc(step, 1)
            for i in range(2):
                dve.wait_ge(counted, i + 1)
                nc.vector.tensor_scalar(blk[:, 1 + i * half:1 + (i + 1) * half], pb[i][:, :], -1.0, None, ALU.add).then_inc(step, 1)
            dve.wait_ge(step, 6)
            nc.vector.tensor_scalar(k.ucol[:, :, 0], blk[:, 1:], float(P), None, ALU.mult).then_inc(step, 1)
            nc.vector.tensor_tensor(k.ucol[:, :, 1], blk[:, 1:], blk[:, 0:UNITS], ALU.is_equal).then_inc(step, 1)
            nc.vector.tensor_tensor(grp[:, :], k.unit_row[0:1, :], blk[0:1, 1:], ALU.subtract).then_inc(step, 1)
            nc.vector.tensor_copy(k.ureg[:, :, 1], blk[0:1, 1:]).then_inc(step, 1)
            nc.vector.memset(k.ureg[:, :, 2:], 0).then_inc(step, 1)
            dve.wait_ge(step, 11)
            nc.vector.tensor_copy(k.ureg[:, RING:, 2], blk[0:1, 1:UNITS + 1 - RING]).then_inc(step, 1)
            nc.vector.tensor_scalar(k.ucol[:, :, 2], k.ucol[:, :, 1], -1.0, 2.0 * FAR, ALU.add, ALU.mult).then_inc(step, 1)
            nc.vector.tensor_copy(k.ureg[:, :, 0], grp[:, :]).then_inc(step, 1)

        @block.tensor
        def _(pe):
            pe.wait_ge(begun_s, 1)
            for i in range(2):
                nc.tensor.matmul(pb[i][:, :], k.ones[0:BLOCKS, :], begun[:, i * half:(i + 1) * half],
                                 start=True, stop=True).then_inc(counted, 1)


def run_flags(nc, st, a, far_rows):
    here = st.sb("f_here", [P, FLAG_TILES * P], I32)
    prev = st.sb("f_prev", [P, FLAG_TILES * P], I32)
    flag = st.sb("f_flag", [P, FLAG_TILES * P])
    neg = st.sb("f_neg", [P, FLAG_TILES * P])
    come = st.dma_sem("f_in")
    made = st.sem("f_made")
    out = st.dma_sem("f_out")
    rows = far_rows.rearrange("(p k) h e -> p k h e", p=P)
    with nc.Block() as block:

        @block.sync
        def _(sp):
            sp.dma_start(here[:, :], a["dst_rows"]).then_inc(come, 16)
            sp.dma_start(prev[:, :], a["dst_prev_rows"]).then_inc(come, 16)
            sp.wait_ge(made, 2)
            for h in range(H):
                sp.dma_start(rows[:, :, h, :], neg[:, :].rearrange("p (k e) -> p k e", e=P)).then_inc(out, 16)
            sp.wait_ge(out, 16 * H)

        @block.vector
        def _(dve):
            dve.wait_ge(come, 32)
            nc.vector.tensor_tensor(flag[:, :], here[:, :], prev[:, :], ALU.not_equal).then_inc(made, 1)
            dve.wait_ge(made, 1)
            nc.vector.tensor_scalar(neg[:, :], flag[:, :], -3.0e38, None, ALU.mult).then_inc(made, 1)


class Split:

    def __init__(self, nc, st, name, shape):
        self.nc = nc
        self.left = [st.sb(f"{name}_left{i}", shape) for i in range(2)]
        self.part_done = [st.sem(f"{name}_part{i}") for i in range(2)]
        self.left_done = [st.sem(f"{name}_leftd{i}") for i in range(2)]

    def on_vector(self, dve, j, value, part, done):
        nc = self.nc
        for i in range(PARTS):
            last = nc.vector.tensor_copy(part(i), value)
            if i == PARTS - 1:
                last.then_inc(done, 1)
                return
            last.then_inc(self.part_done[i], 1)
            dve.wait_ge(self.part_done[i], j + 1)
            left = self.left[i]
            nc.vector.tensor_tensor(left[tuple(slice(None) for _ in left.shape)], value, part(i), ALU.subtract).then_inc(self.left_done[i], 1)
            dve.wait_ge(self.left_done[i], j + 1)
            value = left[tuple(slice(None) for _ in left.shape)]


def project0(nc, st, k, a, table0, tgt0):
    wcat = st.sb("p_wcat", [P, D + 2 * H])
    xt = st.sb("p_xt", [P, NBLK, 3 * P])
    res = st.sb("p_res", [P, NBLK, 3, ROW0])
    parts = st.sb("p_parts", [P, NBLK, 3, PARTS, H], BF16)
    split = Split(nc, st, "p_split", [P, 3, H])
    pw = st.ps("p_pw", [P, 2 * H])
    pp = [st.ps(f"p_pp{i}", [P, 3, D + 2 * H]) for i in range(NBLK)]
    w_ready, w_mm = st.sem("p_w_ready"), st.sem("p_w_mm")
    x_in = st.ring_sems("p_x_in", NBLK)
    mm_done, res_done, copied = st.sem("p_mm_done"), st.sem("p_res_done"), st.sem("p_copied")
    stored = st.ring_sems("p_stored", NBLK)
    steps = BLOCKS // 3
    t0 = table0.rearrange("(s b p) c -> s p b c", b=3, p=P)
    t1 = tgt0.rearrange("(s b p) c -> s p b c", b=3, p=P)
    xs = a["xT"].rearrange("p (s c) -> s p c", s=steps)
    with nc.Block() as block:

        @block.sync
        def _(sp):
            def step(j, p):
                if has(j, -NBLK, steps):
                    sp.wait_ge(mm_done, j - NBLK + 1)
                sp.dma_start(xt[:, p, :], xs[bass.ds(j, 1), :, :].rearrange("o p c -> (o p) c")).then_inc(x_in[p], 16)

            over_ring(sp, steps, NBLK, step)

        @block.tensor
        def _(pe):
            nc.tensor.matmul(pw[:, :], k.w0t[:, :], k.att0[:, :], start=True, stop=True).then_inc(w_mm, 1)
            pe.wait_ge(w_ready, 2)

            def step(j, p):
                if has(j, -NBLK, steps):
                    pe.wait_ge(res_done, j - NBLK + 1)
                pe.wait_ge(x_in[p], laps(j, p, NBLK, 16))
                for b in range(3):
                    last = nc.tensor.matmul(pp[p][:, b, :], xt[:, p, b * P:(b + 1) * P], wcat[:, :], start=True, stop=True)
                last.then_inc(mm_done, 1)

            over_ring(pe, steps, NBLK, step)

        @block.vector
        def _(dve):
            nc.vector.tensor_copy(wcat[:, 0:D], k.w0[:, :]).then_inc(w_ready, 1)
            dve.wait_ge(w_mm, 1)
            nc.vector.tensor_copy(wcat[:, D:], pw[:, :]).then_inc(w_ready, 1)

            def step(j, p):
                if has(j, -NBLK, steps):
                    dve.wait_ge(stored[p], laps(j - NBLK, p, NBLK, 32))
                dve.wait_ge(mm_done, j + 1)
                nc.vector.tensor_copy(res[:, p, :, :], pp[p][:, :, 0:ROW0]).then_inc(copied, 1)
                split.on_vector(dve, j, pp[p][:, :, ROW0:], lambda i: parts[:, p, :, i, :], res_done)

            over_ring(dve, steps, NBLK, step)

        @block.scalar
        def _(act):
            def step(j, p):
                act.wait_ge(res_done, j + 1)
                act.wait_ge(copied, j + 1)
                act.dma_start(t0[bass.ds(j, 1), :, :, :].rearrange("o p b c -> (o p) b c"), res[:, p, :, :]).then_inc(stored[p], 16)
                act.dma_start(t1[bass.ds(j, 1), :, :, :].rearrange("o p b c -> (o p) b c"), parts[:, p, :, :, :].rearrange("p b i h -> p b (i h)")).then_inc(stored[p], 16)

            over_ring(act, steps, NBLK, step)
            for p in range(NBLK):
                act.wait_ge(stored[p], laps(steps - NBLK + p, p, NBLK, 32))


def rows_of(table, b):
    return table.rearrange("(b p) c -> b p c", p=P)[bass.ds(b, 1), :, :].rearrange("o p c -> (o p) c")


def layer_buffers(nc, st, u, name, sum_banks):
    u.cols = st.sb(name + "_cols", [P, RING, 3 * TILES], I32)
    u.unit = st.sb(name + "_unit", [P, RING, 3])
    u.rel = st.sb(name + "_rel", [P, RING, TILES])
    u.hot = st.sb(name + "_hot", [P, RING, TILES, P], BF16)
    u.hot_f = st.sb(name + "_hot_f", [P, RING, TILES, P])
    u.hot_t = st.sb(name + "_hot_t", [P, RING, TILES, P], BF16)
    u.wgt = st.sb(name + "_wgt", [P, RING, TILES, H, HC])
    u.acc = st.sb(name + "_acc", [P, RING, H, HC])
    u.p_hot = st.ps(name + "_p_hot", [P, TILES, P], BF16)
    u.p_sum = [st.ps(f"{name}_p_sum{i}", [P, H, HC]) for i in range(sum_banks)]
    u.cols_in = st.ring_sems(name + "_cols_in", RING)
    u.gathered = st.ring_sems(name + "_gathered", RING)
    u.stored = st.ring_sems(name + "_stored", RING)
    u.ucol_in, u.rel_done, u.hot_done = st.sem(name + "_ucol_in"), st.sem(name + "_rel_done"), st.sem(name + "_hot_done")
    u.hot_mm, u.hot_t_done, u.hot_f_done = st.sem(name + "_hot_mm"), st.sem(name + "_hot_t_done"), st.sem(name + "_hot_f_done")
    u.exp_done, u.wgt_done, u.sum_mm = st.sem(name + "_exp_done"), st.sem(name + "_wgt_done"), st.sem(name + "_sum_mm")
    u.acc_done, u.pool_passed, u.sp_passed = st.sem(name + "_acc_done"), st.sem(name + "_pool_passed"), st.sem(name + "_sp_passed")


def unit_registers(nc, sp, k, regs, j):
    sp.load(regs, k.ureg[0:1, bass.ds(j, 1), :].rearrange("a o c -> a (o c)"))
    return (sp.snap(regs[0], min_val=0, max_val=GROUPS - 1), sp.snap(regs[1], min_val=0, max_val=BLOCKS - 1),
            sp.snap(regs[2], min_val=0, max_val=BLOCKS - 1))


def store_sums(nc, sp, u, j, p, blk, agg):
    sp.wait_ge(u.acc_done, j + 1)
    gate(sp, u.sp_passed)
    if has(j, -1, UNITS):
        q = (p - 1) % RING
        sp.wait_ge(u.stored[q], laps(j - 1, q, RING, 16))
        gate(sp, u.sp_passed)
    sp.dma_start(rows_of(agg, blk), u.acc[:, p, :, :].rearrange("p h c -> p (h c)")).then_inc(u.stored[p], 16)


def store_last_sums(nc, sp, k, u, agg):
    for j in range(UNITS - RING, UNITS):
        blk = sp.value_load(k.ureg[0:1, j, 1:2], min_val=0, max_val=BLOCKS - 1)
        store_sums(nc, sp, u, j, j % RING, blk, agg)
    for p in range(RING):
        sp.wait_ge(u.stored[p], laps(UNITS - RING + p, p, RING, 16))


def load_indices(nc, sp, a, u, j, p, grp, cols_read):
    if has(j, -RING, UNITS):
        sp.wait_ge(u.gathered[p], laps(j - RING, p, RING, 16 * TILES))
        gate(sp, u.sp_passed)
        sp.wait_ge(cols_read, j - RING + 1)
        gate(sp, u.sp_passed)
    sp.dma_start(u.cols[:, p, :], a["edge_cols"][bass.ds(grp, 1), :, :].rearrange("o p c -> (o p) c")).then_inc(u.cols_in[p], 16)


def gather_rows(nc, pool, u, j, p, table, dest):
    pool.wait_ge(u.cols_in[p], laps(j, p, RING, 16))
    gate(pool, u.pool_passed)
    add = {} if dest.add is None else {"compute_op": dest.add}
    for t in range(TILES):
        nc.gpsimd.indirect_dma_start(
            out=dest.at(p, t), out_offset=None, in_=table,
            in_offset=bass.IndirectOffsetOnAxis(ap=u.cols[:, p, t:t + 1], axis=0), **add).then_inc(u.gathered[p], 16)


def unit_scalars(nc, act, k, u, j, p, last_use):
    if has(j, -RING, UNITS):
        act.wait_ge(last_use, j - RING + 1)
    nc.scalar.copy(u.unit[:, p, :], k.ucol[:, bass.ds(j, 1), :].rearrange("p o c -> p (o c)")).then_inc(u.ucol_in, 1)


def place_edges(nc, dve, u, j, p):
    dve.wait_ge(u.cols_in[p], laps(j, p, RING, 16))
    dve.wait_ge(u.ucol_in, j + 1)
    nc.vector.tensor_scalar(u.rel[:, p, :], u.cols[:, p, TILES:2 * TILES], u.unit[:, p, 0:1], None, ALU.subtract).then_inc(u.rel_done, 1)


def make_hot(nc, dve, k, u, j, p):
    dve.wait_ge(u.rel_done, j + 1)
    if has(j, -RING, UNITS):
        dve.wait_ge(u.hot_f_done, j - RING + 1)
        dve.wait_ge(u.sum_mm, j - RING + 1)
    for t in range(TILES):
        last = nc.vector.tensor_scalar(u.hot[:, p, t, :], k.iota_b[:, :], u.rel[:, p, t:t + 1], None, ALU.is_equal)
    last.then_inc(u.hot_done, 1)


def copy_hot(nc, act, u, j, p):
    act.wait_ge(u.hot_done, j + 1)
    if has(j, -RING, UNITS):
        act.wait_ge(u.sum_mm, j - RING + 1)
    nc.scalar.copy(u.hot_f[:, p, :, :], u.hot[:, p, :, :]).then_inc(u.hot_f_done, 1)


def transpose_hot(nc, pe, k, u, j, p):
    pe.wait_ge(u.hot_done, j + 1)
    if has(j, -1, UNITS):
        pe.wait_ge(u.hot_t_done, j)
    for t in range(TILES):
        last = nc.tensor.transpose(u.p_hot[:, t, :], u.hot[:, p, t, :], k.ident_b[:, :])
    last.then_inc(u.hot_mm, 1)


def copy_hot_t(nc, act, u, j, p, last_use):
    act.wait_ge(u.hot_mm, j + 1)
    if has(j, -RING, UNITS):
        act.wait_ge(last_use, j - RING + 1)
    nc.scalar.copy(u.hot_t[:, p, :, :], u.p_hot[:, :, :]).then_inc(u.hot_t_done, 1)


def sum_edges(nc, pe, u, j, p):
    pe.wait_ge(u.wgt_done, j + 1)
    pe.wait_ge(u.hot_f_done, j + 1)
    banks = len(u.p_sum)
    if has(j, -banks, UNITS):
        pe.wait_ge(u.acc_done, j + 1 - banks)
    for t in range(TILES):
        last = nc.tensor.matmul(u.p_sum[p % banks][:, :, :].rearrange("p h c -> p (h c)"), u.hot_f[:, p, t, :],
                                u.wgt[:, p, t, :, :].rearrange("p h c -> p (h c)"), start=(t == 0), stop=(t == TILES - 1))
    last.then_inc(u.sum_mm, 1)


class Dest:

    def __init__(self, at, add=None):
        self.at, self.add = at, add


def gat_layer(nc, st, k, a, table0, tgt0, agg0):
    u = Names()
    layer_buffers(nc, st, u, "g", 2)
    rows = st.sb("g_rows", [P, RING, TILES, ROW0])
    tblk = st.sb("g_tblk", [P, RING, PARTS, H], BF16)
    score = st.sb("g_score", [P, RING, TILES * H])
    leak = st.sb("g_leak", [P, RING, TILES, H])
    p_tgt = [st.ps(f"g_p_tgt{i}", [P, TILES, H]) for i in range(2)]
    tblk_in = st.ring_sems("g_tblk_in", RING)
    tgt_mm, score_done, leak_done, zeroed = st.sem("g_tgt_mm"), st.sem("g_score_done"), st.sem("g_leak_done"), st.sem("g_zeroed")
    regs = [nc.sync.alloc_register(f"g_reg{i}") for i in range(3)]
    dest = Dest(lambda s, t: rows[:, s, t, :])

    with nc.Block() as block:

        @block.sync
        def _(sp):
            def step(j, p):
                grp, blk, old = unit_registers(nc, sp, k, regs, j)
                load_indices(nc, sp, a, u, j, p, grp, u.rel_done)
                if has(j, -RING, UNITS):
                    sp.wait_ge(tgt_mm, j - RING + 1)
                    gate(sp, u.sp_passed)
                sp.dma_start(tblk[:, p, :, :].rearrange("p i h -> p (i h)"), rows_of(tgt0, blk)).then_inc(tblk_in[p], 16)
                if has(j, -RING, UNITS):
                    store_sums(nc, sp, u, j - RING, p, old, agg0)

            over_ring(sp, UNITS, RING, step)
            store_last_sums(nc, sp, k, u, agg0)

        @block.gpsimd
        def _(pool):
            def step(j, p):
                if has(j, -RING, UNITS):
                    pool.wait_ge(u.wgt_done, j - RING + 1)
                    gate(pool, u.pool_passed)
                gather_rows(nc, pool, u, j, p, table0, dest)

            over_ring(pool, UNITS, RING, step)

        @block.vector
        def _(dve):
            nc.vector.memset(u.acc[:, RING - 1, :, :], 0.0).then_inc(zeroed, 1)
            dve.wait_ge(zeroed, 1)

            def step(s, p):
                if has(s, 3, UNITS):
                    place_edges(nc, dve, u, s + 3, (p + 3) % RING)
                if has(s, 1, UNITS):
                    j, q = s + 1, (p + 1) % RING
                    dve.wait_ge(u.gathered[q], laps(j, q, RING, 16 * TILES))
                    dve.wait_ge(tgt_mm, j + 1)
                    nc.vector.tensor_tensor(score[:, q, :].rearrange("p (t h) -> p t h", h=H), rows[:, q, :, D:], p_tgt[q % 2][:, :, :], ALU.add).then_inc(score_done, 1)
                if has(s, -1, UNITS):
                    j, q = s - 1, (p - 1) % RING
                    dve.wait_ge(u.sum_mm, j + 1)
                    if has(j, -RING, UNITS):
                        dve.wait_ge(u.stored[q], laps(j - RING, q, RING, 16))
                    if has(j, -1, UNITS):
                        dve.wait_ge(u.acc_done, j)
                    nc.vector.scalar_tensor_tensor(
                        out=u.acc[:, q, :, :].rearrange("p h c -> p (h c)"), in0=u.acc[:, (q - 1) % RING, :, :].rearrange("p h c -> p (h c)"),
                        scalar=u.unit[:, q, 1:2], in1=u.p_sum[q % 2][:, :, :].rearrange("p h c -> p (h c)"),
                        op0=ALU.mult, op1=ALU.add).then_inc(u.acc_done, 1)
                if has(s, 3, UNITS):
                    make_hot(nc, dve, k, u, s + 3, (p + 3) % RING)
                if has(s, 1, UNITS):
                    j, q = s + 1, (p + 1) % RING
                    dve.wait_ge(score_done, j + 1)
                    nc.vector.scalar_tensor_tensor(
                        out=leak[:, q, :, :].rearrange("p t h -> p (t h)"), in0=score[:, q, :], scalar=0.2,
                        in1=score[:, q, :], op0=ALU.mult, op1=ALU.max).then_inc(leak_done, 1)
                if has(s, 0, UNITS):
                    dve.wait_ge(u.exp_done, s + 1)
                    nc.vector.tensor_tensor(
                        u.wgt[:, p, :, :, 0:C], rows[:, p, :, 0:D].rearrange("p t (h c) -> p t h c", h=H),
                        u.wgt[:, p, :, :, C:HC].to_broadcast([P, TILES, H, C]), ALU.mult).then_inc(u.wgt_done, 1)

            staggered(dve, 3, 1, step)

        @block.scalar
        def _(act):
            def step(s, p):
                if has(s, 4, UNITS):
                    unit_scalars(nc, act, k, u, s + 4, (p + 4) % RING, u.acc_done)
                if has(s, 3, UNITS):
                    copy_hot(nc, act, u, s + 3, (p + 3) % RING)
                    copy_hot_t(nc, act, u, s + 3, (p + 3) % RING, tgt_mm)
                if has(s, 1, UNITS):
                    j, q = s + 1, (p + 1) % RING
                    act.wait_ge(leak_done, j + 1)
                    if has(j, -RING, UNITS):
                        act.wait_ge(u.sum_mm, j - RING + 1)
                    nc.scalar.activation(u.wgt[:, q, :, :, C], leak[:, q, :, :], ACT.Exp).then_inc(u.exp_done, 1)

            staggered(act, 4, 0, step)

        @block.tensor
        def _(pe):
            def step(s, p):
                if has(s, 2, UNITS):
                    j, q = s + 2, (p + 2) % RING
                    pe.wait_ge(u.hot_t_done, j + 1)
                    pe.wait_ge(tblk_in[q], laps(j, q, RING, 16))
                    if has(j, -2, UNITS):
                        pe.wait_ge(score_done, j - 1)
                    for t in range(TILES):
                        for i in range(PARTS):
                            last = nc.tensor.matmul(p_tgt[q % 2][:, t, :], u.hot_t[:, q, t, :], tblk[:, q, i, :],
                                                    start=(i == 0), stop=(i == PARTS - 1))
                    last.then_inc(tgt_mm, 1)
                if has(s, 3, UNITS):
                    transpose_hot(nc, pe, k, u, s + 3, (p + 3) % RING)
                if has(s, 0, UNITS):
                    sum_edges(nc, pe, u, s, p)

            staggered(pe, 3, 0, step)


def step_rows(table, j):
    return table.rearrange("(s b p) c -> s p b c", b=NBLK, p=P)[bass.ds(j, 1), :, :, :].rearrange("o p b c -> (o p) b c")


class LayerNorm:

    def __init__(self, nc, st, name):
        self.nc = nc
        self.stats = st.sb(name + "_stats", [P, NBLK, 6])
        self.mv = st.sb(name + "_mv", [P, NBLK, 2])
        self.std = st.sb(name + "_std", [P, NBLK])
        self.rstd = st.sb(name + "_rstd", [P, NBLK])
        self.stats_done, self.mv_done = st.sem(name + "_stats_done"), st.sem(name + "_mv_done")
        self.passed = st.sem(name + "_passed")
        self.std_done, self.rstd_done = st.sem(name + "_std_done"), st.sem(name + "_rstd_done")

    def on_vector(self, dve, j, y, out, done):
        nc = self.nc
        for b in range(NBLK):
            last = nc.vector.bn_stats(self.stats[:, b, :], y[:, b, :])
        last.then_inc(self.stats_done, 1)
        dve.wait_ge(self.stats_done, j + 1)
        gate(dve, self.passed)
        for b in range(NBLK):
            last = nc.vector.bn_aggr(self.mv[:, b, :], self.stats[:, b, :])
        last.then_inc(self.mv_done, 1)
        dve.wait_ge(self.std_done, j + 1)
        nc.vector.reciprocal(self.rstd[:, :], self.std[:, :]).then_inc(self.rstd_done, 1)
        dve.wait_ge(self.rstd_done, j + 1)
        for b in range(NBLK):
            last = nc.vector.tensor_scalar(out[:, b, :], y[:, b, :], self.mv[:, b, 0:1], self.rstd[:, b:b + 1],
                                           ALU.subtract, ALU.mult)
        last.then_inc(done, 1)

    def on_scalar(self, act, k, j):
        act.wait_ge(self.mv_done, j + 1)
        self.nc.scalar.activation(self.std[:, :], self.mv[:, :, 1], ACT.Sqrt, bias=k.eps[:, 0:1]).then_inc(self.std_done, 1)


def middle(nc, st, k, a, agg0, kv_table, q_table, node1):
    agg = st.sb("m_agg", [P, NBLK, NBLK, H, HC])
    xin = st.sb("m_xin", [P, NBLK, NBLK, D])
    den = st.sb("m_den", [P, NBLK, H])
    rec = st.sb("m_rec", [P, NBLK, H])
    att = st.sb("m_att", [P, NBLK, D])
    attb = st.sb("m_attb", [P, NBLK, D])
    y = st.sb("m_y", [P, NBLK, D])
    x1t = st.sb("m_x1t", [P, NBLK, P])
    node = st.sb("m_node", [P, NBLK, NBLK, NODE1])
    kv = st.sb("m_kv", [P, NBLK, NBLK, 2 * D])
    p_t = st.ps("m_p_t", [P, NBLK, P])
    p_w = [st.ps(f"m_p_w{b}", [P, 4 * D]) for b in range(NBLK)]
    qparts = st.sb("m_qparts", [P, NBLK, NBLK, PARTS, D], BF16)
    q = st.sb("m_q", [P, NBLK, D])
    split = Split(nc, st, "m_split", [P, NBLK, D])
    q_done = st.sem("m_q_done")
    ln = LayerNorm(nc, st, "m_ln")
    loaded = st.ring_sems("m_loaded", NBLK)
    stored = st.ring_sems("m_stored", NBLK)
    scaled, den_done, rec_done = st.sem("m_scaled"), st.sem("m_den_done"), st.sem("m_rec_done")
    att_done, attb_done, y_done = st.sem("m_att_done"), st.sem("m_attb_done"), st.sem("m_y_done")
    x1_done, t_mm, x1t_done = st.sem("m_x1_done"), st.sem("m_t_mm"), st.sem("m_x1t_done")
    w_mm, split_done, node_done = st.sem("m_w_mm"), st.sem("m_split_done"), st.sem("m_node_done")
    steps = BLOCKS // NBLK
    with nc.Block() as block:

        @block.sync
        def _(sp):
            def step(j, p):
                if has(j, -NBLK, steps):
                    sp.wait_ge(y_done, j - NBLK + 1)
                sp.dma_start(agg[:, p, :, :, :].rearrange("p b h c -> p b (h c)"), step_rows(agg0, j)).then_inc(loaded[p], 16)
                sp.dma_start(xin[:, p, :, :], step_rows(a["x_rows"], j)).then_inc(loaded[p], 16)

            over_ring(sp, steps, NBLK, step)

        @block.vector
        def _(dve):
            nc.vector.tensor_scalar(k.wcat1[:, 0:D], k.wcat1[:, 0:D], float(C) ** -0.5, None, ALU.mult).then_inc(scaled, 1)
            nc.vector.tensor_scalar(k.bcat1[:, 0:D], k.bcat1[:, 0:D], float(C) ** -0.5, None, ALU.mult).then_inc(scaled, 1)
            dve.wait_ge(scaled, 2)

            def step(j, p):
                dve.wait_ge(loaded[p], laps(j, p, NBLK, 32))
                if has(j, -NBLK, steps):
                    dve.wait_ge(stored[p], laps(j - NBLK, p, NBLK, 48))
                nc.vector.tensor_scalar(den[:, :, :], agg[:, p, :, :, C], 1e-16, None, ALU.add).then_inc(den_done, 1)
                dve.wait_ge(den_done, j + 1)
                nc.vector.reciprocal(rec[:, :, :], den[:, :, :]).then_inc(rec_done, 1)
                dve.wait_ge(rec_done, j + 1)
                nc.vector.tensor_tensor(att[:, :, :].rearrange("p b (h c) -> p b h c", h=H), agg[:, p, :, :, 0:C],
                                        rec[:, :, :].unsqueeze(3).to_broadcast([P, NBLK, H, C]), ALU.mult).then_inc(att_done, 1)
                dve.wait_ge(att_done, j + 1)
                nc.vector.tensor_tensor(attb[:, :, :], att[:, :, :], k.bias0[:, :].unsqueeze(1).to_broadcast([P, NBLK, D]), ALU.add).then_inc(attb_done, 1)
                dve.wait_ge(attb_done, j + 1)
                nc.vector.tensor_tensor(y[:, :, :], attb[:, :, :], xin[:, p, :, :], ALU.add).then_inc(y_done, 1)
                dve.wait_ge(y_done, j + 1)
                ln.on_vector(dve, j, y[:, :, :], node[:, p, :, D:], x1_done)
                for b in range(NBLK):
                    if b == 0:
                        dve.wait_ge(w_mm, j + 1)
                    w = p_w[b]
                    nc.vector.tensor_tensor(kv[:, p, b, :], w[:, D:3 * D], k.bcat1[:, D:3 * D], ALU.add).then_inc(split_done, 1)
                    nc.vector.tensor_tensor(q[:, b, :], w[:, 0:D], k.bcat1[:, 0:D], ALU.add).then_inc(split_done, 1)
                    nc.vector.tensor_tensor(node[:, p, b, 0:D], w[:, 3 * D:], k.bcat1[:, 3 * D:], ALU.add).then_inc(split_done, 1)
                dve.wait_ge(split_done, 9 * j + 9)
                nc.vector.tensor_tensor(node[:, p, :, 0:D], node[:, p, :, 0:D], node[:, p, :, D:], ALU.add).then_inc(node_done, 1)
                split.on_vector(dve, j, q[:, :, :], lambda i: qparts[:, p, :, i, :], q_done)

            over_ring(dve, steps, NBLK, step)

        @block.tensor
        def _(pe):
            pe.wait_ge(scaled, 2)

            def step(j, p):
                pe.wait_ge(x1_done, j + 1)
                if has(j, -1, steps):
                    pe.wait_ge(x1t_done, j)
                for b in range(NBLK):
                    last = nc.tensor.transpose(p_t[:, b, :], node[:, p, b, D:], k.ident[:, :])
                last.then_inc(t_mm, 1)
                pe.wait_ge(x1t_done, j + 1)
                if has(j, -1, steps):
                    pe.wait_ge(node_done, j)
                for b in range(NBLK):
                    last = nc.tensor.matmul(p_w[b][:, :], x1t[:, b, :], k.wcat1[:, :], start=True, stop=True)
                last.then_inc(w_mm, 1)

            over_ring(pe, steps, NBLK, step)

        @block.scalar
        def _(act):
            def step(j, p):
                ln.on_scalar(act, k, j)
                act.wait_ge(t_mm, j + 1)
                if has(j, -1, steps):
                    act.wait_ge(w_mm, j)
                nc.scalar.copy(x1t[:, :, :], p_t[:, :, :]).then_inc(x1t_done, 1)

            over_ring(act, steps, NBLK, step)

        @block.gpsimd
        def _(pool):
            def step(j, p):
                pool.wait_ge(node_done, j + 1)
                pool.dma_start(step_rows(kv_table, j), kv[:, p, :, :]).then_inc(stored[p], 16)
                pool.dma_start(step_rows(node1, j), node[:, p, :, :]).then_inc(stored[p], 16)
                pool.wait_ge(q_done, j + 1)
                pool.dma_start(step_rows(q_table, j), qparts[:, p, :, :, :].rearrange("p b i c -> p b (i c)")).then_inc(stored[p], 16)

            over_ring(pool, steps, NBLK, step)
            for p in range(NBLK):
                pool.wait_ge(stored[p], laps(steps - NBLK + p, p, NBLK, 48))


def edge_layer(nc, st, k, a, kv_table, q_table, neg_rows, agg1):
    u = Names()
    layer_buffers(nc, st, u, "e", 1)
    kv = st.sb("e_kv", [P, RING, TILES, 2, D])
    attr = st.sb("e_attr", [2 * ED, RING, TILES // 2, P])
    neg = st.sb("e_neg", [TILES * H, RING, P])
    qblk = st.sb("e_qblk", [P, RING, PARTS, D], BF16)
    prod = st.sb("e_prod", [P, TILES * H, C])
    logit = st.sb("e_logit", [P, RING, TILES, H])
    runmax = st.sb("e_runmax", [TILES * H, 2, P])
    lastmax = st.sb("e_lastmax", [P, 2, TILES, H])
    high = st.sb("e_high", [P, RING, TILES, H + 1], BF16)
    low = st.sb("e_low", [P, 2, TILES, H], BF16)
    absent = st.sb("e_absent", [P, 2, TILES])
    cand = st.sb("e_cand", [P, 2, TILES, H])
    newmax = st.sb("e_newmax", [P, 2, H])
    before = st.sb("e_before", [P, 2, H])
    top = st.sb("e_top", [P, 2, H])
    top_high = st.sb("e_top_high", [P, 2, H], BF16)
    top_low = st.sb("e_top_low", [P, 2, H], BF16)
    drop = st.sb("e_drop", [P, 2, H])
    scale = st.sb("e_scale", [P, 2, H])
    shifted = st.sb("e_shifted", [P, 2, TILES, H])
    scaled = st.sb("e_scaled", [P, H, HC])
    p_e = st.ps("e_p_e", [P, TILES, D])
    p_qs = [st.ps(f"e_p_q{i}", [P, TILES, D]) for i in range(2)]
    p_lt = st.ps("e_p_lt", [TILES * H, P])
    p_edge = st.ps("e_p_edge", [P, 2, TILES * H])
    p_node = st.ps("e_p_node", [P, TILES, H + 1])
    p_run = p_edge[:, 0, :].rearrange("p (t h) -> p t h", h=H)
    p_top = p_edge[:, 1, :].rearrange("p (t h) -> p t h", h=H)
    e_in = st.ring_sems("e_e_in", RING)
    blk_in = st.ring_sems("e_blk_in", RING)
    e_mm, e_done, q_mm, prod_done, logit_done = (st.sem("e_" + n) for n in ("e_mm", "e_done", "q_mm", "prod_done", "logit_done"))
    lt_mm, run_done, run_mm, last_done, lastmax_done = (st.sem("e_" + n) for n in ("lt_mm", "run_done", "run_mm", "last_done", "lastmax_done"))
    high_done, low_done, node_mm, absent_done, cand_done = (st.sem("e_" + n) for n in ("high_done", "low_done", "node_mm", "absent_done", "cand_done"))
    newmax_done, before_done, top_done, top_high_done, top_low_done = (st.sem("e_" + n) for n in ("newmax_done", "before_done", "top_done", "top_high_done", "top_low_done"))
    drop_done, scale_done, top_mm, shifted_done, scaled_done = (st.sem("e_" + n) for n in ("drop_done", "scale_done", "top_mm", "shifted_done", "scaled_done"))
    zeroed, pe_passed = st.sem("e_zeroed"), st.sem("e_pe_passed")
    regs = [nc.sync.alloc_register(f"e_reg{i}") for i in range(3)]
    dest = Dest(lambda s, t: kv[:, s, t, :, :].rearrange("p a c -> p (a c)"), ALU.add)
    EDGE_LEAD = 5
    HOT_LEAD = 4

    with nc.Block() as block:

        @block.sync
        def _(sp):
            def step(j, p):
                grp, blk, old = unit_registers(nc, sp, k, regs, j)
                load_indices(nc, sp, a, u, j, p, grp, last_done)
                if has(j, -RING, UNITS):
                    sp.wait_ge(e_mm, j - RING + 1)
                    gate(sp, u.sp_passed)
                sp.dma_start(attr[:, p, :, :].rearrange("p b e -> p (b e)"), a["attr_t"][bass.ds(grp, 1), :, :].rearrange("o p c -> (o p) c")).then_inc(e_in[p], 16)
                if has(j, -RING, UNITS):
                    sp.wait_ge(run_done, j - RING + 1)
                    gate(sp, u.sp_passed)
                sp.dma_start(qblk[:, p, :, :].rearrange("p i c -> p (i c)"), rows_of(q_table, blk)).then_inc(blk_in[p], 16)
                sp.dma_start(neg[:, p, :], neg_rows.rearrange("(g t) h e -> g (t h) e", t=TILES)[bass.ds(grp, 1), :, :]
                             .rearrange("o p c -> (o p) c")).then_inc(blk_in[p], 16)
                if has(j, -RING, UNITS):
                    store_sums(nc, sp, u, j - RING, p, old, agg1)

            over_ring(sp, UNITS, RING, step)
            store_last_sums(nc, sp, k, u, agg1)

        @block.gpsimd
        def _(pool):
            def step(j, p):
                pool.wait_ge(e_done, j + 1)
                gate(pool, u.pool_passed)
                gather_rows(nc, pool, u, j, p, kv_table, dest)

            over_ring(pool, UNITS, RING, step)

        @block.vector
        def _(dve):
            nc.vector.memset(u.acc[:, RING - 1, :, :], 0.0).then_inc(zeroed, 1)
            nc.vector.memset(top[:, 1, :], -FAR).then_inc(zeroed, 1)
            dve.wait_ge(zeroed, 2)

            def step(s, p):
                b = p % 2
                c, n, n2, n4 = 1 - b, (p + 1) % RING, (p + 2) % RING, (p + HOT_LEAD) % RING
                if has(s, 1, UNITS):
                    dve.wait_ge(lt_mm, s + 2)
                    dve.wait_ge(blk_in[n], laps(s + 1, n, RING, 32))
                    if has(s, -1, UNITS):
                        dve.wait_ge(run_mm, s)
                    nc.vector.tensor_tensor_scan(runmax[:, c, :], neg[:, n, :], p_lt[:, :], -3.0e38, ALU.add, ALU.max).then_inc(run_done, 1)
                if has(s, 0, UNITS):
                    dve.wait_ge(before_done, s + 1)
                    dve.wait_ge(newmax_done, s + 1)
                    if has(s, -2, UNITS):
                        dve.wait_ge(top_high_done, s - 1)
                    nc.vector.tensor_tensor(top[:, b, :], newmax[:, b, :], before[:, b, :], ALU.max).then_inc(top_done, 1)
                if has(s, 2, UNITS):
                    dve.wait_ge(u.gathered[n2], laps(s + 2, n2, RING, 16 * TILES))
                    dve.wait_ge(q_mm, s + 3)
                    if has(s, 1, UNITS):
                        dve.wait_ge(logit_done, s + 2)
                    nc.vector.tensor_tensor(prod[:, :, :].rearrange("p (t h) c -> p t (h c)", t=TILES), kv[:, n2, :, 0, :], p_qs[b][:, :, :], ALU.mult).then_inc(prod_done, 1)
                if has(s, 1, UNITS):
                    dve.wait_ge(run_mm, s + 2)
                    dve.wait_ge(last_done, s + 2)
                    if has(s, -1, UNITS):
                        dve.wait_ge(high_done, s)
                        dve.wait_ge(low_done, s)
                    nc.vector.tensor_tensor(lastmax[:, c, :, :], p_run, high[:, n, :, H:].to_broadcast([P, TILES, H]), ALU.mult).then_inc(lastmax_done, 1)
                if has(s, 0, UNITS):
                    dve.wait_ge(top_high_done, s + 1)
                    if has(s, -2, UNITS):
                        dve.wait_ge(top_mm, s - 1)
                    nc.vector.tensor_tensor(top_low[:, b, :], top[:, b, :], top_high[:, b, :], ALU.subtract).then_inc(top_low_done, 1)
                    if has(s, -2, UNITS):
                        dve.wait_ge(scale_done, s - 1)
                    nc.vector.tensor_tensor(drop[:, b, :], before[:, b, :], top[:, b, :], ALU.subtract).then_inc(drop_done, 1)
                if has(s, 1, UNITS):
                    dve.wait_ge(u.ucol_in, s + 2)
                    if has(s, 0, UNITS):
                        dve.wait_ge(top_done, s + 1)
                    if has(s, -1, UNITS):
                        dve.wait_ge(drop_done, s)
                    nc.vector.tensor_scalar(before[:, c, :], top[:, b, :], u.unit[:, n, 1:2], u.unit[:, n, 2:3], ALU.mult, ALU.add).then_inc(before_done, 1)
                if has(s, -1, UNITS):
                    dve.wait_ge(scale_done, s)
                    if has(s, -2, UNITS):
                        dve.wait_ge(u.acc_done, s - 1)
                    nc.vector.tensor_tensor(scaled[:, :, :], u.acc[:, (p - 2) % RING, :, :],
                                            scale[:, c, :].unsqueeze(2).to_broadcast([P, H, HC]), ALU.mult).then_inc(scaled_done, 1)
                if has(s, HOT_LEAD, UNITS):
                    place_edges(nc, dve, u, s + HOT_LEAD, n4)
                    nc.vector.tensor_tensor(high[:, n4, :, H], u.cols[:, n4, TILES:2 * TILES], u.cols[:, n4, 2 * TILES:], ALU.not_equal).then_inc(last_done, 1)
                if has(s, 2, UNITS):
                    dve.wait_ge(prod_done, s + 3)
                    if has(s, 2 - RING, UNITS):
                        dve.wait_ge(shifted_done, s + 3 - RING)
                    nc.vector.tensor_reduce(out=logit[:, n2, :, :].rearrange("p t h -> p (t h)"), in_=prod[:, :, :], op=ALU.add, axis=AX.X).then_inc(logit_done, 1)
                if has(s, -1, UNITS):
                    q = (p - 1) % RING
                    dve.wait_ge(scaled_done, s)
                    dve.wait_ge(u.sum_mm, s)
                    if has(s, -1 - RING, UNITS):
                        dve.wait_ge(u.stored[q], laps(s - 1 - RING, q, RING, 16))
                    nc.vector.tensor_tensor(u.acc[:, q, :, :], scaled[:, :, :], u.p_sum[0][:, :, :], ALU.add).then_inc(u.acc_done, 1)
                if has(s, 1, UNITS):
                    dve.wait_ge(high_done, s + 2)
                    if has(s, -1, UNITS):
                        dve.wait_ge(node_mm, s)
                    dve.wait_ge(lastmax_done, s + 2)
                    nc.vector.tensor_tensor(low[:, c, :, :], lastmax[:, c, :, :], high[:, n, :, 0:H], ALU.subtract).then_inc(low_done, 1)
                if has(s, 0, UNITS):
                    dve.wait_ge(top_mm, s + 1)
                    dve.wait_ge(logit_done, s + 1)
                    if has(s, -2, UNITS):
                        dve.wait_ge(u.exp_done, s - 1)
                    nc.vector.tensor_tensor(shifted[:, b, :, :], logit[:, p, :, :], p_top, ALU.subtract).then_inc(shifted_done, 1)
                if has(s, HOT_LEAD, UNITS):
                    make_hot(nc, dve, k, u, s + HOT_LEAD, n4)
                if has(s, 1, UNITS):
                    dve.wait_ge(node_mm, s + 2)
                    nc.vector.tensor_scalar(absent[:, c, :], p_node[:, :, H], -1.0, FAR, ALU.add, ALU.mult).then_inc(absent_done, 1)
                if has(s, 0, UNITS):
                    dve.wait_ge(u.exp_done, s + 1)
                    nc.vector.tensor_tensor(
                        u.wgt[:, p, :, :, 0:C], kv[:, p, :, 1, :].rearrange("p t (h c) -> p t h c", h=H),
                        u.wgt[:, p, :, :, C:HC].to_broadcast([P, TILES, H, C]), ALU.mult).then_inc(u.wgt_done, 1)
                if has(s, 1, UNITS):
                    dve.wait_ge(absent_done, s + 2)
                    nc.vector.tensor_tensor(cand[:, c, :, :], p_node[:, :, 0:H], absent[:, c, :].unsqueeze(2).to_broadcast([P, TILES, H]), ALU.add).then_inc(cand_done, 1)
                if has(s, 1, UNITS):
                    dve.wait_ge(cand_done, s + 2)
                    nc.vector.tensor_reduce(out=newmax[:, c, :], in_=cand[:, c, :, :].rearrange("p t h -> p h t"), op=ALU.max, axis=AX.X).then_inc(newmax_done, 1)

            staggered(dve, HOT_LEAD, 1, step)

        @block.scalar
        def _(act):
            def step(s, p):
                b = p % 2
                c = 1 - b
                n4 = (p + HOT_LEAD) % RING
                if has(s, HOT_LEAD + 1, UNITS):
                    unit_scalars(nc, act, k, u, s + HOT_LEAD + 1, (p + HOT_LEAD + 1) % RING, before_done)
                if has(s, 0, UNITS):
                    act.wait_ge(top_done, s + 1)
                    if has(s, -2, UNITS):
                        act.wait_ge(top_mm, s - 1)
                    nc.scalar.copy(top_high[:, b, :], top[:, b, :]).then_inc(top_high_done, 1)
                if has(s, EDGE_LEAD, UNITS):
                    j, q = s + EDGE_LEAD, (p + EDGE_LEAD) % RING
                    act.wait_ge(e_mm, j + 1)
                    if has(j, -RING, UNITS):
                        act.wait_ge(u.wgt_done, j - RING + 1)
                    nc.scalar.copy(kv[:, q, :, :, :], p_e[:, :, :].unsqueeze(2).to_broadcast([P, TILES, 2, D])).then_inc(e_done, 1)
                if has(s, 1, UNITS):
                    act.wait_ge(lastmax_done, s + 2)
                    if has(s, 1 - RING, UNITS):
                        act.wait_ge(node_mm, s + 2 - RING)
                    nc.scalar.copy(high[:, (p + 1) % RING, :, 0:H], lastmax[:, c, :, :]).then_inc(high_done, 1)
                if has(s, 0, UNITS):
                    act.wait_ge(drop_done, s + 1)
                    if has(s, -2, UNITS):
                        act.wait_ge(scaled_done, s - 1)
                    nc.scalar.activation(scale[:, b, :], drop[:, b, :], ACT.Exp).then_inc(scale_done, 1)
                    act.wait_ge(shifted_done, s + 1)
                    if has(s, -RING, UNITS):
                        act.wait_ge(u.sum_mm, s - RING + 1)
                    nc.scalar.activation(u.wgt[:, p, :, :, C], shifted[:, b, :, :], ACT.Exp).then_inc(u.exp_done, 1)
                if has(s, HOT_LEAD, UNITS):
                    copy_hot(nc, act, u, s + HOT_LEAD, n4)
                    copy_hot_t(nc, act, u, s + HOT_LEAD, n4, top_mm)

            staggered(act, max(EDGE_LEAD, HOT_LEAD + 1), 0, step)

        @block.tensor
        def _(pe):
            def edge_features(s, p, i):
                j, q = s + EDGE_LEAD + 1, (p + EDGE_LEAD + 1) % RING
                if not has(s, EDGE_LEAD + 1, UNITS):
                    return
                if i == 0:
                    pe.wait_ge(e_in[q], laps(j, q, RING, 16))
                    if has(j, -1, UNITS):
                        pe.wait_ge(e_done, j)
                e = nc.tensor.matmul(p_e[:, 2 * i:2 * i + 2, :].rearrange("p t c -> p (t c)"), attr[:, q, i, :], k.we[:, :], start=True, stop=True)
                if i == TILES // 2 - 1:
                    e.then_inc(e_mm, 1)

            def step(s, p):
                b = p % 2
                c, n, n2, n3 = 1 - b, (p + 1) % RING, (p + 2) % RING, (p + 3) % RING
                if has(s, 1, UNITS):
                    pe.wait_ge(run_done, s + 2)
                    if has(s, -1, UNITS):
                        pe.wait_ge(shifted_done, s)
                    gate(pe, pe_passed)
                    nc.tensor.transpose(p_edge[:, 0, :], runmax[:, c, :], k.ident[0:TILES * H, 0:TILES * H]).then_inc(run_mm, 1)
                if has(s, 3, UNITS):
                    pe.wait_ge(u.hot_t_done, s + 4)
                    pe.wait_ge(blk_in[n3], laps(s + 3, n3, RING, 32))
                    if has(s, 1, UNITS):
                        pe.wait_ge(prod_done, s + 2)
                    for t in range(TILES):
                        for i in range(PARTS):
                            last = nc.tensor.matmul(p_qs[c][:, t, :], u.hot_t[:, n3, t, :], qblk[:, n3, i, :], start=(i == 0), stop=(i == PARTS - 1))
                    last.then_inc(q_mm, 1)
                if has(s, 0, UNITS):
                    pe.wait_ge(top_low_done, s + 1)
                    pe.wait_ge(top_high_done, s + 1)
                    for t in range(TILES):
                        nc.tensor.matmul(p_top[:, t, :], u.hot_t[:, p, t, :], top_high[:, b, :], start=True, stop=False)
                        last = nc.tensor.matmul(p_top[:, t, :], u.hot_t[:, p, t, :], top_low[:, b, :], start=False, stop=True)
                    last.then_inc(top_mm, 1)
                if has(s, 2, UNITS):
                    pe.wait_ge(logit_done, s + 3)
                    if has(s, 1, UNITS):
                        pe.wait_ge(run_done, s + 2)
                    nc.tensor.transpose(p_lt[:, :], logit[:, n2, :, :].rearrange("p t h -> p (t h)"), k.ident[:, :]).then_inc(lt_mm, 1)
                if has(s, 1, UNITS):
                    pe.wait_ge(low_done, s + 2)
                    pe.wait_ge(high_done, s + 2)
                    if has(s, 0, UNITS):
                        pe.wait_ge(cand_done, s + 1)
                    for t in range(TILES):
                        nc.tensor.matmul(p_node[:, t, :], u.hot[:, n, t, :], high[:, n, t, :], start=True, stop=False)
                        last = nc.tensor.matmul(p_node[:, t, 0:H], u.hot[:, n, t, :], low[:, c, t, :], start=False, stop=True)
                    last.then_inc(node_mm, 1)
                edge_features(s, p, 0)
                if has(s, HOT_LEAD, UNITS):
                    transpose_hot(nc, pe, k, u, s + HOT_LEAD, (p + HOT_LEAD) % RING)
                edge_features(s, p, 1)
                if has(s, 0, UNITS):
                    sum_edges(nc, pe, u, s, p)

            staggered(pe, EDGE_LEAD + 1, 0, step)


def finish(nc, st, k, agg1, node1, out):
    agg = st.sb("z_agg", [P, NBLK, NBLK, H, HC])
    nod = st.sb("z_nod", [P, NBLK, NBLK, 2 * D])
    den = st.sb("z_den", [P, NBLK, H])
    rec = st.sb("z_rec", [P, NBLK, H])
    conv = st.sb("z_conv", [P, NBLK, D])
    y1 = st.sb("z_y1", [P, NBLK, D])
    n1 = st.sb("z_n1", [P, NBLK, D])
    g1 = st.sb("z_g1", [P, NBLK, D])
    hid = st.sb("z_hid", [P, NBLK, D])
    hb = st.sb("z_hb", [P, NBLK, D])
    ht = st.sb("z_ht", [P, NBLK * P])
    act1 = st.sb("z_act1", [P, FF // P, NBLK * P])
    y2 = st.sb("z_y2", [P, NBLK, D])
    n2 = st.sb("z_n2", [P, NBLK, D])
    g2 = st.sb("z_g2", [P, NBLK, D])
    b2 = st.sb("z_b2", [P, NBLK, D])
    y3 = st.sb("z_y3", [P, NBLK, D])
    res = st.sb("z_res", [P, NBLK, NBLK, D])
    p_t = st.ps("z_p_t", [P, NBLK * P])
    p_f = [st.ps(f"z_p_f{i}", [P, NBLK * P]) for i in range(FF // P)]
    p_o = st.ps("z_p_o", [P, NBLK, D])
    ln1, ln2, ln3 = LayerNorm(nc, st, "z_ln1"), LayerNorm(nc, st, "z_ln2"), LayerNorm(nc, st, "z_ln3")
    loaded = st.ring_sems("z_loaded", NBLK)
    stored = st.ring_sems("z_stored", NBLK)
    den_done, rec_done, conv_done, y1_done = st.sem("z_den_done"), st.sem("z_rec_done"), st.sem("z_conv_done"), st.sem("z_y1_done")
    n1_done, g1_done, hid_done, hb_done = st.sem("z_n1_done"), st.sem("z_g1_done"), st.sem("z_hid_done"), st.sem("z_hb_done")
    t_mm, ht_done, f_mm, act_done = st.sem("z_t_mm"), st.sem("z_ht_done"), st.sem("z_f_mm"), st.sem("z_act_done")
    o_mm, y2_done, n2_done, g2_done = st.sem("z_o_mm"), st.sem("z_y2_done"), st.sem("z_n2_done"), st.sem("z_g2_done")
    b2_done, y3_done, res_done = st.sem("z_b2_done"), st.sem("z_y3_done"), st.sem("z_res_done")
    steps = BLOCKS // NBLK

    def wide(row):
        return row[:, :].unsqueeze(1).to_broadcast([P, NBLK, D])

    with nc.Block() as block:

        @block.sync
        def _(sp):
            def step(j, p):
                if has(j, -NBLK, steps):
                    sp.wait_ge(y3_done, j - NBLK + 1)
                sp.dma_start(agg[:, p, :, :, :].rearrange("p b h c -> p b (h c)"), step_rows(agg1, j)).then_inc(loaded[p], 16)
                sp.dma_start(nod[:, p, :, :], step_rows(node1, j)).then_inc(loaded[p], 16)

            over_ring(sp, steps, NBLK, step)

        @block.vector
        def _(dve):
            def step(j, p):
                dve.wait_ge(loaded[p], laps(j, p, NBLK, 32))
                nc.vector.tensor_scalar(den[:, :, :], agg[:, p, :, :, C], 1e-30, None, ALU.max).then_inc(den_done, 1)
                dve.wait_ge(den_done, j + 1)
                nc.vector.reciprocal(rec[:, :, :], den[:, :, :]).then_inc(rec_done, 1)
                dve.wait_ge(rec_done, j + 1)
                nc.vector.tensor_tensor(conv[:, :, :].rearrange("p b (h c) -> p b h c", h=H), agg[:, p, :, :, 0:C],
                                        rec[:, :, :].unsqueeze(3).to_broadcast([P, NBLK, H, C]), ALU.mult).then_inc(conv_done, 1)
                dve.wait_ge(conv_done, j + 1)
                nc.vector.tensor_tensor(y1[:, :, :], conv[:, :, :], nod[:, p, :, 0:D], ALU.add).then_inc(y1_done, 1)
                dve.wait_ge(y1_done, j + 1)
                ln1.on_vector(dve, j, y1[:, :, :], n1[:, :, :], n1_done)
                dve.wait_ge(n1_done, j + 1)
                nc.vector.tensor_tensor(g1[:, :, :], n1[:, :, :], wide(k.g1), ALU.mult).then_inc(g1_done, 1)
                dve.wait_ge(g1_done, j + 1)
                nc.vector.tensor_tensor(hid[:, :, :], g1[:, :, :], wide(k.b1), ALU.add).then_inc(hid_done, 1)
                dve.wait_ge(hid_done, j + 1)
                nc.vector.tensor_tensor(hb[:, :, :], hid[:, :, :], wide(k.bf2), ALU.add).then_inc(hb_done, 1)
                dve.wait_ge(hb_done, j + 1)
                dve.wait_ge(o_mm, j + 1)
                nc.vector.tensor_tensor(y2[:, :, :], hb[:, :, :], p_o[:, :, :], ALU.add).then_inc(y2_done, 1)
                dve.wait_ge(y2_done, j + 1)
                ln2.on_vector(dve, j, y2[:, :, :], n2[:, :, :], n2_done)
                dve.wait_ge(n2_done, j + 1)
                nc.vector.tensor_tensor(g2[:, :, :], n2[:, :, :], wide(k.g2), ALU.mult).then_inc(g2_done, 1)
                dve.wait_ge(g2_done, j + 1)
                nc.vector.tensor_tensor(b2[:, :, :], g2[:, :, :], wide(k.b2), ALU.add).then_inc(b2_done, 1)
                dve.wait_ge(b2_done, j + 1)
                nc.vector.tensor_tensor(y3[:, :, :], b2[:, :, :], nod[:, p, :, D:], ALU.add).then_inc(y3_done, 1)
                dve.wait_ge(y3_done, j + 1)
                if has(j, -NBLK, steps):
                    dve.wait_ge(stored[p], laps(j - NBLK, p, NBLK, 16))
                ln3.on_vector(dve, j, y3[:, :, :], res[:, p, :, :], res_done)

            over_ring(dve, steps, NBLK, step)

        @block.tensor
        def _(pe):
            def step(j, p):
                pe.wait_ge(hid_done, j + 1)
                for b in range(NBLK):
                    last = nc.tensor.transpose(p_t[:, b * P:(b + 1) * P], hid[:, b, :], k.ident[:, :])
                last.then_inc(t_mm, 1)
                pe.wait_ge(ht_done, j + 1)
                for f in range(FF // P):
                    nc.tensor.matmul(p_f[f][:, :], k.wf1[:, f * P:(f + 1) * P], ht[:, :], start=True, stop=True).then_inc(f_mm, 1)
                pe.wait_ge(act_done, 4 * j + 4)
                for b in range(NBLK):
                    for f in range(FF // P):
                        last = nc.tensor.matmul(p_o[:, b, :], act1[:, f, b * P:(b + 1) * P], k.wf2[:, f, :],
                                                start=(f == 0), stop=(f == FF // P - 1))
                last.then_inc(o_mm, 1)

            over_ring(pe, steps, NBLK, step)

        @block.scalar
        def _(act):
            def step(j, p):
                ln1.on_scalar(act, k, j)
                act.wait_ge(t_mm, j + 1)
                nc.scalar.copy(ht[:, :], p_t[:, :]).then_inc(ht_done, 1)
                for f in range(FF // P):
                    act.wait_ge(f_mm, 4 * j + f + 1)
                    nc.scalar.activation(act1[:, f, :], p_f[f][:, :], ACT.Gelu, bias=k.bf1[:, f:f + 1]).then_inc(act_done, 1)
                ln2.on_scalar(act, k, j)
                ln3.on_scalar(act, k, j)

            over_ring(act, steps, NBLK, step)

        @block.gpsimd
        def _(pool):
            def step(j, p):
                pool.wait_ge(res_done, j + 1)
                pool.dma_start(step_rows(out, j), res[:, p, :, :]).then_inc(stored[p], 16)

            over_ring(pool, steps, NBLK, step)
            for p in range(NBLK):
                pool.wait_ge(stored[p], laps(steps - NBLK + p, p, NBLK, 16))


def build(nc, a, out):

    def scratch(name, shape):
        return nc.dram_tensor(name, shape, F32, kind="Internal").ap()

    table0 = scratch("table0", [NPAD, ROW0])
    tgt0 = nc.dram_tensor("tgt0", [NPAD, PARTS * H], BF16, kind="Internal").ap()
    q_table = nc.dram_tensor("q_table", [NPAD, PARTS * D], BF16, kind="Internal").ap()
    agg0 = scratch("agg0", [NPAD, AGG])
    kv_table = scratch("kv_table", [NPAD, 2 * D])
    node1 = scratch("node1", [NPAD, NODE1])
    agg1 = scratch("agg1", [NPAD, AGG])
    neg_rows = scratch("neg_rows", [P * FLAG_TILES, H, P])

    with ExitStack() as ctx:
        st = Store(nc, ctx, ctx)
        k = Names()
        k.iota, k.ident, k.ones = st.sb("k_iota", [P, P]), st.sb("k_ident", [P, P]), st.sb("k_ones", [P, P])
        k.iota_b, k.ident_b = st.sb("k_iota_b", [P, P], BF16), st.sb("k_ident_b", [P, P], BF16)
        k.eps, k.part, k.block_start = st.sb("k_eps", [P, 1]), st.sb("k_part", [P, 1]), st.sb("k_block_start", [P, 1])
        k.ucol = st.sb("k_ucol", [P, UNITS, 3])
        k.ureg = st.sb("k_ureg", [1, UNITS, 3], I32)
        k.w0, k.w0t, k.att0 = st.sb("k_w0", [P, D]), st.sb("k_w0t", [P, D]), st.sb("k_att0", [P, 2 * H])
        k.bias0 = st.sb("k_bias0", [P, D])
        k.wcat1, k.bcat1, k.we = st.sb("k_wcat1", [P, 4 * D]), st.sb("k_bcat1", [P, 4 * D]), st.sb("k_we", [2 * ED, 2 * D])
        k.g1, k.b1, k.g2, k.b2 = st.sb("k_g1", [P, D]), st.sb("k_b1", [P, D]), st.sb("k_g2", [P, D]), st.sb("k_b2", [P, D])
        k.wf1, k.bf1 = st.sb("k_wf1", [P, FF]), st.sb("k_bf1", [P, FF // P])
        k.wf2, k.bf2 = st.sb("k_wf2", [P, FF // P, D]), st.sb("k_bf2", [P, D])
        k.loaded = st.dma_sem("k_loaded")
        k.loads = [
            (k.w0[:, :], a["W0"]), (k.w0t[:, :], a["W0T"]), (k.att0[:, :], a["att0"]),
            (k.wcat1[:, :], a["wcat1"]), (k.we[:, :], a["We"]), (k.wf1[:, :], a["Wf1"]),
            (k.wf2[:, :, :], a["Wf2"]), (k.bf1[:, :], a["bf1"]),
            (k.bcat1[:, :], a["bcat1"].to_broadcast([P, 4 * D])),
        ] + [(t[:, :], a[n].to_broadcast([P, D])) for t, n in (
            (k.bias0, "bias0"), (k.g1, "g1"), (k.b1, "b1"), (k.g2, "g2"), (k.b2, "b2"), (k.bf2, "bf2"))]

        with ExitStack() as c:
            s = Store(nc, c, ctx)
            k.unit_row = s.sb("k_unit_row", [P, UNITS])
            constants(nc, s, k)
            unit_tables(nc, s, k, a)
            s.over()
        for stage, args in (
                (run_flags, (a, neg_rows)),
                (project0, (k, a, table0, tgt0)),
                (gat_layer, (k, a, table0, tgt0, agg0)),
                (middle, (k, a, agg0, kv_table, q_table, node1)),
                (edge_layer, (k, a, kv_table, q_table, neg_rows, agg1)),
                (finish, (k, agg1, node1, out))):
            with ExitStack() as c:
                s = Store(nc, c, ctx)
                stage(nc, s, *args)
                s.over()


def kernel(**inputs):
    import numpy as np
    import concourse.bacc as bacc
    from concourse.bass_utils import run_bass_kernel_spmd

    i = {n: np.asarray(v) for n, v in inputs.items()}
    x = i["x"]
    x_rows = np.zeros((NPAD, D), x.dtype)
    x_rows[:NODES] = x
    src = np.zeros(GROUPS * GE, np.int32)
    src[:EDGES] = i["src"]
    dst = np.full(P * FLAG_TILES * P, NPAD, np.int32)
    dst[:EDGES] = i["dst"]
    prev = np.concatenate([dst[:1], dst[:-1]])
    dst_rows = dst.reshape(P, FLAG_TILES * P)
    prev_rows = prev.reshape(P, FLAG_TILES * P)
    dst = dst[:GROUPS * GE]
    nxt = np.concatenate([dst[1:], dst[-1:]]).reshape(-1, P).copy()
    nxt[:, -1] = -1
    edge_cols = np.concatenate([v.reshape(GROUPS, TILES, P).transpose(0, 2, 1) for v in (src, dst, nxt)], axis=2)
    attr = np.zeros((GROUPS * GE, ED), i["edge_attr_64"].dtype)
    attr[:EDGES] = i["edge_attr_64"]
    we2 = np.zeros((2 * ED, 2 * D), x.dtype)
    we2[:ED, :D] = we2[ED:, D:] = i["L1_gnn_We"]
    att0 = np.zeros((D, 2 * H), x.dtype)
    for h in range(H):
        att0[h * C:(h + 1) * C, h] = i["L0_gnn_a_left"][:, h]
        att0[h * C:(h + 1) * C, H + h] = i["L0_gnn_a_right"][:, h]
    arrays = {
        "x_rows": x_rows, "xT": x_rows.T, "edge_cols": edge_cols, "last_dst": dst[GE - 1::GE].reshape(1, GROUPS),
        "dst_rows": dst_rows, "dst_prev_rows": prev_rows, "attr_t": attr.reshape(GROUPS, TILES // 2, 2, P, ED).transpose(0, 2, 4, 1, 3).reshape(GROUPS, 2 * ED, GE // 2),
        "W0": i["L0_gnn_W"], "W0T": i["L0_gnn_W"].T, "att0": att0, "bias0": i["L0_gnn_bias"].reshape(1, D),
        "wcat1": np.concatenate([i["L1_gnn_W" + n] for n in ("q", "k", "v", "skip")], axis=1),
        "bcat1": np.concatenate([i["L1_gnn_b" + n] for n in ("q", "k", "v", "skip")]).reshape(1, 4 * D),
        "We": we2, "Wf1": i["L1_gnn_Wf1"], "bf1": i["L1_gnn_bf1"].reshape(FF // P, P).T,
        "Wf2": i["L1_gnn_Wf2"].reshape(FF // P, P, D).transpose(1, 0, 2), "bf2": i["L1_gnn_bf2"].reshape(1, D),
        **{n: i["L1_gnn_" + n].reshape(1, D) for n in ("g1", "b1", "g2", "b2")},
    }
    nc = bacc.Bacc("TRN2", target_bir_lowering=False, num_devices=1)
    feed, aps = {}, {}
    for n, v in arrays.items():
        v = np.ascontiguousarray(v)
        feed["in_" + n] = v
        aps[n] = nc.dram_tensor("in_" + n, v.shape, mybir.dt.from_np(v.dtype), kind="ExternalInput").ap()
    out = nc.dram_tensor("out_rows", (NPAD, D), F32, kind="ExternalOutput").ap()
    build(nc, aps, out)
    r = run_bass_kernel_spmd(nc, [feed], core_ids=[0])
    return r.results[0]["out_rows"][:NODES]
```

```python
from contextlib import ExitStack

import concourse.bass as bass
from concourse import mybir

F32 = mybir.dt.float32
BF16 = mybir.dt.bfloat16
I32 = mybir.dt.int32
ALU = mybir.AluOpType
ACT = mybir.ActivationFunctionType
AX = mybir.AxisListType

P = 128
NODES, EDGES, D, H, ED, FF = 12500, 400000, 128, 8, 64, 512
C = D // H
TILES = 4
GE = TILES * P
GROUPS = -(-EDGES // GE)
RING = 8
BLOCKS = -(-NODES // P) + 1
UNITS = GROUPS + BLOCKS - 1
NPAD = BLOCKS * P
FLAG_TILES = 25
HC = C + 1
ROW0 = D + H
AGG = H * HC
NODE1 = 2 * D
PARTS = 3
FAR = 2.0 ** 100
NBLK = 3
EPS_LN = 1e-5

assert UNITS % RING == 0 and BLOCKS % NBLK == 0


def has(j, d, total):
    return 0 <= j + d < total if isinstance(j, int) else True


def staggered(eng, lead, lag, step, total=UNITS, ring=RING):
    for s in range(-lead, ring):
        step(s, s % ring)
    with eng.Fori(ring, total - 2 * ring + 1, ring) as base:
        for p in range(ring):
            step(base + p, p)
    for s in range(total - ring, total + lag):
        step(s, s % ring)


def laps(j, p, ring, n):
    if isinstance(j, int):
        return n * (j // ring + 1)
    return (j - p) * (n // ring) + n if n % ring == 0 else ((j - p) * n) // ring + n


def over_ring(eng, total, ring, step):
    for p in range(ring):
        step(p, p)
    with eng.Fori(ring, total - 2 * ring + 1, ring) as base:
        for p in range(ring):
            step(base + p, p)
    for p in range(ring):
        step(total - ring + p, p)


def gate(eng, passed):
    eng.sem_inc(passed, 1)


class Store:

    def __init__(self, nc, ctx, whole):
        self.nc, self.ctx, self.whole, self.counted = nc, ctx, whole, []

    def sb(self, name, shape, dt=F32):
        return self.ctx.enter_context(self.nc.sbuf_tensor(name, shape, dt))

    def ps(self, name, shape, dt=F32):
        return self.ctx.enter_context(self.nc.psum_tensor(name, shape, dt))

    def sem(self, name):
        self.counted.append(self.ctx.enter_context(self.nc.semaphore(name)))
        return self.counted[-1]

    def dma_sem(self, name):
        return self.whole.enter_context(self.nc.semaphore(name))

    def ring_sems(self, name, n):
        return [self.dma_sem(f"{name}{i}") for i in range(n)]

    def over(self):
        with self.nc.Block() as block:

            @block.sync
            def _(sp):
                for sem in self.counted:
                    sp.sem_clear(sem)


class Names:
    pass


def constants(nc, st, k):
    iota_i = st.sb("iota_i", [P, P], I32)
    part_i = st.sb("part_i", [P, 1], I32)
    unit_i = st.sb("unit_i", [P, UNITS], I32)
    part_f = st.sb("part_f", [P, 1])
    iota_s = st.sem("c_iota")
    done_s = st.sem("c_done")
    conv_s = st.sem("c_conv")
    with nc.Block() as block:

        @block.gpsimd
        def _(pool):
            nc.gpsimd.iota(iota_i[:, :], pattern=[[1, P]], base=0, channel_multiplier=0).then_inc(iota_s, 1)
            nc.gpsimd.iota(part_i[:, :], pattern=[[0, 1]], base=0, channel_multiplier=1).then_inc(iota_s, 1)
            nc.gpsimd.iota(unit_i[:, :], pattern=[[1, UNITS]], base=0, channel_multiplier=0).then_inc(iota_s, 1)

        @block.vector
        def _(dve):
            dve.wait_ge(iota_s, 3)
            nc.vector.tensor_copy(k.iota_b[:, :], iota_i[:, :]).then_inc(done_s, 1)
            nc.vector.tensor_copy(k.iota[:, :], iota_i[:, :]).then_inc(conv_s, 1)
            nc.vector.tensor_copy(part_f[:, :], part_i[:, :]).then_inc(conv_s, 1)
            nc.vector.tensor_copy(k.unit_row[:, :], unit_i[:, :]).then_inc(conv_s, 1)
            nc.vector.memset(k.ones[:, :], 1.0).then_inc(done_s, 1)
            nc.vector.memset(k.eps[:, :], EPS_LN).then_inc(done_s, 1)
            dve.wait_ge(conv_s, 3)
            nc.vector.tensor_scalar(k.ident_b[:, :], k.iota[:, :], part_f[:, 0:1], None, ALU.is_equal).then_inc(done_s, 1)
            nc.vector.tensor_scalar(k.ident[:, :], k.iota[:, :], part_f[:, 0:1], None, ALU.is_equal).then_inc(done_s, 1)
            nc.vector.tensor_scalar(k.block_start[:, :], part_f[:, :], float(P), None, ALU.mult).then_inc(done_s, 1)
            nc.vector.tensor_copy(k.part[:, :], part_f[:, :]).then_inc(done_s, 1)

        @block.sync
        def _(sp):
            n = 0
            for dst, src in k.loads:
                sp.dma_start(dst, src).then_inc(k.loaded, 16)
                n += 16
            sp.wait_ge(k.loaded, n)


def unit_tables(nc, st, k, a):
    last_i = st.sb("u_last_i", [BLOCKS, GROUPS], I32)
    below = st.sb("u_below", [BLOCKS, GROUPS])
    first = st.sb("u_first", [BLOCKS, 2])
    begun = st.sb("u_begun", [BLOCKS, UNITS])
    blk = st.sb("u_blk", [P, UNITS + 1])
    grp = st.sb("u_grp", [1, UNITS])
    pb = [st.ps(f"u_psum{i}", [P, UNITS // 2]) for i in range(2)]
    last_in = st.dma_sem("u_last_in")
    step = st.sem("u_step")
    counted = st.sem("u_counted")
    begun_s = st.sem("u_begun_s")
    half = UNITS // 2
    with nc.Block() as block:

        @block.sync
        def _(sp):
            sp.dma_start(last_i[:, :], a["last_dst"].to_broadcast([BLOCKS, GROUPS])).then_inc(last_in, 16)

        @block.vector
        def _(dve):
            dve.wait_ge(last_in, 16)
            nc.vector.tensor_scalar(below[:, :], last_i[:, :], k.block_start[0:BLOCKS, 0:1], None, ALU.is_lt).then_inc(step, 1)
            dve.wait_ge(step, 1)
            nc.vector.tensor_reduce(out=first[:, 0:1], in_=below[:, :], op=ALU.add, axis=AX.X).then_inc(step, 1)
            dve.wait_ge(step, 2)
            nc.vector.tensor_tensor(first[:, 1:2], first[:, 0:1], k.part[0:BLOCKS, :], ALU.add).then_inc(step, 1)
            dve.wait_ge(step, 3)
            nc.vector.tensor_scalar(begun[:, :], k.unit_row[0:BLOCKS, :], first[:, 1:2], None, ALU.is_ge).then_inc(begun_s, 1)
            nc.vector.memset(blk[:, 0:1], -1.0).then_inc(step, 1)
            for i in range(2):
                dve.wait_ge(counted, i + 1)
                nc.vector.tensor_scalar(blk[:, 1 + i * half:1 + (i + 1) * half], pb[i][:, :], -1.0, None, ALU.add).then_inc(step, 1)
            dve.wait_ge(step, 6)
            nc.vector.tensor_scalar(k.ucol[:, :, 0], blk[:, 1:], float(P), None, ALU.mult).then_inc(step, 1)
            nc.vector.tensor_tensor(k.ucol[:, :, 1], blk[:, 1:], blk[:, 0:UNITS], ALU.is_equal).then_inc(step, 1)
            nc.vector.tensor_tensor(grp[:, :], k.unit_row[0:1, :], blk[0:1, 1:], ALU.subtract).then_inc(step, 1)
            nc.vector.tensor_copy(k.ureg[:, :, 1], blk[0:1, 1:]).then_inc(step, 1)
            nc.vector.memset(k.ureg[:, :, 2:], 0).then_inc(step, 1)
            dve.wait_ge(step, 11)
            nc.vector.tensor_copy(k.ureg[:, RING:, 2], blk[0:1, 1:UNITS + 1 - RING]).then_inc(step, 1)
            nc.vector.tensor_scalar(k.ucol[:, :, 2], k.ucol[:, :, 1], -1.0, 2.0 * FAR, ALU.add, ALU.mult).then_inc(step, 1)
            nc.vector.tensor_copy(k.ureg[:, :, 0], grp[:, :]).then_inc(step, 1)

        @block.tensor
        def _(pe):
            pe.wait_ge(begun_s, 1)
            for i in range(2):
                nc.tensor.matmul(pb[i][:, :], k.ones[0:BLOCKS, :], begun[:, i * half:(i + 1) * half],
                                 start=True, stop=True).then_inc(counted, 1)


class RunFlags:

    def __init__(self, nc, st, a, far_rows):
        self.nc, self.a = nc, a
        self.here = st.sb("f_here", [P, FLAG_TILES * P], I32)
        self.prev = st.sb("f_prev", [P, FLAG_TILES * P], I32)
        self.flag = st.sb("f_flag", [P, FLAG_TILES * P])
        self.neg = st.sb("f_neg", [P, FLAG_TILES * P])
        self.come = st.dma_sem("f_in")
        self.made = st.sem("f_made")
        self.out = st.dma_sem("f_out")
        self.rows = far_rows.rearrange("(p k) h e -> p k h e", p=P)

    def on_pool(self, pool):
        pool.dma_start(self.here[:, :], self.a["dst_rows"]).then_inc(self.come, 16)
        pool.dma_start(self.prev[:, :], self.a["dst_prev_rows"]).then_inc(self.come, 16)
        pool.wait_ge(self.made, 2)
        for h in range(H):
            pool.dma_start(self.rows[:, :, h, :], self.neg[:, :].rearrange("p (k e) -> p k e", e=P)).then_inc(self.out, 16)
        pool.wait_ge(self.out, 16 * H)

    def on_vector(self, dve):
        nc = self.nc
        dve.wait_ge(self.come, 32)
        nc.vector.tensor_tensor(self.flag[:, :], self.here[:, :], self.prev[:, :], ALU.not_equal).then_inc(self.made, 1)
        dve.wait_ge(self.made, 1)
        nc.vector.tensor_scalar(self.neg[:, :], self.flag[:, :], -3.0e38, None, ALU.mult).then_inc(self.made, 1)


class Split:

    def __init__(self, nc, st, name, shape):
        self.nc = nc
        self.left = [st.sb(f"{name}_left{i}", shape) for i in range(2)]
        self.part_done = [st.sem(f"{name}_part{i}") for i in range(2)]
        self.left_done = [st.sem(f"{name}_leftd{i}") for i in range(2)]

    def on_vector(self, dve, j, value, part, done):
        nc = self.nc
        for i in range(PARTS):
            last = nc.vector.tensor_copy(part(i), value)
            if i == PARTS - 1:
                last.then_inc(done, 1)
                return
            last.then_inc(self.part_done[i], 1)
            dve.wait_ge(self.part_done[i], j + 1)
            left = self.left[i]
            nc.vector.tensor_tensor(left[tuple(slice(None) for _ in left.shape)], value, part(i), ALU.subtract).then_inc(self.left_done[i], 1)
            dve.wait_ge(self.left_done[i], j + 1)
            value = left[tuple(slice(None) for _ in left.shape)]


def project0(nc, st, k, a, table0, tgt0, neg_rows):
    flags = RunFlags(nc, st, a, neg_rows)
    wcat = st.sb("p_wcat", [P, D + 2 * H])
    xt = st.sb("p_xt", [P, NBLK, 3 * P])
    res = st.sb("p_res", [P, NBLK, 3, ROW0])
    parts = st.sb("p_parts", [P, NBLK, 3, PARTS, H], BF16)
    split = Split(nc, st, "p_split", [P, 3, H])
    pw = st.ps("p_pw", [P, 2 * H])
    pp = [st.ps(f"p_pp{i}", [P, 3, D + 2 * H]) for i in range(NBLK)]
    w_ready, w_mm = st.sem("p_w_ready"), st.sem("p_w_mm")
    x_in = st.ring_sems("p_x_in", NBLK)
    mm_done, res_done, copied = st.sem("p_mm_done"), st.sem("p_res_done"), st.sem("p_copied")
    stored = st.ring_sems("p_stored", NBLK)
    steps = BLOCKS // 3
    t0 = table0.rearrange("(s b p) c -> s p b c", b=3, p=P)
    t1 = tgt0.rearrange("(s b p) c -> s p b c", b=3, p=P)
    xs = a["xT"].rearrange("p (s c) -> s p c", s=steps)
    with nc.Block() as block:

        @block.sync
        def _(sp):
            def step(j, p):
                if has(j, -NBLK, steps):
                    sp.wait_ge(mm_done, j - NBLK + 1)
                sp.dma_start(xt[:, p, :], xs[bass.ds(j, 1), :, :].rearrange("o p c -> (o p) c")).then_inc(x_in[p], 16)

            over_ring(sp, steps, NBLK, step)

        @block.gpsimd
        def _(pool):
            flags.on_pool(pool)

        @block.tensor
        def _(pe):
            nc.tensor.matmul(pw[:, :], k.w0t[:, :], k.att0[:, :], start=True, stop=True).then_inc(w_mm, 1)
            pe.wait_ge(w_ready, 2)

            def step(j, p):
                if has(j, -NBLK, steps):
                    pe.wait_ge(res_done, j - NBLK + 1)
                pe.wait_ge(x_in[p], laps(j, p, NBLK, 16))
                for b in range(3):
                    last = nc.tensor.matmul(pp[p][:, b, :], xt[:, p, b * P:(b + 1) * P], wcat[:, :], start=True, stop=True)
                last.then_inc(mm_done, 1)

            over_ring(pe, steps, NBLK, step)

        @block.vector
        def _(dve):
            nc.vector.tensor_copy(wcat[:, 0:D], k.w0[:, :]).then_inc(w_ready, 1)
            dve.wait_ge(w_mm, 1)
            nc.vector.tensor_copy(wcat[:, D:], pw[:, :]).then_inc(w_ready, 1)
            flags.on_vector(dve)

            def step(j, p):
                if has(j, -NBLK, steps):
                    dve.wait_ge(stored[p], laps(j - NBLK, p, NBLK, 32))
                dve.wait_ge(mm_done, j + 1)
                nc.vector.tensor_copy(res[:, p, :, :], pp[p][:, :, 0:ROW0]).then_inc(copied, 1)
                split.on_vector(dve, j, pp[p][:, :, ROW0:], lambda i: parts[:, p, :, i, :], res_done)

            over_ring(dve, steps, NBLK, step)

        @block.scalar
        def _(act):
            def step(j, p):
                act.wait_ge(res_done, j + 1)
                act.wait_ge(copied, j + 1)
                act.dma_start(t0[bass.ds(j, 1), :, :, :].rearrange("o p b c -> (o p) b c"), res[:, p, :, :]).then_inc(stored[p], 16)
                act.dma_start(t1[bass.ds(j, 1), :, :, :].rearrange("o p b c -> (o p) b c"), parts[:, p, :, :, :].rearrange("p b i h -> p b (i h)")).then_inc(stored[p], 16)

            over_ring(act, steps, NBLK, step)
            for p in range(NBLK):
                act.wait_ge(stored[p], laps(steps - NBLK + p, p, NBLK, 32))


def rows_of(table, b):
    return table.rearrange("(b p) c -> b p c", p=P)[bass.ds(b, 1), :, :].rearrange("o p c -> (o p) c")


def layer_buffers(nc, st, u, name, sum_banks):
    u.cols = st.sb(name + "_cols", [P, RING, 3 * TILES], I32)
    u.unit = st.sb(name + "_unit", [P, RING, 3])
    u.rel = st.sb(name + "_rel", [P, RING, TILES])
    u.hot = st.sb(name + "_hot", [P, RING, TILES, P], BF16)
    u.hot_f = st.sb(name + "_hot_f", [P, RING, TILES, P])
    u.hot_t = st.sb(name + "_hot_t", [P, RING, TILES, P], BF16)
    u.wgt = st.sb(name + "_wgt", [P, RING, TILES, H, HC])
    u.acc = st.sb(name + "_acc", [P, RING, H, HC])
    u.p_hot = st.ps(name + "_p_hot", [P, TILES, P], BF16)
    u.p_sum = [st.ps(f"{name}_p_sum{i}", [P, H, HC]) for i in range(sum_banks)]
    u.cols_in = st.ring_sems(name + "_cols_in", RING)
    u.gathered = st.ring_sems(name + "_gathered", RING)
    u.stored = st.ring_sems(name + "_stored", RING)
    u.ucol_in, u.rel_done, u.hot_done = st.sem(name + "_ucol_in"), st.sem(name + "_rel_done"), st.sem(name + "_hot_done")
    u.hot_mm, u.hot_t_done, u.hot_f_done = st.sem(name + "_hot_mm"), st.sem(name + "_hot_t_done"), st.sem(name + "_hot_f_done")
    u.exp_done, u.wgt_done, u.sum_mm = st.sem(name + "_exp_done"), st.sem(name + "_wgt_done"), st.sem(name + "_sum_mm")
    u.acc_done, u.pool_passed, u.sp_passed = st.sem(name + "_acc_done"), st.sem(name + "_pool_passed"), st.sem(name + "_sp_passed")


def unit_registers(nc, sp, k, regs, j):
    sp.load(regs, k.ureg[0:1, bass.ds(j, 1), :].rearrange("a o c -> a (o c)"))
    return (sp.snap(regs[0], min_val=0, max_val=GROUPS - 1), sp.snap(regs[1], min_val=0, max_val=BLOCKS - 1),
            sp.snap(regs[2], min_val=0, max_val=BLOCKS - 1))


def store_sums(nc, sp, u, j, p, blk, agg):
    sp.wait_ge(u.acc_done, j + 1)
    gate(sp, u.sp_passed)
    if has(j, -1, UNITS):
        q = (p - 1) % RING
        sp.wait_ge(u.stored[q], laps(j - 1, q, RING, 16))
        gate(sp, u.sp_passed)
    sp.dma_start(rows_of(agg, blk), u.acc[:, p, :, :].rearrange("p h c -> p (h c)")).then_inc(u.stored[p], 16)


def store_last_sums(nc, sp, k, u, agg):
    for j in range(UNITS - RING, UNITS):
        blk = sp.value_load(k.ureg[0:1, j, 1:2], min_val=0, max_val=BLOCKS - 1)
        store_sums(nc, sp, u, j, j % RING, blk, agg)
    for p in range(RING):
        sp.wait_ge(u.stored[p], laps(UNITS - RING + p, p, RING, 16))


def load_indices(nc, sp, a, u, j, p, grp, cols_read):
    if has(j, -RING, UNITS):
        sp.wait_ge(u.gathered[p], laps(j - RING, p, RING, 16 * TILES))
        gate(sp, u.sp_passed)
        sp.wait_ge(cols_read, j - RING + 1)
        gate(sp, u.sp_passed)
    sp.dma_start(u.cols[:, p, :], a["edge_cols"][bass.ds(grp, 1), :, :].rearrange("o p c -> (o p) c")).then_inc(u.cols_in[p], 16)


def gather_rows(nc, pool, u, j, p, table, dest):
    pool.wait_ge(u.cols_in[p], laps(j, p, RING, 16))
    gate(pool, u.pool_passed)
    add = {} if dest.add is None else {"compute_op": dest.add}
    for t in range(TILES):
        nc.gpsimd.indirect_dma_start(
            out=dest.at(p, t), out_offset=None, in_=table,
            in_offset=bass.IndirectOffsetOnAxis(ap=u.cols[:, p, t:t + 1], axis=0), **add).then_inc(u.gathered[p], 16)


def unit_scalars(nc, act, k, u, j, p, last_use):
    if has(j, -RING, UNITS):
        act.wait_ge(last_use, j - RING + 1)
    nc.scalar.copy(u.unit[:, p, :], k.ucol[:, bass.ds(j, 1), :].rearrange("p o c -> p (o c)")).then_inc(u.ucol_in, 1)


def place_edges(nc, dve, u, j, p):
    dve.wait_ge(u.cols_in[p], laps(j, p, RING, 16))
    dve.wait_ge(u.ucol_in, j + 1)
    nc.vector.tensor_scalar(u.rel[:, p, :], u.cols[:, p, TILES:2 * TILES], u.unit[:, p, 0:1], None, ALU.subtract).then_inc(u.rel_done, 1)


def make_hot(nc, dve, k, u, j, p):
    dve.wait_ge(u.rel_done, j + 1)
    if has(j, -RING, UNITS):
        dve.wait_ge(u.hot_f_done, j - RING + 1)
        dve.wait_ge(u.sum_mm, j - RING + 1)
    for t in range(TILES):
        last = nc.vector.tensor_scalar(u.hot[:, p, t, :], k.iota_b[:, :], u.rel[:, p, t:t + 1], None, ALU.is_equal)
    last.then_inc(u.hot_done, 1)


def copy_hot(nc, act, u, j, p):
    act.wait_ge(u.hot_done, j + 1)
    if has(j, -RING, UNITS):
        act.wait_ge(u.sum_mm, j - RING + 1)
    nc.scalar.copy(u.hot_f[:, p, :, :], u.hot[:, p, :, :]).then_inc(u.hot_f_done, 1)


def transpose_hot(nc, pe, k, u, j, p):
    pe.wait_ge(u.hot_done, j + 1)
    if has(j, -1, UNITS):
        pe.wait_ge(u.hot_t_done, j)
    for t in range(TILES):
        last = nc.tensor.transpose(u.p_hot[:, t, :], u.hot[:, p, t, :], k.ident_b[:, :])
    last.then_inc(u.hot_mm, 1)


def copy_hot_t(nc, act, u, j, p, last_use):
    act.wait_ge(u.hot_mm, j + 1)
    if has(j, -RING, UNITS):
        act.wait_ge(last_use, j - RING + 1)
    nc.scalar.copy(u.hot_t[:, p, :, :], u.p_hot[:, :, :]).then_inc(u.hot_t_done, 1)


def sum_edges(nc, pe, u, j, p):
    pe.wait_ge(u.wgt_done, j + 1)
    pe.wait_ge(u.hot_f_done, j + 1)
    banks = len(u.p_sum)
    if has(j, -banks, UNITS):
        pe.wait_ge(u.acc_done, j + 1 - banks)
    for t in range(TILES):
        last = nc.tensor.matmul(u.p_sum[p % banks][:, :, :].rearrange("p h c -> p (h c)"), u.hot_f[:, p, t, :],
                                u.wgt[:, p, t, :, :].rearrange("p h c -> p (h c)"), start=(t == 0), stop=(t == TILES - 1))
    last.then_inc(u.sum_mm, 1)


class Dest:

    def __init__(self, at, add=None):
        self.at, self.add = at, add


def gat_layer(nc, st, k, a, table0, tgt0, agg0):
    u = Names()
    layer_buffers(nc, st, u, "g", 2)
    rows = st.sb("g_rows", [P, RING, TILES, ROW0])
    tblk = st.sb("g_tblk", [P, RING, PARTS, H], BF16)
    score = st.sb("g_score", [P, RING, TILES * H])
    leak = st.sb("g_leak", [P, RING, TILES, H])
    p_tgt = [st.ps(f"g_p_tgt{i}", [P, TILES, H]) for i in range(2)]
    tblk_in = st.ring_sems("g_tblk_in", RING)
    tgt_mm, score_done, leak_done, zeroed = st.sem("g_tgt_mm"), st.sem("g_score_done"), st.sem("g_leak_done"), st.sem("g_zeroed")
    regs = [nc.sync.alloc_register(f"g_reg{i}") for i in range(3)]
    dest = Dest(lambda s, t: rows[:, s, t, :])

    with nc.Block() as block:

        @block.sync
        def _(sp):
            def step(j, p):
                grp, blk, old = unit_registers(nc, sp, k, regs, j)
                load_indices(nc, sp, a, u, j, p, grp, u.rel_done)
                if has(j, -RING, UNITS):
                    sp.wait_ge(tgt_mm, j - RING + 1)
                    gate(sp, u.sp_passed)
                sp.dma_start(tblk[:, p, :, :].rearrange("p i h -> p (i h)"), rows_of(tgt0, blk)).then_inc(tblk_in[p], 16)
                if has(j, -RING, UNITS):
                    store_sums(nc, sp, u, j - RING, p, old, agg0)

            over_ring(sp, UNITS, RING, step)
            store_last_sums(nc, sp, k, u, agg0)

        @block.gpsimd
        def _(pool):
            def step(j, p):
                if has(j, -RING, UNITS):
                    pool.wait_ge(u.wgt_done, j - RING + 1)
                    gate(pool, u.pool_passed)
                gather_rows(nc, pool, u, j, p, table0, dest)

            over_ring(pool, UNITS, RING, step)

        @block.vector
        def _(dve):
            nc.vector.memset(u.acc[:, RING - 1, :, :], 0.0).then_inc(zeroed, 1)
            dve.wait_ge(zeroed, 1)

            def step(s, p):
                if has(s, 3, UNITS):
                    place_edges(nc, dve, u, s + 3, (p + 3) % RING)
                if has(s, 1, UNITS):
                    j, q = s + 1, (p + 1) % RING
                    dve.wait_ge(u.gathered[q], laps(j, q, RING, 16 * TILES))
                    dve.wait_ge(tgt_mm, j + 1)
                    nc.vector.tensor_tensor(score[:, q, :].rearrange("p (t h) -> p t h", h=H), rows[:, q, :, D:], p_tgt[q % 2][:, :, :], ALU.add).then_inc(score_done, 1)
                if has(s, -1, UNITS):
                    j, q = s - 1, (p - 1) % RING
                    dve.wait_ge(u.sum_mm, j + 1)
                    if has(j, -RING, UNITS):
                        dve.wait_ge(u.stored[q], laps(j - RING, q, RING, 16))
                    if has(j, -1, UNITS):
                        dve.wait_ge(u.acc_done, j)
                    nc.vector.scalar_tensor_tensor(
                        out=u.acc[:, q, :, :].rearrange("p h c -> p (h c)"), in0=u.acc[:, (q - 1) % RING, :, :].rearrange("p h c -> p (h c)"),
                        scalar=u.unit[:, q, 1:2], in1=u.p_sum[q % 2][:, :, :].rearrange("p h c -> p (h c)"),
                        op0=ALU.mult, op1=ALU.add).then_inc(u.acc_done, 1)
                if has(s, 3, UNITS):
                    make_hot(nc, dve, k, u, s + 3, (p + 3) % RING)
                if has(s, 1, UNITS):
                    j, q = s + 1, (p + 1) % RING
                    dve.wait_ge(score_done, j + 1)
                    nc.vector.scalar_tensor_tensor(
                        out=leak[:, q, :, :].rearrange("p t h -> p (t h)"), in0=score[:, q, :], scalar=0.2,
                        in1=score[:, q, :], op0=ALU.mult, op1=ALU.max).then_inc(leak_done, 1)
                if has(s, 0, UNITS):
                    dve.wait_ge(u.exp_done, s + 1)
                    nc.vector.tensor_tensor(
                        u.wgt[:, p, :, :, 0:C], rows[:, p, :, 0:D].rearrange("p t (h c) -> p t h c", h=H),
                        u.wgt[:, p, :, :, C:HC].to_broadcast([P, TILES, H, C]), ALU.mult).then_inc(u.wgt_done, 1)

            staggered(dve, 3, 1, step)

        @block.scalar
        def _(act):
            def step(s, p):
                if has(s, 4, UNITS):
                    unit_scalars(nc, act, k, u, s + 4, (p + 4) % RING, u.acc_done)
                if has(s, 3, UNITS):
                    copy_hot(nc, act, u, s + 3, (p + 3) % RING)
                    copy_hot_t(nc, act, u, s + 3, (p + 3) % RING, tgt_mm)
                if has(s, 1, UNITS):
                    j, q = s + 1, (p + 1) % RING
                    act.wait_ge(leak_done, j + 1)
                    if has(j, -RING, UNITS):
                        act.wait_ge(u.sum_mm, j - RING + 1)
                    nc.scalar.activation(u.wgt[:, q, :, :, C], leak[:, q, :, :], ACT.Exp).then_inc(u.exp_done, 1)

            staggered(act, 4, 0, step)

        @block.tensor
        def _(pe):
            def step(s, p):
                if has(s, 2, UNITS):
                    j, q = s + 2, (p + 2) % RING
                    pe.wait_ge(u.hot_t_done, j + 1)
                    pe.wait_ge(tblk_in[q], laps(j, q, RING, 16))
                    if has(j, -2, UNITS):
                        pe.wait_ge(score_done, j - 1)
                    for t in range(TILES):
                        for i in range(PARTS):
                            last = nc.tensor.matmul(p_tgt[q % 2][:, t, :], u.hot_t[:, q, t, :], tblk[:, q, i, :],
                                                    start=(i == 0), stop=(i == PARTS - 1))
                    last.then_inc(tgt_mm, 1)
                if has(s, 3, UNITS):
                    transpose_hot(nc, pe, k, u, s + 3, (p + 3) % RING)
                if has(s, 0, UNITS):
                    sum_edges(nc, pe, u, s, p)

            staggered(pe, 3, 0, step)


def step_rows(table, j):
    return table.rearrange("(s b p) c -> s p b c", b=NBLK, p=P)[bass.ds(j, 1), :, :, :].rearrange("o p b c -> (o p) b c")


class LayerNorm:

    def __init__(self, nc, st, name):
        self.nc = nc
        self.stats = st.sb(name + "_stats", [P, NBLK, 6])
        self.mv = st.sb(name + "_mv", [P, NBLK, 2])
        self.std = st.sb(name + "_std", [P, NBLK])
        self.rstd = st.sb(name + "_rstd", [P, NBLK])
        self.stats_done, self.mv_done = st.sem(name + "_stats_done"), st.sem(name + "_mv_done")
        self.passed = st.sem(name + "_passed")
        self.std_done, self.rstd_done = st.sem(name + "_std_done"), st.sem(name + "_rstd_done")

    def moments(self, dve, j, y):
        nc = self.nc
        for b in range(NBLK):
            last = nc.vector.bn_stats(self.stats[:, b, :], y[:, b, :])
        last.then_inc(self.stats_done, 1)
        dve.wait_ge(self.stats_done, j + 1)
        gate(dve, self.passed)
        for b in range(NBLK):
            last = nc.vector.bn_aggr(self.mv[:, b, :], self.stats[:, b, :])
        last.then_inc(self.mv_done, 1)

    def normalize(self, dve, j, y, out, done):
        nc = self.nc
        dve.wait_ge(self.std_done, j + 1)
        nc.vector.reciprocal(self.rstd[:, :], self.std[:, :]).then_inc(self.rstd_done, 1)
        dve.wait_ge(self.rstd_done, j + 1)
        for b in range(NBLK):
            last = nc.vector.tensor_scalar(out[:, b, :], y[:, b, :], self.mv[:, b, 0:1], self.rstd[:, b:b + 1],
                                           ALU.subtract, ALU.mult)
        last.then_inc(done, 1)

    def on_scalar(self, act, k, j):
        act.wait_ge(self.mv_done, j + 1)
        self.nc.scalar.activation(self.std[:, :], self.mv[:, :, 1], ACT.Sqrt, bias=k.eps[:, 0:1]).then_inc(self.std_done, 1)


def middle(nc, st, k, a, agg0, kv_table, q_table, node1):
    agg = st.sb("m_agg", [P, NBLK, NBLK, H, HC])
    xin = st.sb("m_xin", [P, NBLK, NBLK, D])
    den = st.sb("m_den", [P, NBLK, H])
    rec = st.sb("m_rec", [P, NBLK, H])
    att = st.sb("m_att", [P, NBLK, D])
    attb = st.sb("m_attb", [P, NBLK, D])
    y = st.sb("m_y", [P, NBLK, D])
    x1t = st.sb("m_x1t", [P, NBLK, P])
    node = st.sb("m_node", [P, NBLK, NBLK, NODE1])
    kv = st.sb("m_kv", [P, NBLK, NBLK, 2 * D])
    p_t = st.ps("m_p_t", [P, NBLK, P])
    p_w = [st.ps(f"m_p_w{b}", [P, 4 * D]) for b in range(NBLK)]
    qparts = st.sb("m_qparts", [P, NBLK, NBLK, PARTS, D], BF16)
    q = st.sb("m_q", [P, NBLK, D])
    split = Split(nc, st, "m_split", [P, NBLK, D])
    q_done = st.sem("m_q_done")
    ln = LayerNorm(nc, st, "m_ln")
    loaded = st.ring_sems("m_loaded", NBLK)
    stored = st.ring_sems("m_stored", NBLK)
    scaled, den_done, rec_done = st.sem("m_scaled"), st.sem("m_den_done"), st.sem("m_rec_done")
    att_done, attb_done, y_done = st.sem("m_att_done"), st.sem("m_attb_done"), st.sem("m_y_done")
    x1_done, t_mm, x1t_done = st.sem("m_x1_done"), st.sem("m_t_mm"), st.sem("m_x1t_done")
    w_mm, split_done, node_done = st.sem("m_w_mm"), st.sem("m_split_done"), st.sem("m_node_done")
    steps = BLOCKS // NBLK
    with nc.Block() as block:

        @block.sync
        def _(sp):
            def step(j, p):
                if has(j, -NBLK, steps):
                    sp.wait_ge(y_done, j - NBLK + 1)
                sp.dma_start(agg[:, p, :, :, :].rearrange("p b h c -> p b (h c)"), step_rows(agg0, j)).then_inc(loaded[p], 16)
                sp.dma_start(xin[:, p, :, :], step_rows(a["x_rows"], j)).then_inc(loaded[p], 16)

            over_ring(sp, steps, NBLK, step)

        @block.vector
        def _(dve):
            nc.vector.tensor_scalar(k.wcat1[:, 0:D], k.wcat1[:, 0:D], float(C) ** -0.5, None, ALU.mult).then_inc(scaled, 1)
            nc.vector.tensor_scalar(k.bcat1[:, 0:D], k.bcat1[:, 0:D], float(C) ** -0.5, None, ALU.mult).then_inc(scaled, 1)
            dve.wait_ge(scaled, 2)

            def step(s, p):
                j, n = s + 1, (p + 1) % NBLK
                if has(s, 1, steps):
                    dve.wait_ge(loaded[n], laps(j, n, NBLK, 32))
                    nc.vector.tensor_scalar(den[:, :, :], agg[:, n, :, :, C], 1e-16, None, ALU.add).then_inc(den_done, 1)
                    dve.wait_ge(den_done, j + 1)
                    nc.vector.reciprocal(rec[:, :, :], den[:, :, :]).then_inc(rec_done, 1)
                    dve.wait_ge(rec_done, j + 1)
                    nc.vector.tensor_tensor(att[:, :, :].rearrange("p b (h c) -> p b h c", h=H), agg[:, n, :, :, 0:C],
                                            rec[:, :, :].unsqueeze(3).to_broadcast([P, NBLK, H, C]), ALU.mult).then_inc(att_done, 1)
                    dve.wait_ge(att_done, j + 1)
                    nc.vector.tensor_tensor(attb[:, :, :], att[:, :, :], k.bias0[:, :].unsqueeze(1).to_broadcast([P, NBLK, D]), ALU.add).then_inc(attb_done, 1)
                    dve.wait_ge(attb_done, j + 1)
                    nc.vector.tensor_tensor(y[:, :, :], attb[:, :, :], xin[:, n, :, :], ALU.add).then_inc(y_done, 1)
                    dve.wait_ge(y_done, j + 1)
                    ln.moments(dve, j, y[:, :, :])
                if has(s, 0, steps):
                    dve.wait_ge(w_mm, s + 1)
                    for b in range(NBLK):
                        w = p_w[b]
                        nc.vector.tensor_tensor(kv[:, p, b, :], w[:, D:3 * D], k.bcat1[:, D:3 * D], ALU.add).then_inc(split_done, 1)
                        nc.vector.tensor_tensor(q[:, b, :], w[:, 0:D], k.bcat1[:, 0:D], ALU.add).then_inc(split_done, 1)
                        nc.vector.tensor_tensor(node[:, p, b, 0:D], w[:, 3 * D:], k.bcat1[:, 3 * D:], ALU.add).then_inc(split_done, 1)
                if has(s, 1, steps):
                    if has(j, -NBLK, steps):
                        dve.wait_ge(stored[n], laps(j - NBLK, n, NBLK, 48))
                    ln.normalize(dve, j, y[:, :, :], node[:, n, :, D:], x1_done)
                if has(s, 0, steps):
                    dve.wait_ge(split_done, 9 * s + 9)
                    nc.vector.tensor_tensor(node[:, p, :, 0:D], node[:, p, :, 0:D], node[:, p, :, D:], ALU.add).then_inc(node_done, 1)
                    split.on_vector(dve, s, q[:, :, :], lambda i: qparts[:, p, :, i, :], q_done)

            staggered(dve, 1, 0, step, steps, NBLK)

        @block.tensor
        def _(pe):
            pe.wait_ge(scaled, 2)

            def step(j, p):
                pe.wait_ge(x1_done, j + 1)
                if has(j, -1, steps):
                    pe.wait_ge(x1t_done, j)
                for b in range(NBLK):
                    last = nc.tensor.transpose(p_t[:, b, :], node[:, p, b, D:], k.ident[:, :])
                last.then_inc(t_mm, 1)
                pe.wait_ge(x1t_done, j + 1)
                if has(j, -1, steps):
                    pe.wait_ge(node_done, j)
                for b in range(NBLK):
                    last = nc.tensor.matmul(p_w[b][:, :], x1t[:, b, :], k.wcat1[:, :], start=True, stop=True)
                last.then_inc(w_mm, 1)

            over_ring(pe, steps, NBLK, step)

        @block.scalar
        def _(act):
            def step(j, p):
                ln.on_scalar(act, k, j)
                act.wait_ge(t_mm, j + 1)
                if has(j, -1, steps):
                    act.wait_ge(w_mm, j)
                nc.scalar.copy(x1t[:, :, :], p_t[:, :, :]).then_inc(x1t_done, 1)

            over_ring(act, steps, NBLK, step)

        @block.gpsimd
        def _(pool):
            def step(j, p):
                pool.wait_ge(node_done, j + 1)
                pool.dma_start(step_rows(kv_table, j), kv[:, p, :, :]).then_inc(stored[p], 16)
                pool.dma_start(step_rows(node1, j), node[:, p, :, :]).then_inc(stored[p], 16)
                pool.wait_ge(q_done, j + 1)
                pool.dma_start(step_rows(q_table, j), qparts[:, p, :, :, :].rearrange("p b i c -> p b (i c)")).then_inc(stored[p], 16)

            over_ring(pool, steps, NBLK, step)
            for p in range(NBLK):
                pool.wait_ge(stored[p], laps(steps - NBLK + p, p, NBLK, 48))


def edge_layer(nc, st, k, a, kv_table, q_table, neg_rows, agg1):
    u = Names()
    layer_buffers(nc, st, u, "e", 1)
    kv = st.sb("e_kv", [P, RING, TILES, 2, D])
    attr = st.sb("e_attr", [2 * ED, RING, TILES // 2, P])
    neg = st.sb("e_neg", [TILES * H, RING, P])
    qblk = st.sb("e_qblk", [P, RING, PARTS, D], BF16)
    prod = st.sb("e_prod", [P, TILES * H, C])
    logit = st.sb("e_logit", [P, RING, TILES, H])
    runmax = st.sb("e_runmax", [TILES * H, 2, P])
    lastmax = st.sb("e_lastmax", [P, 2, TILES, H])
    high = st.sb("e_high", [P, RING, TILES, H + 1], BF16)
    low = st.sb("e_low", [P, 2, TILES, H], BF16)
    far = st.sb("e_far", [P, RING, TILES, H], BF16)
    one_row = st.sb("e_one_row", [1, P], BF16)
    less_far = st.sb("e_less_far", [1, H], BF16)
    newmax = st.sb("e_newmax", [P, 2, H])
    top = st.sb("e_top", [P, 2, H])
    top_high = st.sb("e_top_high", [P, 2, H], BF16)
    top_low = st.sb("e_top_low", [P, 2, H], BF16)
    drop = st.sb("e_drop", [P, 2, H])
    scale = st.sb("e_scale", [P, 2, H])
    shifted = st.sb("e_shifted", [P, 2, TILES, H])
    scaled = st.sb("e_scaled", [P, H, HC])
    p_e = st.ps("e_p_e", [P, TILES, D])
    p_qs = [st.ps(f"e_p_q{i}", [P, TILES, D]) for i in range(2)]
    p_lt = st.ps("e_p_lt", [TILES * H, P])
    p_edge = st.ps("e_p_edge", [P, 2, TILES * H])
    p_node = st.ps("e_p_node", [P, TILES, H])
    p_run = p_edge[:, 0, :].rearrange("p (t h) -> p t h", h=H)
    p_top = p_edge[:, 1, :].rearrange("p (t h) -> p t h", h=H)
    e_in = st.ring_sems("e_e_in", RING)
    blk_in = st.ring_sems("e_blk_in", RING)
    e_mm, e_done, q_mm, prod_done, logit_done = (st.sem("e_" + n) for n in ("e_mm", "e_done", "q_mm", "prod_done", "logit_done"))
    lt_mm, run_done, run_mm, last_done, lastmax_done = (st.sem("e_" + n) for n in ("lt_mm", "run_done", "run_mm", "last_done", "lastmax_done"))
    high_done, low_done, node_mm, far_done = (st.sem("e_" + n) for n in ("high_done", "low_done", "node_mm", "far_done"))
    newmax_done, top_done, top_high_done, top_low_done = (st.sem("e_" + n) for n in ("newmax_done", "top_done", "top_high_done", "top_low_done"))
    drop_done, scale_done, top_mm, shifted_done, scaled_done = (st.sem("e_" + n) for n in ("drop_done", "scale_done", "top_mm", "shifted_done", "scaled_done"))
    zeroed, pe_passed = st.sem("e_zeroed"), st.sem("e_pe_passed")
    regs = [nc.sync.alloc_register(f"e_reg{i}") for i in range(3)]
    dest = Dest(lambda s, t: kv[:, s, t, :, :].rearrange("p a c -> p (a c)"), ALU.add)
    EDGE_LEAD = 5
    HOT_LEAD = 4

    with nc.Block() as block:

        @block.sync
        def _(sp):
            def step(j, p):
                grp, blk, old = unit_registers(nc, sp, k, regs, j)
                load_indices(nc, sp, a, u, j, p, grp, last_done)
                if has(j, -RING, UNITS):
                    sp.wait_ge(e_mm, j - RING + 1)
                    gate(sp, u.sp_passed)
                sp.dma_start(attr[:, p, :, :].rearrange("p b e -> p (b e)"), a["attr_t"][bass.ds(grp, 1), :, :].rearrange("o p c -> (o p) c")).then_inc(e_in[p], 16)
                if has(j, -RING, UNITS):
                    sp.wait_ge(run_done, j - RING + 1)
                    gate(sp, u.sp_passed)
                sp.dma_start(qblk[:, p, :, :].rearrange("p i c -> p (i c)"), rows_of(q_table, blk)).then_inc(blk_in[p], 16)
                sp.dma_start(neg[:, p, :], neg_rows.rearrange("(g t) h e -> g (t h) e", t=TILES)[bass.ds(grp, 1), :, :]
                             .rearrange("o p c -> (o p) c")).then_inc(blk_in[p], 16)
                if has(j, -RING, UNITS):
                    store_sums(nc, sp, u, j - RING, p, old, agg1)

            over_ring(sp, UNITS, RING, step)
            store_last_sums(nc, sp, k, u, agg1)

        @block.gpsimd
        def _(pool):
            def step(j, p):
                pool.wait_ge(e_done, j + 1)
                gate(pool, u.pool_passed)
                gather_rows(nc, pool, u, j, p, kv_table, dest)

            over_ring(pool, UNITS, RING, step)

        @block.vector
        def _(dve):
            nc.vector.memset(u.acc[:, RING - 1, :, :], 0.0).then_inc(zeroed, 1)
            nc.vector.memset(top[:, 1, :], -FAR).then_inc(zeroed, 1)
            nc.vector.memset(one_row[:, :], 1.0).then_inc(zeroed, 1)
            nc.vector.memset(less_far[:, :], -FAR).then_inc(zeroed, 1)
            dve.wait_ge(zeroed, 4)

            def step(s, p):
                b = p % 2
                c, n, n2, n4 = 1 - b, (p + 1) % RING, (p + 2) % RING, (p + HOT_LEAD) % RING
                if has(s, 1, UNITS):
                    dve.wait_ge(lt_mm, s + 2)
                    dve.wait_ge(blk_in[n], laps(s + 1, n, RING, 32))
                    if has(s, -1, UNITS):
                        dve.wait_ge(run_mm, s)
                    nc.vector.tensor_tensor_scan(runmax[:, c, :], neg[:, n, :], p_lt[:, :], -3.0e38, ALU.add, ALU.max).then_inc(run_done, 1)
                if has(s, 0, UNITS):
                    dve.wait_ge(newmax_done, s + 1)
                    if has(s, -2, UNITS):
                        dve.wait_ge(drop_done, s)
                        dve.wait_ge(top_high_done, s - 1)
                    nc.vector.scalar_tensor_tensor(out=top[:, b, :], in0=top[:, c, :], scalar=u.unit[:, p, 2:3], in1=newmax[:, b, :],
                                                   op0=ALU.add, op1=ALU.max).then_inc(top_done, 1)
                if has(s, 2, UNITS):
                    dve.wait_ge(u.gathered[n2], laps(s + 2, n2, RING, 16 * TILES))
                    dve.wait_ge(q_mm, s + 3)
                    if has(s, 1, UNITS):
                        dve.wait_ge(logit_done, s + 2)
                    nc.vector.tensor_tensor(prod[:, :, :].rearrange("p (t h) c -> p t (h c)", t=TILES), kv[:, n2, :, 0, :], p_qs[b][:, :, :], ALU.mult).then_inc(prod_done, 1)
                if has(s, 1, UNITS):
                    dve.wait_ge(run_mm, s + 2)
                    dve.wait_ge(last_done, s + 2)
                    if has(s, -1, UNITS):
                        dve.wait_ge(high_done, s)
                        dve.wait_ge(low_done, s)
                    nc.vector.tensor_tensor(lastmax[:, c, :, :], p_run, high[:, n, :, H:].to_broadcast([P, TILES, H]), ALU.mult).then_inc(lastmax_done, 1)
                if has(s, 0, UNITS):
                    dve.wait_ge(top_high_done, s + 1)
                    if has(s, -2, UNITS):
                        dve.wait_ge(top_mm, s - 1)
                    nc.vector.tensor_tensor(top_low[:, b, :], top[:, b, :], top_high[:, b, :], ALU.subtract).then_inc(top_low_done, 1)
                    if has(s, -2, UNITS):
                        dve.wait_ge(scale_done, s - 1)
                    nc.vector.tensor_tensor(drop[:, b, :], top[:, c, :], top[:, b, :], ALU.subtract).then_inc(drop_done, 1)
                if has(s, -1, UNITS):
                    dve.wait_ge(scale_done, s)
                    if has(s, -2, UNITS):
                        dve.wait_ge(u.acc_done, s - 1)
                    nc.vector.tensor_tensor(scaled[:, :, :], u.acc[:, (p - 2) % RING, :, :],
                                            scale[:, c, :].unsqueeze(2).to_broadcast([P, H, HC]), ALU.mult).then_inc(scaled_done, 1)
                if has(s, HOT_LEAD, UNITS):
                    place_edges(nc, dve, u, s + HOT_LEAD, n4)
                    nc.vector.tensor_tensor(high[:, n4, :, H], u.cols[:, n4, TILES:2 * TILES], u.cols[:, n4, 2 * TILES:], ALU.not_equal).then_inc(last_done, 1)
                if has(s, 2, UNITS):
                    dve.wait_ge(prod_done, s + 3)
                    if has(s, 2 - RING, UNITS):
                        dve.wait_ge(shifted_done, s + 3 - RING)
                    nc.vector.tensor_reduce(out=logit[:, n2, :, :].rearrange("p t h -> p (t h)"), in_=prod[:, :, :], op=ALU.add, axis=AX.X).then_inc(logit_done, 1)
                if has(s, -1, UNITS):
                    q = (p - 1) % RING
                    dve.wait_ge(scaled_done, s)
                    dve.wait_ge(u.sum_mm, s)
                    if has(s, -1 - RING, UNITS):
                        dve.wait_ge(u.stored[q], laps(s - 1 - RING, q, RING, 16))
                    nc.vector.tensor_tensor(u.acc[:, q, :, :], scaled[:, :, :], u.p_sum[0][:, :, :], ALU.add).then_inc(u.acc_done, 1)
                if has(s, 1, UNITS):
                    dve.wait_ge(high_done, s + 2)
                    if has(s, -1, UNITS):
                        dve.wait_ge(node_mm, s)
                    dve.wait_ge(lastmax_done, s + 2)
                    nc.vector.tensor_tensor(low[:, c, :, :], lastmax[:, c, :, :], high[:, n, :, 0:H], ALU.subtract).then_inc(low_done, 1)
                if has(s, 0, UNITS):
                    dve.wait_ge(top_mm, s + 1)
                    dve.wait_ge(logit_done, s + 1)
                    if has(s, -2, UNITS):
                        dve.wait_ge(u.exp_done, s - 1)
                    nc.vector.tensor_tensor(shifted[:, b, :, :], logit[:, p, :, :], p_top, ALU.subtract).then_inc(shifted_done, 1)
                if has(s, HOT_LEAD, UNITS):
                    make_hot(nc, dve, k, u, s + HOT_LEAD, n4)
                if has(s, 0, UNITS):
                    dve.wait_ge(u.exp_done, s + 1)
                    nc.vector.tensor_tensor(
                        u.wgt[:, p, :, :, 0:C], kv[:, p, :, 1, :].rearrange("p t (h c) -> p t h c", h=H),
                        u.wgt[:, p, :, :, C:HC].to_broadcast([P, TILES, H, C]), ALU.mult).then_inc(u.wgt_done, 1)
                if has(s, 1, UNITS):
                    dve.wait_ge(node_mm, s + 2)
                    if has(s, -1, UNITS):
                        dve.wait_ge(top_done, s)
                    nc.vector.tensor_reduce(out=newmax[:, c, :], in_=p_node[:, :, :].rearrange("p t h -> p h t"), op=ALU.max, axis=AX.X).then_inc(newmax_done, 1)

            staggered(dve, HOT_LEAD, 1, step)

        @block.scalar
        def _(act):
            def step(s, p):
                b = p % 2
                c = 1 - b
                n4 = (p + HOT_LEAD) % RING
                if has(s, HOT_LEAD + 1, UNITS):
                    unit_scalars(nc, act, k, u, s + HOT_LEAD + 1, (p + HOT_LEAD + 1) % RING, scale_done)
                if has(s, 0, UNITS):
                    act.wait_ge(top_done, s + 1)
                    if has(s, -2, UNITS):
                        act.wait_ge(top_mm, s - 1)
                    nc.scalar.copy(top_high[:, b, :], top[:, b, :]).then_inc(top_high_done, 1)
                if has(s, EDGE_LEAD, UNITS):
                    j, q = s + EDGE_LEAD, (p + EDGE_LEAD) % RING
                    act.wait_ge(e_mm, j + 1)
                    if has(j, -RING, UNITS):
                        act.wait_ge(u.wgt_done, j - RING + 1)
                    nc.scalar.copy(kv[:, q, :, :, :], p_e[:, :, :].unsqueeze(2).to_broadcast([P, TILES, 2, D])).then_inc(e_done, 1)
                if has(s, 1, UNITS):
                    act.wait_ge(lastmax_done, s + 2)
                    if has(s, 1 - RING, UNITS):
                        act.wait_ge(node_mm, s + 2 - RING)
                    nc.scalar.copy(high[:, (p + 1) % RING, :, 0:H], lastmax[:, c, :, :]).then_inc(high_done, 1)
                if has(s, 0, UNITS):
                    act.wait_ge(drop_done, s + 1)
                    if has(s, -2, UNITS):
                        act.wait_ge(scaled_done, s - 1)
                    nc.scalar.activation(scale[:, b, :], drop[:, b, :], ACT.Exp, bias=u.unit[:, p, 2:3]).then_inc(scale_done, 1)
                    act.wait_ge(shifted_done, s + 1)
                    if has(s, -RING, UNITS):
                        act.wait_ge(u.sum_mm, s - RING + 1)
                    nc.scalar.activation(u.wgt[:, p, :, :, C], shifted[:, b, :, :], ACT.Exp).then_inc(u.exp_done, 1)
                if has(s, HOT_LEAD, UNITS):
                    act.wait_ge(last_done, s + HOT_LEAD + 1)
                    if has(s, HOT_LEAD - RING, UNITS):
                        act.wait_ge(node_mm, s + HOT_LEAD + 1 - RING)
                    nc.scalar.activation(far[:, n4, :, :], high[:, n4, :, H:].to_broadcast([P, TILES, H]), ACT.Copy, scale=FAR).then_inc(far_done, 1)
                    copy_hot(nc, act, u, s + HOT_LEAD, n4)
                    copy_hot_t(nc, act, u, s + HOT_LEAD, n4, top_mm)

            staggered(act, max(EDGE_LEAD, HOT_LEAD + 1), 0, step)

        @block.tensor
        def _(pe):
            pe.wait_ge(zeroed, 4)

            def edge_features(s, p, i):
                j, q = s + EDGE_LEAD + 1, (p + EDGE_LEAD + 1) % RING
                if not has(s, EDGE_LEAD + 1, UNITS):
                    return
                if i == 0:
                    pe.wait_ge(e_in[q], laps(j, q, RING, 16))
                    if has(j, -1, UNITS):
                        pe.wait_ge(e_done, j)
                e = nc.tensor.matmul(p_e[:, 2 * i:2 * i + 2, :].rearrange("p t c -> p (t c)"), attr[:, q, i, :], k.we[:, :], start=True, stop=True)
                if i == TILES // 2 - 1:
                    e.then_inc(e_mm, 1)

            def step(s, p):
                b = p % 2
                c, n, n2, n3 = 1 - b, (p + 1) % RING, (p + 2) % RING, (p + 3) % RING
                if has(s, 1, UNITS):
                    pe.wait_ge(run_done, s + 2)
                    if has(s, -1, UNITS):
                        pe.wait_ge(shifted_done, s)
                    gate(pe, pe_passed)
                    nc.tensor.transpose(p_edge[:, 0, :], runmax[:, c, :], k.ident[0:TILES * H, 0:TILES * H]).then_inc(run_mm, 1)
                if has(s, -1, UNITS):
                    sum_edges(nc, pe, u, s - 1, (p - 1) % RING)
                if has(s, 0, UNITS):
                    pe.wait_ge(top_low_done, s + 1)
                    pe.wait_ge(top_high_done, s + 1)
                    for t in range(TILES):
                        nc.tensor.matmul(p_top[:, t, :], u.hot_t[:, p, t, :], top_high[:, b, :], start=True, stop=False)
                        last = nc.tensor.matmul(p_top[:, t, :], u.hot_t[:, p, t, :], top_low[:, b, :], start=False, stop=True)
                    last.then_inc(top_mm, 1)
                if has(s, 3, UNITS):
                    pe.wait_ge(u.hot_t_done, s + 4)
                    pe.wait_ge(blk_in[n3], laps(s + 3, n3, RING, 32))
                    if has(s, 1, UNITS):
                        pe.wait_ge(prod_done, s + 2)
                    for t in range(TILES):
                        for i in range(PARTS):
                            last = nc.tensor.matmul(p_qs[c][:, t, :], u.hot_t[:, n3, t, :], qblk[:, n3, i, :], start=(i == 0), stop=(i == PARTS - 1))
                    last.then_inc(q_mm, 1)
                if has(s, 2, UNITS):
                    pe.wait_ge(logit_done, s + 3)
                    if has(s, 1, UNITS):
                        pe.wait_ge(run_done, s + 2)
                    nc.tensor.transpose(p_lt[:, :], logit[:, n2, :, :].rearrange("p t h -> p (t h)"), k.ident[:, :]).then_inc(lt_mm, 1)
                if has(s, 1, UNITS):
                    pe.wait_ge(low_done, s + 2)
                    pe.wait_ge(high_done, s + 2)
                    pe.wait_ge(far_done, s + 2)
                    if has(s, 0, UNITS):
                        pe.wait_ge(newmax_done, s + 1)
                    for t in range(TILES):
                        nc.tensor.matmul(p_node[:, t, :], u.hot[:, n, t, :], far[:, n, t, :], start=True, stop=False)
                        nc.tensor.matmul(p_node[:, t, :], one_row[:, :], less_far[:, :], start=False, stop=False)
                        nc.tensor.matmul(p_node[:, t, :], u.hot[:, n, t, :], high[:, n, t, 0:H], start=False, stop=False)
                        last = nc.tensor.matmul(p_node[:, t, :], u.hot[:, n, t, :], low[:, c, t, :], start=False, stop=True)
                    last.then_inc(node_mm, 1)
                edge_features(s, p, 0)
                if has(s, HOT_LEAD, UNITS):
                    transpose_hot(nc, pe, k, u, s + HOT_LEAD, (p + HOT_LEAD) % RING)
                edge_features(s, p, 1)

            staggered(pe, EDGE_LEAD + 1, 1, step)


def finish(nc, st, k, agg1, node1, out):
    agg = st.sb("z_agg", [P, NBLK, NBLK, H, HC])
    nod = st.sb("z_nod", [P, NBLK, NBLK, 2 * D])
    den = st.sb("z_den", [P, NBLK, H])
    rec = st.sb("z_rec", [P, NBLK, H])
    conv = st.sb("z_conv", [P, NBLK, D])
    y1 = st.sb("z_y1", [P, NBLK, D])
    n1 = st.sb("z_n1", [P, NBLK, D])
    g1 = st.sb("z_g1", [P, NBLK, D])
    hid = st.sb("z_hid", [P, NBLK, D])
    hb = st.sb("z_hb", [P, NBLK, D])
    ht = st.sb("z_ht", [P, NBLK * P])
    act1 = st.sb("z_act1", [P, FF // P, NBLK * P])
    y2 = st.sb("z_y2", [P, NBLK, D])
    n2 = st.sb("z_n2", [P, NBLK, D])
    g2 = st.sb("z_g2", [P, NBLK, D])
    b2 = st.sb("z_b2", [P, NBLK, D])
    y3 = st.sb("z_y3", [P, NBLK, D])
    res = st.sb("z_res", [P, NBLK, NBLK, D])
    p_t = st.ps("z_p_t", [P, NBLK * P])
    p_f = [st.ps(f"z_p_f{i}", [P, NBLK * P]) for i in range(FF // P)]
    p_o = st.ps("z_p_o", [P, NBLK, D])
    ln1, ln2, ln3 = LayerNorm(nc, st, "z_ln1"), LayerNorm(nc, st, "z_ln2"), LayerNorm(nc, st, "z_ln3")
    loaded = st.ring_sems("z_loaded", NBLK)
    stored = st.ring_sems("z_stored", NBLK)
    den_done, rec_done, conv_done, y1_done = st.sem("z_den_done"), st.sem("z_rec_done"), st.sem("z_conv_done"), st.sem("z_y1_done")
    n1_done, g1_done, hid_done, hb_done = st.sem("z_n1_done"), st.sem("z_g1_done"), st.sem("z_hid_done"), st.sem("z_hb_done")
    t_mm, ht_done, f_mm, act_done = st.sem("z_t_mm"), st.sem("z_ht_done"), st.sem("z_f_mm"), st.sem("z_act_done")
    o_mm, y2_done, n2_done, g2_done = st.sem("z_o_mm"), st.sem("z_y2_done"), st.sem("z_n2_done"), st.sem("z_g2_done")
    b2_done, y3_done, res_done = st.sem("z_b2_done"), st.sem("z_y3_done"), st.sem("z_res_done")
    steps = BLOCKS // NBLK

    def wide(row):
        return row[:, :].unsqueeze(1).to_broadcast([P, NBLK, D])

    with nc.Block() as block:

        @block.sync
        def _(sp):
            def step(j, p):
                if has(j, -NBLK, steps):
                    sp.wait_ge(y3_done, j - NBLK + 1)
                sp.dma_start(agg[:, p, :, :, :].rearrange("p b h c -> p b (h c)"), step_rows(agg1, j)).then_inc(loaded[p], 16)
                sp.dma_start(nod[:, p, :, :], step_rows(node1, j)).then_inc(loaded[p], 16)

            over_ring(sp, steps, NBLK, step)

        @block.vector
        def _(dve):
            def step(s, p):
                j, n = s + 1, (p + 1) % NBLK
                if has(s, 1, steps):
                    dve.wait_ge(loaded[n], laps(j, n, NBLK, 32))
                    nc.vector.tensor_scalar(den[:, :, :], agg[:, n, :, :, C], 1e-30, None, ALU.max).then_inc(den_done, 1)
                    dve.wait_ge(den_done, j + 1)
                    nc.vector.reciprocal(rec[:, :, :], den[:, :, :]).then_inc(rec_done, 1)
                    dve.wait_ge(rec_done, j + 1)
                    nc.vector.tensor_tensor(conv[:, :, :].rearrange("p b (h c) -> p b h c", h=H), agg[:, n, :, :, 0:C],
                                            rec[:, :, :].unsqueeze(3).to_broadcast([P, NBLK, H, C]), ALU.mult).then_inc(conv_done, 1)
                    dve.wait_ge(conv_done, j + 1)
                    nc.vector.tensor_tensor(y1[:, :, :], conv[:, :, :], nod[:, n, :, 0:D], ALU.add).then_inc(y1_done, 1)
                    dve.wait_ge(y1_done, j + 1)
                    ln1.moments(dve, j, y1[:, :, :])
                if has(s, 0, steps):
                    dve.wait_ge(hb_done, s + 1)
                    dve.wait_ge(o_mm, s + 1)
                    nc.vector.tensor_tensor(y2[:, :, :], hb[:, :, :], p_o[:, :, :], ALU.add).then_inc(y2_done, 1)
                    dve.wait_ge(y2_done, s + 1)
                    ln2.moments(dve, s, y2[:, :, :])
                if has(s, 1, steps):
                    ln1.normalize(dve, j, y1[:, :, :], n1[:, :, :], n1_done)
                if has(s, 0, steps):
                    ln2.normalize(dve, s, y2[:, :, :], n2[:, :, :], n2_done)
                if has(s, 1, steps):
                    dve.wait_ge(n1_done, j + 1)
                    nc.vector.tensor_tensor(g1[:, :, :], n1[:, :, :], wide(k.g1), ALU.mult).then_inc(g1_done, 1)
                if has(s, 0, steps):
                    dve.wait_ge(n2_done, s + 1)
                    nc.vector.tensor_tensor(g2[:, :, :], n2[:, :, :], wide(k.g2), ALU.mult).then_inc(g2_done, 1)
                if has(s, 1, steps):
                    dve.wait_ge(g1_done, j + 1)
                    nc.vector.tensor_tensor(hid[:, :, :], g1[:, :, :], wide(k.b1), ALU.add).then_inc(hid_done, 1)
                if has(s, 0, steps):
                    dve.wait_ge(g2_done, s + 1)
                    nc.vector.tensor_tensor(b2[:, :, :], g2[:, :, :], wide(k.b2), ALU.add).then_inc(b2_done, 1)
                if has(s, 1, steps):
                    dve.wait_ge(hid_done, j + 1)
                    nc.vector.tensor_tensor(hb[:, :, :], hid[:, :, :], wide(k.bf2), ALU.add).then_inc(hb_done, 1)
                if has(s, 0, steps):
                    dve.wait_ge(b2_done, s + 1)
                    nc.vector.tensor_tensor(y3[:, :, :], b2[:, :, :], nod[:, p, :, D:], ALU.add).then_inc(y3_done, 1)
                    dve.wait_ge(y3_done, s + 1)
                    ln3.moments(dve, s, y3[:, :, :])
                    if has(s, -NBLK, steps):
                        dve.wait_ge(stored[p], laps(s - NBLK, p, NBLK, 16))
                    ln3.normalize(dve, s, y3[:, :, :], res[:, p, :, :], res_done)

            staggered(dve, 1, 0, step, steps, NBLK)

        @block.tensor
        def _(pe):
            def step(j, p):
                pe.wait_ge(hid_done, j + 1)
                for b in range(NBLK):
                    last = nc.tensor.transpose(p_t[:, b * P:(b + 1) * P], hid[:, b, :], k.ident[:, :])
                last.then_inc(t_mm, 1)
                pe.wait_ge(ht_done, j + 1)
                for f in range(FF // P):
                    nc.tensor.matmul(p_f[f][:, :], k.wf1[:, f * P:(f + 1) * P], ht[:, :], start=True, stop=True).then_inc(f_mm, 1)
                pe.wait_ge(act_done, 4 * j + 4)
                for b in range(NBLK):
                    for f in range(FF // P):
                        last = nc.tensor.matmul(p_o[:, b, :], act1[:, f, b * P:(b + 1) * P], k.wf2[:, f, :],
                                                start=(f == 0), stop=(f == FF // P - 1))
                last.then_inc(o_mm, 1)

            over_ring(pe, steps, NBLK, step)

        @block.scalar
        def _(act):
            def step(s, p):
                if has(s, 1, steps):
                    ln1.on_scalar(act, k, s + 1)
                if has(s, 0, steps):
                    ln2.on_scalar(act, k, s)
                if has(s, 1, steps):
                    act.wait_ge(t_mm, s + 2)
                    nc.scalar.copy(ht[:, :], p_t[:, :]).then_inc(ht_done, 1)
                if has(s, 0, steps):
                    ln3.on_scalar(act, k, s)
                if has(s, 1, steps):
                    for f in range(FF // P):
                        act.wait_ge(f_mm, 4 * s + f + 5)
                        nc.scalar.activation(act1[:, f, :], p_f[f][:, :], ACT.Gelu, bias=k.bf1[:, f:f + 1]).then_inc(act_done, 1)

            staggered(act, 1, 0, step, steps, NBLK)

        @block.gpsimd
        def _(pool):
            def step(j, p):
                pool.wait_ge(res_done, j + 1)
                pool.dma_start(step_rows(out, j), res[:, p, :, :]).then_inc(stored[p], 16)

            over_ring(pool, steps, NBLK, step)
            for p in range(NBLK):
                pool.wait_ge(stored[p], laps(steps - NBLK + p, p, NBLK, 16))


def build(nc, a, out):

    def scratch(name, shape):
        return nc.dram_tensor(name, shape, F32, kind="Internal").ap()

    table0 = scratch("table0", [NPAD, ROW0])
    tgt0 = nc.dram_tensor("tgt0", [NPAD, PARTS * H], BF16, kind="Internal").ap()
    q_table = nc.dram_tensor("q_table", [NPAD, PARTS * D], BF16, kind="Internal").ap()
    agg0 = scratch("agg0", [NPAD, AGG])
    kv_table = scratch("kv_table", [NPAD, 2 * D])
    node1 = scratch("node1", [NPAD, NODE1])
    agg1 = scratch("agg1", [NPAD, AGG])
    neg_rows = scratch("neg_rows", [P * FLAG_TILES, H, P])

    with ExitStack() as ctx:
        st = Store(nc, ctx, ctx)
        k = Names()
        k.iota, k.ident, k.ones = st.sb("k_iota", [P, P]), st.sb("k_ident", [P, P]), st.sb("k_ones", [P, P])
        k.iota_b, k.ident_b = st.sb("k_iota_b", [P, P], BF16), st.sb("k_ident_b", [P, P], BF16)
        k.eps, k.part, k.block_start = st.sb("k_eps", [P, 1]), st.sb("k_part", [P, 1]), st.sb("k_block_start", [P, 1])
        k.ucol = st.sb("k_ucol", [P, UNITS, 3])
        k.ureg = st.sb("k_ureg", [1, UNITS, 3], I32)
        k.w0, k.w0t, k.att0 = st.sb("k_w0", [P, D]), st.sb("k_w0t", [P, D]), st.sb("k_att0", [P, 2 * H])
        k.bias0 = st.sb("k_bias0", [P, D])
        k.wcat1, k.bcat1, k.we = st.sb("k_wcat1", [P, 4 * D]), st.sb("k_bcat1", [P, 4 * D]), st.sb("k_we", [2 * ED, 2 * D])
        k.g1, k.b1, k.g2, k.b2 = st.sb("k_g1", [P, D]), st.sb("k_b1", [P, D]), st.sb("k_g2", [P, D]), st.sb("k_b2", [P, D])
        k.wf1, k.bf1 = st.sb("k_wf1", [P, FF]), st.sb("k_bf1", [P, FF // P])
        k.wf2, k.bf2 = st.sb("k_wf2", [P, FF // P, D]), st.sb("k_bf2", [P, D])
        k.loaded = st.dma_sem("k_loaded")
        k.loads = [
            (k.w0[:, :], a["W0"]), (k.w0t[:, :], a["W0T"]), (k.att0[:, :], a["att0"]),
            (k.wcat1[:, :], a["wcat1"]), (k.we[:, :], a["We"]), (k.wf1[:, :], a["Wf1"]),
            (k.wf2[:, :, :], a["Wf2"]), (k.bf1[:, :], a["bf1"]),
            (k.bcat1[:, :], a["bcat1"].to_broadcast([P, 4 * D])),
        ] + [(t[:, :], a[n].to_broadcast([P, D])) for t, n in (
            (k.bias0, "bias0"), (k.g1, "g1"), (k.b1, "b1"), (k.g2, "g2"), (k.b2, "b2"), (k.bf2, "bf2"))]

        with ExitStack() as c:
            s = Store(nc, c, ctx)
            k.unit_row = s.sb("k_unit_row", [P, UNITS])
            constants(nc, s, k)
            unit_tables(nc, s, k, a)
            s.over()
        for stage, args in (
                (project0, (k, a, table0, tgt0, neg_rows)),
                (gat_layer, (k, a, table0, tgt0, agg0)),
                (middle, (k, a, agg0, kv_table, q_table, node1)),
                (edge_layer, (k, a, kv_table, q_table, neg_rows, agg1)),
                (finish, (k, agg1, node1, out))):
            with ExitStack() as c:
                s = Store(nc, c, ctx)
                stage(nc, s, *args)
                s.over()


def kernel(**inputs):
    import numpy as np
    import concourse.bacc as bacc
    from concourse.bass_utils import run_bass_kernel_spmd

    i = {n: np.asarray(v) for n, v in inputs.items()}
    x = i["x"]
    x_rows = np.zeros((NPAD, D), x.dtype)
    x_rows[:NODES] = x
    src = np.zeros(GROUPS * GE, np.int32)
    src[:EDGES] = i["src"]
    dst = np.full(P * FLAG_TILES * P, NPAD, np.int32)
    dst[:EDGES] = i["dst"]
    prev = np.concatenate([dst[:1], dst[:-1]])
    dst_rows = dst.reshape(P, FLAG_TILES * P)
    prev_rows = prev.reshape(P, FLAG_TILES * P)
    dst = dst[:GROUPS * GE]
    nxt = np.concatenate([dst[1:], dst[-1:]]).reshape(-1, P).copy()
    nxt[:, -1] = -1
    edge_cols = np.concatenate([v.reshape(GROUPS, TILES, P).transpose(0, 2, 1) for v in (src, dst, nxt)], axis=2)
    attr = np.zeros((GROUPS * GE, ED), i["edge_attr_64"].dtype)
    attr[:EDGES] = i["edge_attr_64"]
    we2 = np.zeros((2 * ED, 2 * D), x.dtype)
    we2[:ED, :D] = we2[ED:, D:] = i["L1_gnn_We"]
    att0 = np.zeros((D, 2 * H), x.dtype)
    for h in range(H):
        att0[h * C:(h + 1) * C, h] = i["L0_gnn_a_left"][:, h]
        att0[h * C:(h + 1) * C, H + h] = i["L0_gnn_a_right"][:, h]
    arrays = {
        "x_rows": x_rows, "xT": x_rows.T, "edge_cols": edge_cols, "last_dst": dst[GE - 1::GE].reshape(1, GROUPS),
        "dst_rows": dst_rows, "dst_prev_rows": prev_rows, "attr_t": attr.reshape(GROUPS, TILES // 2, 2, P, ED).transpose(0, 2, 4, 1, 3).reshape(GROUPS, 2 * ED, GE // 2),
        "W0": i["L0_gnn_W"], "W0T": i["L0_gnn_W"].T, "att0": att0, "bias0": i["L0_gnn_bias"].reshape(1, D),
        "wcat1": np.concatenate([i["L1_gnn_W" + n] for n in ("q", "k", "v", "skip")], axis=1),
        "bcat1": np.concatenate([i["L1_gnn_b" + n] for n in ("q", "k", "v", "skip")]).reshape(1, 4 * D),
        "We": we2, "Wf1": i["L1_gnn_Wf1"], "bf1": i["L1_gnn_bf1"].reshape(FF // P, P).T,
        "Wf2": i["L1_gnn_Wf2"].reshape(FF // P, P, D).transpose(1, 0, 2), "bf2": i["L1_gnn_bf2"].reshape(1, D),
        **{n: i["L1_gnn_" + n].reshape(1, D) for n in ("g1", "b1", "g2", "b2")},
    }
    nc = bacc.Bacc("TRN2", target_bir_lowering=False, num_devices=1)
    feed, aps = {}, {}
    for n, v in arrays.items():
        v = np.ascontiguousarray(v)
        feed["in_" + n] = v
        aps[n] = nc.dram_tensor("in_" + n, v.shape, mybir.dt.from_np(v.dtype), kind="ExternalInput").ap()
    out = nc.dram_tensor("out_rows", (NPAD, D), F32, kind="ExternalOutput").ap()
    build(nc, aps, out)
    r = run_bass_kernel_spmd(nc, [feed], core_ids=[0])
    return r.results[0]["out_rows"][:NODES]
```
